# Optimizing a Trainium2 kernel written in Bass

```python
import numpy as np
import jax
import jax.numpy as jnp

def _softmax(x, axis=-1):
    return jax.nn.softmax(x, axis=axis)

def _gelu(x):
    return jax.nn.gelu(x, approximate=True)

def _silu(x):
    return jax.nn.silu(x)

def _sigmoid(x):
    return jax.nn.sigmoid(x)

def _layernorm(x, axis=-1, eps=1e-05):
    m = jnp.mean(x, axis=axis, keepdims=True)
    v = jnp.var(x, axis=axis, keepdims=True)
    return (x - m) / jnp.sqrt(v + eps)

def _scatter_add(tgt, idx, src, axis=0):
    return tgt.at[idx].add(src)

def _segment_sum(src, seg, n):
    return jax.ops.segment_sum(src, seg, n)
kernel_name = 'mk_decoder_preln_d1_seqx_r4_1216a4'

def setup_inputs(seed: int=0):
    np.random.seed(seed)
    _w = jnp.asarray

    def _rec_inputs():
        import jax
        import jax.numpy as jnp
        _rk = jax.random.key(seed)
        x = 7.22e-05 + 1 * jax.random.normal(jax.random.fold_in(_rk, 1), (4, 1024, 256), jnp.float32)
        _lenS = 1024 - jax.random.randint(jax.random.fold_in(_rk, 7), (4,), 0, max(1, 1024 // 4) + 1, jnp.int32)
        _lenS2 = 77 - jax.random.randint(jax.random.fold_in(_rk, 8), (4,), 0, max(1, 77 // 4) + 1, jnp.int32)
        _ctx_1024P = jax.random.normal(jax.random.fold_in(_rk, 11), (4, 16, 256), jnp.float32)
        _ctx_1024c = jax.random.dirichlet(jax.random.fold_in(_rk, 511), 0.3 * jnp.ones((16,), jnp.float32), (4, 77))
        _ctx_1024t = jnp.einsum('bsk,bkd->bsd', _ctx_1024c, _ctx_1024P)
        _ctx_1024t = _ctx_1024t * jax.lax.rsqrt(jnp.mean(jnp.square(_ctx_1024t)) + 1e-12) * 0.953939
        ctx_1024 = 4.13588e-05 + 0.999923 * (_ctx_1024t + 0.3 * jax.random.normal(jax.random.fold_in(_rk, 611), (4, 77, 256), jnp.float32))
        return (x, ctx_1024)
    x, ctx_1024 = _rec_inputs()

    def _L0_attn_setup():
        import jax, jax.numpy as jnp
        import numpy as np
        import math
        H = 16
        EPS = 1e-06

        def _apply_kernel(x, orf):
            m, d_k = orf.shape
            proj = jnp.einsum('bhld,md->bhlm', x, orf) / d_k ** 0.25
            norm = jnp.sum(x * x, axis=-1, keepdims=True) / (2.0 * math.sqrt(d_k))
            return (jnp.exp(proj - norm) + EPS) / math.sqrt(m)
        key = jax.random.key(seed)
        ks = jax.random.split(key, 10)
        B, L, D, m = (4, 1024, 256, 64)
        d_k = D // H
        s = 1.0 / math.sqrt(D)
        return {'x': jax.random.normal(ks[0], (B, L, D), jnp.float32), 'Wq': jax.random.normal(ks[1], (D, D), jnp.float32) * s, 'bq': jax.random.normal(ks[2], (D,), jnp.float32) * s, 'Wk': jax.random.normal(ks[3], (D, D), jnp.float32) * s, 'bk': jax.random.normal(ks[4], (D,), jnp.float32) * s, 'Wv': jax.random.normal(ks[5], (D, D), jnp.float32) * s, 'bv': jax.random.normal(ks[6], (D,), jnp.float32) * s, 'Wo': jax.random.normal(ks[7], (D, D), jnp.float32) * s, 'bo': jax.random.normal(ks[8], (D,), jnp.float32) * s, 'orf': jax.random.normal(ks[9], (m, d_k), jnp.float32)}
    _L0_attn_all = _L0_attn_setup()
    _L0_attn_in = {k: v for k, v in _L0_attn_all.items() if k in ('Wq', 'bq', 'Wk', 'bk', 'Wv', 'bv', 'Wo', 'bo', 'orf')}
    del _L0_attn_all

    def _L0_xattn_setup():
        import jax, jax.numpy as jnp
        import numpy as np
        C = 256
        B, SQ, SKV = (4, 512, 512)
        key = jax.random.key(seed)
        ks = jax.random.split(key, 10)
        s = 1.0 / np.sqrt(C)
        return {'x': jax.random.normal(ks[0], (B, SQ, C), jnp.float32), 'content_embeddings': jax.random.normal(ks[1], (B, SKV, C), jnp.float32), 'Wq': jax.random.normal(ks[2], (C, C), jnp.float32) * s, 'bq': jnp.zeros((C,), jnp.float32), 'Wk': jax.random.normal(ks[3], (C, C), jnp.float32) * s, 'bk': jnp.zeros((C,), jnp.float32), 'Wv': jax.random.normal(ks[4], (C, C), jnp.float32) * s, 'bv': jnp.zeros((C,), jnp.float32), 'Wo': jax.random.normal(ks[5], (C, C), jnp.float32) * s, 'bo': jnp.zeros((C,), jnp.float32)}
    _L0_xattn_all = _L0_xattn_setup()
    _L0_xattn_in = {k: v for k, v in _L0_xattn_all.items() if k in ('Wq', 'bq', 'Wk', 'bk', 'Wv', 'bv', 'Wo', 'bo')}
    del _L0_xattn_all

    def _L0_ffn_setup():
        import jax, jax.numpy as jnp
        import numpy as np
        HIDDEN = 256
        MOE_FF = 128
        SHARED_FF = 704
        NUM_EXPERTS = 16
        TOP_K = 2
        NORM_TOPK = True
        key = jax.random.key(seed)
        ks = jax.random.split(key, 8)
        s = 0.02
        return {'layer_input': jax.random.normal(ks[0], (1, 512, HIDDEN), dtype=jnp.float32), 'gate_w': jax.random.normal(ks[1], (NUM_EXPERTS, HIDDEN), dtype=jnp.float32) * s, 'w_gate_up': jax.random.normal(ks[2], (NUM_EXPERTS, HIDDEN, 2 * MOE_FF), dtype=jnp.float32) * s, 'w_down': jax.random.normal(ks[3], (NUM_EXPERTS, MOE_FF, HIDDEN), dtype=jnp.float32) * s, 'shared_w_gate': jax.random.normal(ks[4], (SHARED_FF, HIDDEN), dtype=jnp.float32) * s, 'shared_w_up': jax.random.normal(ks[5], (SHARED_FF, HIDDEN), dtype=jnp.float32) * s, 'shared_w_down': jax.random.normal(ks[6], (HIDDEN, SHARED_FF), dtype=jnp.float32) * s, 'shared_gate_w': jax.random.normal(ks[7], (1, HIDDEN), dtype=jnp.float32) * s}
    _L0_ffn_all = _L0_ffn_setup()
    _L0_ffn_in = {k: v for k, v in _L0_ffn_all.items() if k in ('gate_w', 'w_gate_up', 'w_down', 'shared_w_gate', 'shared_w_up', 'shared_w_down', 'shared_gate_w')}
    del _L0_ffn_all
    return {'x': x, 'ctx_1024': ctx_1024, 'L0_attn_Wq': _L0_attn_in['Wq'], 'L0_attn_bq': _L0_attn_in['bq'], 'L0_attn_Wk': _L0_attn_in['Wk'], 'L0_attn_bk': _L0_attn_in['bk'], 'L0_attn_Wv': _L0_attn_in['Wv'], 'L0_attn_bv': _L0_attn_in['bv'], 'L0_attn_Wo': _L0_attn_in['Wo'], 'L0_attn_bo': _L0_attn_in['bo'], 'L0_attn_orf': _L0_attn_in['orf'], 'L0_xattn_Wq': _L0_xattn_in['Wq'], 'L0_xattn_bq': _L0_xattn_in['bq'], 'L0_xattn_Wk': _L0_xattn_in['Wk'], 'L0_xattn_bk': _L0_xattn_in['bk'], 'L0_xattn_Wv': _L0_xattn_in['Wv'], 'L0_xattn_bv': _L0_xattn_in['bv'], 'L0_xattn_Wo': _L0_xattn_in['Wo'], 'L0_xattn_bo': _L0_xattn_in['bo'], 'L0_ffn_gate_w': _L0_ffn_in['gate_w'], 'L0_ffn_w_gate_up': _L0_ffn_in['w_gate_up'], 'L0_ffn_w_down': _L0_ffn_in['w_down'], 'L0_ffn_shared_w_gate': _L0_ffn_in['shared_w_gate'], 'L0_ffn_shared_w_up': _L0_ffn_in['shared_w_up'], 'L0_ffn_shared_w_down': _L0_ffn_in['shared_w_down'], 'L0_ffn_shared_gate_w': _L0_ffn_in['shared_gate_w']}

def reference(x, ctx_1024, L0_attn_Wq, L0_attn_bq, L0_attn_Wk, L0_attn_bk, L0_attn_Wv, L0_attn_bv, L0_attn_Wo, L0_attn_bo, L0_attn_orf, L0_xattn_Wq, L0_xattn_bq, L0_xattn_Wk, L0_xattn_bk, L0_xattn_Wv, L0_xattn_bv, L0_xattn_Wo, L0_xattn_bo, L0_ffn_gate_w, L0_ffn_w_gate_up, L0_ffn_w_down, L0_ffn_shared_w_gate, L0_ffn_shared_w_up, L0_ffn_shared_w_down, L0_ffn_shared_gate_w):
    import jax
    import jax.numpy as jnp

    def _L0_attn_ref(x, Wq, bq, Wk, bk, Wv, bv, Wo, bo, orf):
        import jax, jax.numpy as jnp
        import numpy as np
        import math
        H = 16
        EPS = 1e-06

        def _apply_kernel(x, orf):
            m, d_k = orf.shape
            proj = jnp.einsum('bhld,md->bhlm', x, orf) / d_k ** 0.25
            norm = jnp.sum(x * x, axis=-1, keepdims=True) / (2.0 * math.sqrt(d_k))
            return (jnp.exp(proj - norm) + EPS) / math.sqrt(m)
        B, L, D = x.shape
        d_k = D // H

        def split(y):
            return y.reshape(B, L, H, d_k).transpose(0, 2, 1, 3)
        q = split(x @ Wq.T + bq)
        k = split(x @ Wk.T + bk)
        v = split(x @ Wv.T + bv)
        q_phi = _apply_kernel(q, orf)
        k_phi = _apply_kernel(k, orf)
        kv = jnp.einsum('bhlm,bhld->bhmd', k_phi, v)
        ksum = jnp.sum(k_phi, axis=2)
        num = jnp.einsum('bhlm,bhmd->bhld', q_phi, kv)
        den = jnp.einsum('bhlm,bhm->bhl', q_phi, ksum)
        out = num / den[..., None]
        out = out.transpose(0, 2, 1, 3).reshape(B, L, D)
        return out @ Wo.T + bo

    def _L0_xattn_ref(x, content_embeddings, Wq, bq, Wk, bk, Wv, bv, Wo, bo):
        import jax, jax.numpy as jnp
        import numpy as np
        C = 256
        B, SQ, SKV = (4, 512, 512)
        queries = x @ Wq.T + bq
        keys = content_embeddings @ Wk.T + bk
        values = content_embeddings @ Wv.T + bv
        scale = 1.0 / jnp.sqrt(jnp.asarray(C, x.dtype))
        scores = jnp.einsum('bqc,bkc->bqk', queries, keys) * scale
        attn = jax.nn.softmax(scores, axis=-1)
        attended = jnp.einsum('bqk,bkc->bqc', attn, values)
        out = x + attended
        return out @ Wo.T + bo

    def _L0_ffn_ref(layer_input, gate_w, w_gate_up, w_down, shared_w_gate, shared_w_up, shared_w_down, shared_gate_w):
        import jax, jax.numpy as jnp
        import numpy as np
        HIDDEN = 256
        MOE_FF = 128
        SHARED_FF = 704
        NUM_EXPERTS = 16
        TOP_K = 2
        NORM_TOPK = True
        B, S, D = layer_input.shape
        x = layer_input.reshape(-1, D)
        N = x.shape[0]
        shared = jax.nn.silu(x @ shared_w_gate.T) * (x @ shared_w_up.T) @ shared_w_down.T
        shared = shared * jax.nn.sigmoid(x @ shared_gate_w.T)
        logits = x @ gate_w.T
        probs = jax.nn.softmax(logits.astype(jnp.float32), axis=-1)
        rw, sel = jax.lax.top_k(probs, TOP_K)
        if NORM_TOPK:
            rw = rw / rw.sum(axis=-1, keepdims=True)
        rw = rw.astype(x.dtype)
        combine = jnp.zeros((N, NUM_EXPERTS), x.dtype).at[jnp.arange(N)[:, None], sel].set(rw)
        gu = jnp.einsum('nd,edf->nef', x, w_gate_up)
        g, h = jnp.split(gu, 2, axis=-1)
        h = jax.nn.silu(g) * h
        expert_out = jnp.einsum('nef,efd,ne->nd', h, w_down, combine)
        out = expert_out + shared
        return out.reshape(B, S, D)
    x = x + _L0_attn_ref(_layernorm(x, axis=-1), L0_attn_Wq, L0_attn_bq, L0_attn_Wk, L0_attn_bk, L0_attn_Wv, L0_attn_bv, L0_attn_Wo, L0_attn_bo, L0_attn_orf)
    x = x + _L0_xattn_ref(_layernorm(x, axis=-1), ctx_1024, L0_xattn_Wq, L0_xattn_bq, L0_xattn_Wk, L0_xattn_bk, L0_xattn_Wv, L0_xattn_bv, L0_xattn_Wo, L0_xattn_bo)
    x = x + _L0_ffn_ref(_layernorm(x, axis=-1), L0_ffn_gate_w, L0_ffn_w_gate_up, L0_ffn_w_down, L0_ffn_shared_w_gate, L0_ffn_shared_w_up, L0_ffn_shared_w_down, L0_ffn_shared_gate_w)
    return x

_drawn_inputs = setup_inputs


def setup_inputs(seed=0):
    import zlib

    import numpy as np

    out = dict(_drawn_inputs(seed))
    spreads = {'L0_xattn_bq': (0.0, 0.55),
     'L0_xattn_bk': (0.0, 0.8),
     'L0_xattn_bv': (0.0, 0.1),
     'L0_xattn_bo': (0.0, 0.1)}
    factors = {'L0_attn_bq': 8.0,
     'L0_attn_bk': 8.0,
     'L0_ffn_gate_w': 8.0,
     'L0_ffn_w_gate_up': 8.0,
     'L0_ffn_w_down': 8.0,
     'L0_ffn_shared_w_gate': 6.174,
     'L0_ffn_shared_w_up': 6.003,
     'L0_ffn_shared_w_down': 6.062,
     'L0_ffn_shared_gate_w': 8.0}
    for name, (base, spread) in spreads.items():
        noise = np.random.default_rng([zlib.crc32(name.encode()), seed]).standard_normal(out[name].shape)
        drawn = base * np.exp(spread * noise) if base else spread * noise
        out[name] = jnp.asarray(drawn.astype(out[name].dtype))
    for name, factor in factors.items():
        out[name] = (out[name] * factor).astype(out[name].dtype)
    return out
```

```python
from contextlib import ExitStack

import concourse.bass as bass
from concourse import mybir

F32 = mybir.dt.float32
I32 = mybir.dt.int32
ALU = mybir.AluOpType
ACT = mybir.ActivationFunctionType
AX_X = mybir.AxisListType.X

P = 128
B, L, D = 4, 1024, 256
H, DK, M = 16, 16, 64
SKV = 77
E, FF, SFF = 16, 128, 704
T = B * L // P
TPC = 4
CH = T // TPC
CT = TPC * P
KD = D // P
HV = H * (DK + 1)
HV2 = 2 * (DK + 1)
PAIRS = H // 2
SF = [P] * (SFF // P) + ([SFF % P] if SFF % P else [])
NF = len(SF)
ST = (2 * T * P + E * (P - 1)) // P
ST = -(-ST // 4) * 4
KEPS = 1e-6
LN_EPS = 1e-5
NCONST = 13


def wait(eng, sem, value):
    if not (isinstance(value, int) and value <= 0):
        eng.wait_ge(sem, value)


def decoder_layer(nc, x, ctxT, wqT, bq, wkT, bk, wvT, bv, woT, bo, orfT,
                  xwq, xbq, xwkT, xbk, xwvT, xbv, xwoT, xbo,
                  gwT, wgu, wdn, sgT, suT, sdT, ident_d, tri_d, normblk_d, desc16_d, iota_d, out):
    slots_x = nc.dram_tensor("slots_x", (ST * P, D), F32, kind="Internal").ap()
    slots_y = nc.dram_tensor("slots_y", (ST * P, D), F32, kind="Internal").ap()

    with ExitStack() as ctx:
        def sb(name, shape, dt=F32):
            return ctx.enter_context(nc.sbuf_tensor(name, shape, dt))[tuple(slice(None) for _ in shape)]

        def sem(name):
            return ctx.enter_context(nc.semaphore(name))

        def bank(name):
            return ctx.enter_context(nc.psum_tensor(name, [P, 512], F32))

        X = sb("X", [P, T, D])
        XT = sb("XT", [P, KD, T * P])
        XN3 = sb("XN3", [P, T * D])
        ARENA = sb("ARENA", [P, 12288])
        WA = sb("WA", [P, 4, KD, D])
        XWO = sb("XWO", [P, KD, D])
        VP = sb("VP", [P, B, D])
        GK = sb("GK", [P, KD, B * SKV])
        GQ = sb("GQ", [1, B * SKV])
        KVN = sb("KVN", [P, 2, B * HV])
        SG = sb("SG", [P, KD, SFF])
        SU = sb("SU", [P, KD, SFF])
        SD = sb("SD", [P, NF, D])
        GW = sb("GW", [P, KD, E + 1])
        R = sb("R", [P, 4 * M])
        IDENT = sb("IDENT", [P, P])
        TRI = sb("TRI", [P, P])
        ONES = sb("ONES", [P, P])
        EPS = sb("EPS", [P, P])
        BQK = sb("BQK", [P, 2, KD])
        XB = sb("XB", [P, 3, KD])
        BVR = sb("BVR", [P, D])
        BOR = sb("BOR", [P, D])
        XBOR = sb("XBOR", [P, D])
        HALF = sb("HALF", [P, 4])
        NSUM = sb("NSUM", [P, 2, HV])
        REC = sb("REC", [P, 2, H])
        SMX = sb("SMX", [P, 3, TPC])
        SOFT = sb("SOFT", [P, 3, TPC * SKV])
        PROBT = sb("PROBT", [P, CT])
        LOG = sb("LOG", [P, T, E + 1])
        RW = sb("RW", [P, 2, T])
        SIG = sb("SIG", [P, T])
        SLOT = sb("SLOT", [P, 2, T], I32)
        EID = sb("EID", [P, ST], I32)
        SMALL = sb("SMALL", [P, 12, T])
        DESC = sb("DESC", [P, E])
        IOTA = sb("IOTA", [P, ST])
        lnbuf = [[sb(f"ln{n}_{w}", [P, TPC] + s) for w, s in (("st", [6]), ("mv", [2]), ("ve", []), ("rstd", []))]
                 for n in range(3)]

        KDT = ARENA[:, 0:4096].rearrange("p (b q n) -> p b q n", b=2, q=4)
        QPHI = ARENA[:, 4096:8192].rearrange("p (i n) -> p i n", i=8)
        XN3C = ARENA[:, 2048:3072].rearrange("p (j d) -> p j d", j=TPC)
        X1T = ARENA[:, 6144:8192].rearrange("p (b h n) -> p b h n", b=2, h=KD)
        XN = ARENA[:, 8192:9216].rearrange("p (j d) -> p j d", j=TPC)
        X2T = ARENA[:, 9216:10240].rearrange("p (h n) -> p h n", h=KD)
        AT = ARENA[:, 10240:11264].rearrange("p (h n) -> p h n", h=KD)
        ATT = ARENA[:, 11264:12288].rearrange("p (j d) -> p j d", j=TPC)
        WGU = ARENA[:, 0:8192].rearrange("p (e k f) -> p e k f", e=E, k=KD)
        WDN = ARENA[:, 8192:12288].rearrange("p (e d) -> p e d", e=E)
        VEXT = XN3[:, 0:8 * HV].rearrange("p (b j n) -> p b j n", b=2, j=TPC)
        KPHI = XN3[:, 2176:4224].rearrange("p (b n) -> p b n", b=2)
        n0 = 4224
        CTXT = XN3[:, n0:n0 + 616].rearrange("p (h n) -> p h n", h=KD)
        KT = XN3[:, n0 + 616:n0 + 1232].rearrange("p (h n) -> p h n", h=KD)
        VT = XN3[:, n0 + 1232:n0 + 1848].rearrange("p (h n) -> p h n", h=KD)
        XWQ, XWK, XWV = (XN3[:, n0 + 1848 + 512 * i:n0 + 2360 + 512 * i].rearrange("p (h n) -> p h n", h=KD)
                         for i in range(3))
        XN3T = XN3[:, :].rearrange("p (t d) -> p t d", t=T)
        ZERO = ARENA[:, 4096:6144]
        KVX = KVN[:, 0, :].rearrange("p (b n) -> p b n", b=B)
        NB = KVN[:, 1, :].rearrange("p (b n) -> p b n", b=B)
        HT = [KVN[:, i // 2, 512 * (i % 2):512 * (i % 2) + 512] for i in range(3)]
        SDIF, PEXP, PROB = (SOFT[:, i, :].rearrange("p (j n) -> p j n", j=TPC) for i in range(3))
        SIL = [SOFT[:, 0:2, :].rearrange("p a n -> p (a n)")[:, 0:512], PROBT[:, :]]
        WQ, WK, WV, WO = (WA[:, i] for i in range(4))
        TMP = [WA[:, i].rearrange("p k n -> p (k n)") for i in range(4)] + [XWO[:, :, :].rearrange("p k n -> p (k n)")] \
            + [VP[:, 2 * i:2 * i + 2, :].rearrange("p k n -> p (k n)") for i in range(2)]
        XE = XN3[:, 0:1024].rearrange("p (b d) -> p b d", b=4)
        XET = XN3[:, 1024:1536].rearrange("p (b d) -> p b d", b=2)
        ESIL = XN3[:, 1536:1792].rearrange("p (b d) -> p b d", b=2)
        HE = XN3[:, 1792:2048].rearrange("p (b d) -> p b d", b=2)
        HET = XN3[:, 2048:2304].rearrange("p (b d) -> p b d", b=2)
        YE = XN3[:, 2304:3328].rearrange("p (b d) -> p b d", b=4)
        YG = XN3[:, 4096:8192].rearrange("p (b d) -> p b d", b=16)

        pT = [bank("pT0"), bank("pT1")]
        pK = [bank("pK0"), bank("pK1")]
        pF = [bank("pF0"), bank("pF1")]
        pO = [bank("pO0"), bank("pO1")]
        pN = [pK[1], pK[0]]
        pS = pK[0][:, 0:TPC * 80].rearrange("p (j n) -> p j n", j=TPC)
        pR = pK[0][:, 0:TPC * 32].rearrange("p (j n) -> p j n", j=TPC)

        ld_const = sem("ld_const")
        ld_ctx = sem("ld_ctx")
        ld_attn = sem("ld_attn")
        ld_x = sem("ld_x")
        ld_ffn = sem("ld_ffn")
        ld_exp = sem("ld_exp")
        cleared = sem("cleared")
        orf_in = sem("orf_in")
        r_ready = sem("r_ready")
        zeroed = sem("zeroed")
        prep_ps = sem("prep_ps")
        prep_ev = sem("prep_ev")
        ln = [[sem(f"ln{n}_{w}") for w in ("st", "mv", "ve", "rstd", "xn")] for n in range(3)]
        xt_save = [sem(f"xt_save{i}") for i in range(2)]
        t1_ps, t1_a, t1_d = sem("t1_ps"), sem("t1_a"), sem("t1_d")
        k_ps, k_lin, k_sq = sem("k_ps"), sem("k_lin"), sem("k_sq")
        v_ps, v_ev = sem("v_ps"), sem("v_ev")
        kf_ps, k_exp = sem("kf_ps"), sem("k_exp")
        kv_ps, kv_ev = sem("kv_ps"), sem("kv_ev")
        nb_ps, nb_ev = sem("nb_ps"), sem("nb_ev")
        bo_in = sem("bo_in")
        q_ps, q_lin, q_sq = sem("q_ps"), sem("q_lin"), sem("q_sq")
        qf_ps, q_exp = sem("qf_ps"), sem("q_exp")
        n_ps, n_step, att_rdy = sem("n_ps"), sem("n_step"), sem("att_rdy")
        at_ps, at_a, at_d = sem("at_ps"), sem("at_a"), sem("at_d")
        wo_ps, x1 = sem("wo_ps"), sem("x1")
        t2_ps, t2_a, t2_d = sem("t2_ps"), sem("t2_a"), sem("t2_d")
        s_ps, s_max, s_dif, s_exp, s_step, prob = (sem(n) for n in ("s_ps", "s_max", "s_dif", "s_exp", "s_step", "prob"))
        pt_ps, pt_ev = sem("pt_ps"), sem("pt_ev")
        o_ps, x2 = sem("o_ps"), sem("x2")
        t3_ps, t3_a, t3_d = sem("t3_ps"), sem("t3_a"), sem("t3_d")
        r_ps, r_ev = sem("r_ps"), sem("r_ev")
        rt = sem("rt")
        rt_a = sem("rt_a")
        rt_ps = sem("rt_ps")
        mask_rdy, probe_max, slots_rdy, eid_rdy = sem("mask_rdy"), sem("probe_max"), sem("slots_rdy"), sem("eid_rdy")
        sc = sem("sc")
        g_ps, u_ps, silu, h_rdy, d_ps, s_res = (sem(n) for n in ("g_ps", "u_ps", "silu", "h_rdy", "d_ps", "s_res"))
        xe_in = [sem(f"xe_in{k}") for k in range(4)]
        e_t, e_tev, e_gu, e_silu, e_h, e_ht, e_htev, e_dn, e_yev = (
            sem(n) for n in ("e_t", "e_tev", "e_gu", "e_silu", "e_h", "e_ht", "e_htev", "e_dn", "e_yev"))
        ye_out = [sem(f"ye_out{k}") for k in range(4)]
        yg_in = [sem(f"yg_in{k}") for k in range(16)]
        comb1, comb = sem("comb1"), sem("comb")
        stored = sem("stored")
        passed = sem("passed")

        def apart(eng):
            eng.sem_inc(passed, 1)

        def tok(a, c):
            return a[bass.ds(c * CT, CT), :].rearrange("(p j) d -> p j d", j=TPC)

        def feat(a):
            return a.rearrange("(k p) n -> p k n", p=P)

        block = ctx.enter_context(nc.Block())

        @block.sync
        def _(sp):
            n = [0] * 4
            for dst, src in ((CTXT, feat(ctxT)), (XWK, feat(xwkT)), (XWV, feat(xwvT)), (XWQ, feat(xwq)), (XWO, feat(xwoT))):
                sp.dma_start(dst, src).then_inc(ld_ctx, 16)
            for c in range(CH):
                sp.dma_start(X[:, TPC * c:TPC * c + TPC, :], tok(x, c)).then_inc(ld_x, 16)
            for dst, src in ((WK, wkT), (WV, wvT), (WQ, wqT), (WO, woT)):
                sp.dma_start(dst, feat(src)).then_inc(ld_attn, 16)
            for dst, src in ((SG, feat(sgT)), (SU, feat(suT)), (GW, feat(gwT)),
                             (SD[:, 0:NF - 1, :], feat(sdT[0:(NF - 1) * P, :])), (SD[0:SF[-1], NF - 1, :], sdT[(NF - 1) * P:SFF, :])):
                sp.dma_start(dst, src).then_inc(ld_ffn, 16)
            sp.wait_ge(cleared, 6)
            flat = slots_x.rearrange("(p r) d -> p (r d)", p=P)
            per = ST * D // 10
            def zero(i):
                sp.dma_start(flat[:, bass.ds(i * per, per)], ZERO[:, 0:per]).then_inc(zeroed, 16)

            def save(c, src, rdy_a, rdy_d, n, s):
                sp.wait_ge(rdy_a, n)
                sp.wait_ge(rdy_d, n)
                sp.dma_start(XT[:, :, bass.ds(c * CT, CT)], src).then_inc(s, 16)

            zero(0)
            zero(1)
            with sp.Fori(0, B) as b:
                for i in range(2):
                    save(2 * b + i, X1T[:, i], t1_a, t1_d, 2 * b + i + 1, xt_save[i])
                    zero(2 * b + i + 2)
            with sp.Fori(0, CH) as d:
                sp.wait_ge(ln[2][4], TPC * (d + 1))
                sp.dma_start(XN3T[:, bass.ds(TPC * d, TPC), :], XN3C).then_inc(xt_save[1], 16)
                save(d, X2T, t3_a, t3_d, d + 1, xt_save[0])
            sp.wait_ge(r_ps, CH)
            for e in range(0, E, 4):
                sp.dma_start(WGU[:, e:e + 4].rearrange("p e k f -> p (e k) f"),
                             wgu[e:e + 4].rearrange("e (k p) f -> p (e k) f", p=P)).then_inc(ld_exp, 16)
            sp.dma_start(WDN, wdn.rearrange("e p d -> p e d")).then_inc(ld_exp, 16)

            sp.wait_ge(sc, 16 * 2 * T)

            def load(k, g):
                wait(sp, e_t, 4 * (g - 1) + k + 1)
                sp.dma_start(XE[:, k, :], slots_x[bass.ds((4 * g + k) * P, P), :]).then_inc(xe_in[k], 16)

            def store(k, g):
                sp.wait_ge(e_yev, 4 * g + k + 1)
                sp.dma_start(slots_y[bass.ds((4 * g + k) * P, P), :], YE[:, k, :]).then_inc(ye_out[k], 16)

            for k in range(4):
                load(k, 0)
            for k in range(4):
                load(k, 1)
            with sp.Fori(2, ST // 4) as g:
                for k in range(4):
                    load(k, g)
                    store(k, g - 2)
            for g in range(ST // 4 - 2, ST // 4):
                for k in range(4):
                    store(k, g)
            for c in range(CH):
                sp.wait_ge(comb, TPC * (c + 1))
                sp.dma_start(tok(out, c), X[:, TPC * c:TPC * c + TPC, :]).then_inc(stored, 16)
            sp.wait_ge(stored, 16 * CH)

        @block.gpsimd
        def _(pool):
            pool.memset(R[:, :], 0.0).then_inc(cleared, 1)
            pool.memset(ZERO, 0.0).then_inc(cleared, 1)
            pool.memset(ONES[:, :], 1.0).then_inc(cleared, 1)
            pool.memset(EPS[:, :], KEPS).then_inc(cleared, 1)
            pool.memset(HALF[:, :], -0.5).then_inc(cleared, 1)
            pool.memset(KVN[:, 0, :], 0.0).then_inc(cleared, 1)
            pool.memset(VEXT, 1.0).then_inc(cleared, 1)

            def rstd(c, n):
                _, mv, ve, rs = lnbuf[n]
                _, s_mv, s_ve, s_rstd, _ = ln[n]
                pool.wait_ge(s_mv, TPC * (c + 1))
                apart(pool)
                pool.tensor_scalar(ve[:, :], mv[:, :, 1], LN_EPS, None, ALU.add).then_inc(s_ve, 1)
                pool.wait_ge(s_ve, c + 1)
                pool.tensor_tensor(rs[:, :], ve[:, :], HALF[:, :], ALU.pow).then_inc(s_rstd, 1)

            pool.wait_ge(cleared, 7)
            with pool.Fori(0, CH) as c:
                rstd(c, 0)
            pool.wait_ge(ln[0][4], TPC * CH)
            pool.wait_ge(ld_const, 16 * NCONST)
            with pool.Fori(0, CH) as c:
                xc = X[:, bass.ds(TPC * c, TPC), :]
                pool.tensor_tensor(xc, xc, BOR[:, None, :].to_broadcast((P, TPC, D)), ALU.add).then_inc(bo_in, 1)
            rstd(0, 1)
            with pool.Fori(1, CH) as c:
                rstd(c - 1, 2)
                rstd(c, 1)
            rstd(CH - 1, 2)

            pool.wait_ge(slots_rdy, 1)
            pool.wait_ge(zeroed, 160)
            pool.wait_ge(xt_save[1], 16 * (B + CH))
            for t in range(T):
                for j in range(2):
                    pool.indirect_dma_start(slots_x, bass.IndirectOffsetOnAxis(ap=SLOT[:, j, t:t + 1], axis=0),
                                            XN3T[:, t, :], None).then_inc(sc, 16)
            for k in range(4):
                pool.wait_ge(ye_out[k], 16 * (ST // 4))
            for t in range(T):
                if t >= 8:
                    pool.wait_ge(comb, t - 7)
                for j in range(2):
                    k = 2 * (t % 8) + j
                    pool.indirect_dma_start(YG[:, k, :], None, slots_y,
                                            bass.IndirectOffsetOnAxis(ap=SLOT[:, j, t:t + 1], axis=0)).then_inc(yg_in[k], 16)

        @block.scalar
        def _(act):
            for dst, src in ((IDENT[:, :], ident_d), (TRI[:, :], tri_d),
                             (BQK[:, 0, :], bq.rearrange("(k p) -> p k", p=P)), (BQK[:, 1, :], bk.rearrange("(k p) -> p k", p=P)),
                             (XB[:, 0, :], xbq.rearrange("(k p) -> p k", p=P)), (XB[:, 1, :], xbk.rearrange("(k p) -> p k", p=P)),
                             (XB[:, 2, :], xbv.rearrange("(k p) -> p k", p=P)),
                             (BVR[:, :], bv[None, :].to_broadcast((P, D))), (BOR[:, :], bo[None, :].to_broadcast((P, D))),
                             (XBOR[:, :], xbo[None, :].to_broadcast((P, D))),
                             (DESC[:, :], desc16_d.to_broadcast((P, E))), (IOTA[:, :], iota_d.to_broadcast((P, ST)))):
                with nc.allow_non_contiguous_dma(reason="a few hundred bias values"):
                    act.dma_start(dst, src).then_inc(ld_const, 16)
            act.wait_ge(cleared, 1)
            act.dma_start(R[64:128, :], normblk_d).then_inc(ld_const, 16)
            for h in range(4):
                act.dma_start(R[DK * h:DK * h + DK, M * h:M * h + M], orfT).then_inc(orf_in, 16)

            def exp_k(c, j, par):
                for half in range(2):
                    n = TPC * c + j
                    act.wait_ge(kf_ps, 2 * n + half + 1)
                    if half == 0:
                        wait(act, kv_ps, n - 1)
                    act.activation(KPHI[:, j % 2, 512 * half:512 * half + 512], pF[half][:, :], ACT.Exp).then_inc(k_exp, 1)

            def square(c, dst, lin, sq):
                for q in range(4):
                    act.wait_ge(lin, 4 * c + q + 1)
                    act.activation(dst[64:128, q, :], dst[0:64, q, :], ACT.Square).then_inc(sq, 1)

            def front(c, par):
                act.wait_ge(t1_ps, 2 * c + 1)
                wait(act, xt_save[par], 16 * ((c - par) // 2))
                act.copy(X1T[:, par, 0, :], pT[0][:, :]).then_inc(t1_a, 1)

            def body1(c, d, par):
                if d is not None:
                    exp_k(d, 0, 1 - par)
                if c is not None:
                    front(c, par)
                if d is not None:
                    exp_k(d, 1, 1 - par)
                if c is not None:
                    square(c, KDT[:, par], k_lin, k_sq)
                if d is not None:
                    exp_k(d, 2, 1 - par)
                    exp_k(d, 3, 1 - par)

            body1(0, None, 0)
            body1(1, 0, 1)
            with act.Fori(1, B) as b:
                body1(2 * b, 2 * b - 1, 0)
                body1(2 * b + 1, 2 * b, 1)
            body1(None, CH - 1, 0)

            def exp_q(c, lo, hi):
                for i in range(lo, hi):
                    act.wait_ge(qf_ps, 8 * c + i + 1)
                    act.activation(QPHI[:, i, :], pF[i % 2][:, :], ACT.Exp).then_inc(q_exp, 1)

            def body2(c, d):
                if c is not None:
                    square(c, KDT[:, 0], q_lin, q_sq)
                if d is not None:
                    act.wait_ge(t2_ps, 2 * d + 1)
                    act.wait_ge(xt_save[0], 16 * (B + d))
                    act.copy(X2T[:, 0, :], pT[0][:, :]).then_inc(t2_a, 1)
                if c is not None:
                    exp_q(c, 0, 4)
                if d is not None:
                    act.wait_ge(s_dif, d + 1)
                    act.activation(PEXP, SDIF, ACT.Exp, scale=float(D) ** -0.5).then_inc(s_exp, 1)
                if c is not None:
                    exp_q(c, 4, 8)
                if d is not None:
                    act.wait_ge(pt_ps, d + 1)
                    act.copy(PROBT[0:SKV, :], pT[0][0:SKV, :]).then_inc(pt_ev, 1)
                if c is not None:
                    act.wait_ge(at_ps, 2 * c + 1)
                    act.copy(AT[:, 0, :], pT[0][:, :]).then_inc(at_a, 1)
                if d is not None:
                    act.wait_ge(t3_ps, 2 * d + 1)
                    act.copy(X2T[:, 0, :], pT[0][:, :]).then_inc(t3_a, 1)

            act.wait_ge(zeroed, 160)
            body2(0, None)
            with act.Fori(1, CH) as c:
                body2(c, c - 1)
            body2(None, CH - 1)

            act.wait_ge(probe_max, 1)
            act.activation(TMP[1], TMP[0], ACT.Exp).then_inc(rt_a, 1)
            act.activation(SIG[:, :], LOG[:, :, E], ACT.Exp, scale=-1.0).then_inc(rt_a, 1)

            def shared(u):
                for f in range(NF):
                    i = NF * u + f
                    act.wait_ge(g_ps, i + 1)
                    wait(act, h_rdy, i - 1)
                    act.activation(SIL[f % 2][0:SF[f], :], pK[f % 2][0:SF[f], :], ACT.Silu).then_inc(silu, 1)

            shared(0)
            with act.Fori(1, CH // 2) as u:
                shared(u)

            def copy_xt(s, k):
                act.wait_ge(e_t, s + 1)
                wait(act, e_gu, s - 1)
                act.copy(XET[:, k % 2, :], pT[k % 2][:, 0:D]).then_inc(e_tev, 1)

            def silu_e(s, k):
                act.wait_ge(e_gu, s + 1)
                wait(act, e_h, s - 1)
                act.activation(ESIL[:, k % 2, :], pK[k % 2][:, 0:FF], ACT.Silu).then_inc(e_silu, 1)

            def copy_y(s, k, g):
                act.wait_ge(e_dn, s + 1)
                wait(act, ye_out[k % 4], 16 * g)
                act.copy(YE[:, k % 4, :], pO[k % 2][:, 0:D]).then_inc(e_yev, 1)

            def expert(s, k, g):
                copy_xt(s, k)
                silu_e(s - 1, k - 1)
                copy_y(s - 3, k - 3, g if k % 4 == 3 else g - 1)

            for s in range(4):
                copy_xt(s, s)
                if s >= 1:
                    silu_e(s - 1, s - 1)
                if s >= 3:
                    copy_y(s - 3, s - 3, 0)
            for s in range(4, 8):
                expert(s, s, 1)
            with act.Fori(2, ST // 4) as g:
                for k in range(4):
                    expert(4 * g + k, k, g)
            silu_e(ST - 1, 3)
            for s in range(ST - 3, ST):
                copy_y(s, s, s // 4)
            with act.Fori(CH // 2, CH) as u:
                shared(u)

        @block.tensor
        def _(pe):
            def mm(out_, lhsT, rhs, start=True, stop=True, **kw):
                return pe.matmul(out_, lhsT, rhs, start=start, stop=stop, **kw)

            def project(dst, w, src, m):
                for k in range(KD):
                    last = mm(dst, w[:, k, m * P:m * P + P], src[k], start=(k == 0), stop=(k == KD - 1))
                return last

            pe.wait_ge(ld_ctx, 16 * 5)
            pe.wait_ge(ld_const, 16 * NCONST)
            W2 = B * SKV
            for m in range(KD):
                project(pT[m][:, 0:W2], XWK, [CTXT[:, 0, :], CTXT[:, 1, :]], m).then_inc(prep_ps, 1)
            for m in range(KD):
                project(pK[m][:, 0:W2], XWV, [CTXT[:, 0, :], CTXT[:, 1, :]], m).then_inc(prep_ps, 1)
            pe.wait_ge(prep_ev, 2)
            for m in range(KD):
                project(pF[m][:, 0:W2], XWQ, [KT[:, 0, :], KT[:, 1, :]], m).then_inc(prep_ps, 1)
            for k in range(KD):
                last = mm(pO[0][0:1, 0:W2], XB[:, 0, k:k + 1], KT[:, k, :], start=(k == 0), stop=(k == KD - 1))
            last.then_inc(prep_ps, 1)
            pe.wait_ge(prep_ev, 4)
            for b in range(B):
                dst = (pT[b // 2])[0:SKV, D * (b % 2):D * (b % 2) + D]
                for k in range(KD):
                    last = mm(dst, VT[:, k, b * SKV:b * SKV + SKV], XWO[:, k, :], start=(k == 0), stop=(k == KD - 1))
                last.then_inc(prep_ps, 1)
            pe.wait_ge(prep_ev, 11)

            def t1(c):
                pe.wait_ge(ln[0][4], TPC * (c + 1))
                wait(pe, v_ev, 2 * c)
                for h in range(KD):
                    for j in range(TPC):
                        last = pe.transpose(pT[h][:, j * P:j * P + P], XN[:, j, h * P:h * P + P], IDENT[:, :])
                    last.then_inc(t1_ps, 1)

            def k_proj(c, par):
                pe.wait_ge(t1_a, c + 1)
                pe.wait_ge(t1_d, c + 1)
                for m in range(KD):
                    project(pK[m][:, :], WK, [X1T[:, par, k, :] for k in range(KD)], m).then_inc(k_ps, 1)

            def v_proj(c, par):
                for j in range(TPC):
                    for k in range(KD):
                        last = mm(pT[j // 2][:, D * (j % 2):D * (j % 2) + D], X1T[:, par, k, j * P:j * P + P], WV[:, k, :],
                                  start=(k == 0), stop=(k == KD - 1))
                    if j % 2:
                        last.then_inc(v_ps, 1)

            def k_feat(c, j, par):
                for half in range(2):
                    n = TPC * c + j
                    if j == 0:
                        pe.wait_ge(k_sq, 4 * c + 2 * half + 2)
                    wait(pe, k_exp, 2 * n - 1 + half)
                    for q in range(2):
                        last = mm(pF[half][:, 256 * q:256 * q + 256], KDT[:, par, 2 * half + q, j * P:j * P + P], R[:, :])
                    last.then_inc(kf_ps, 1)

            def kv(c, j, par):
                n = TPC * c + j
                if j == 0:
                    pe.wait_ge(v_ev, 2 * c + 2)
                first = j == 0 and par == 0
                if first:
                    wait(pe, kv_ev, c)
                pe.wait_ge(k_exp, 2 * n + 2)
                mm(pO[0][:, 0:HV], EPS[:, :], VEXT[:, par, j, :], start=first, stop=False, skip_group_check=True)
                for p in range(PAIRS):
                    last = mm(pO[0][:, HV2 * p:HV2 * p + HV2], KPHI[:, j % 2, P * p:P * p + P],
                              VEXT[:, par, j, HV2 * p:HV2 * p + HV2], start=False, stop=(j == TPC - 1 and par == 1 and p == PAIRS - 1),
                              skip_group_check=True)
                last.then_inc(kv_ps, 1)

            def body1(c, d, par):
                if d is not None:
                    k_feat(d, 0, 1 - par)
                if c is not None:
                    t1(c)
                if d is not None:
                    k_feat(d, 1, 1 - par)
                    kv(d, 0, 1 - par)
                if c is not None:
                    k_proj(c, par)
                if d is not None:
                    k_feat(d, 2, 1 - par)
                    kv(d, 1, 1 - par)
                if c is not None:
                    v_proj(c, par)
                if d is not None:
                    k_feat(d, 3, 1 - par)
                    kv(d, 2, 1 - par)
                    kv(d, 3, 1 - par)

            pe.wait_ge(ld_attn, 16 * 4)
            pe.wait_ge(r_ready, 1)
            body1(0, None, 0)
            body1(1, 0, 1)
            with pe.Fori(1, B) as b:
                body1(2 * b, 2 * b - 1, 0)
                body1(2 * b + 1, 2 * b, 1)
            body1(None, CH - 1, 0)
            pe.wait_ge(kv_ev, 2 * B)
            for b in range(B):
                mm((pT + pK)[b][:, 0:HV], EPS[:, :], KVX[:, b, :]).then_inc(nb_ps, 1)
            pe.wait_ge(nb_ev, B)
            for i in range(2):
                pe.wait_ge(xt_save[i], 16 * B)

            def q_proj(c):
                wait(pe, r_ev, c)
                for m in range(KD):
                    project(pK[m][:, :], WQ, [XT[:, k, bass.ds(c * CT, CT)] for k in range(KD)], m).then_inc(q_ps, 1)

            def q_feat(c, lo, hi):
                for i in range(lo, hi):
                    pe.wait_ge(q_sq, 4 * c + i // 2 + 1)
                    if i >= 2:
                        pe.wait_ge(q_exp, 8 * c + i - 1)
                    mm(pF[i % 2][:, :], R[:, P * (i % 2):P * (i % 2) + P], KDT[:, 0, i // 2, :]).then_inc(qf_ps, 1)

            def num(c, d):
                pe.wait_ge(q_exp, 8 * c + 8)
                for j in range(TPC):
                    if j == 1 and d is not None:
                        pe.wait_ge(s_dif, d + 1)
                    if j >= 2:
                        pe.wait_ge(n_step, 8 * c + 2 * (j - 2) + 1)
                    for p in range(PAIRS):
                        last = mm(pN[j % 2][:, HV2 * p:HV2 * p + HV2], QPHI[:, p, j * P:j * P + P],
                                  KVX[:, c // 2, HV2 * p:HV2 * p + HV2])
                    last.then_inc(n_ps, 1)

            def transpose_chunk(src, ps):
                for h in range(KD):
                    for j in range(TPC):
                        last = pe.transpose(pT[h][:, j * P:j * P + P], src(j, h), IDENT[:, :])
                    last.then_inc(ps, 1)

            def att_t(c):
                pe.wait_ge(att_rdy, TPC * (c + 1))
                transpose_chunk(lambda j, h: ATT[:, j, h * P:h * P + P], at_ps)

            def wo(c, d):
                pe.wait_ge(at_a, c + 1)
                pe.wait_ge(at_d, c + 1)
                if d is not None:
                    pe.wait_ge(x2, 2 * d + 2)
                for j in range(TPC):
                    for k in range(KD):
                        last = mm(pO[j // 2][:, D * (j % 2):D * (j % 2) + D], AT[:, k, j * P:j * P + P], WO[:, k, :],
                                  start=(k == 0), stop=(k == KD - 1))
                    if j % 2:
                        last.then_inc(wo_ps, 1)

            def t2(d):
                pe.wait_ge(ln[1][4], TPC * (d + 1))
                transpose_chunk(lambda j, h: XN[:, j, h * P:h * P + P], t2_ps)

            def scores(d):
                pe.wait_ge(t2_a, d + 1)
                pe.wait_ge(t2_d, d + 1)
                for j in range(TPC):
                    for k in range(KD):
                        mm(pS[:, j, 0:SKV], X2T[:, k, j * P:j * P + P], GK[:, k, bass.ds((d // 2) * SKV, SKV)],
                           start=(k == 0), stop=False)
                    last = mm(pS[:, j, 0:SKV], ONES[0:1, :], GQ[0:1, bass.ds((d // 2) * SKV, SKV)], start=False)
                last.then_inc(s_ps, 1)

            def prob_t(d):
                pe.wait_ge(prob, d + 1)
                for j in range(TPC):
                    last = pe.transpose(pT[0][0:SKV, j * P:j * P + P], PROB[:, j, :], IDENT[:, :])
                last.then_inc(pt_ps, 1)

            def out_x(d):
                pe.wait_ge(pt_ev, d + 1)
                for j in range(TPC):
                    dst = pO[j // 2][:, D * (j % 2):D * (j % 2) + D]
                    for k in range(KD):
                        mm(dst, X2T[:, k, j * P:j * P + P], XWO[:, k, :], start=(k == 0), stop=False)
                    last = mm(dst, PROBT[0:SKV, j * P:j * P + P], VP[0:SKV, d // 2, :], start=False)
                    if j % 2:
                        last.then_inc(o_ps, 1)

            def t3(d):
                pe.wait_ge(ln[2][4], TPC * (d + 1))
                transpose_chunk(lambda j, h: XN3C[:, j, h * P:h * P + P], t3_ps)

            def router(d):
                pe.wait_ge(t3_a, d + 1)
                pe.wait_ge(t3_d, d + 1)
                for j in range(TPC):
                    for k in range(KD):
                        last = mm(pR[:, j, 0:E + 1], X2T[:, k, j * P:j * P + P], GW[:, k, :],
                                  start=(k == 0), stop=(k == KD - 1))
                last.then_inc(r_ps, 1)

            def body2(c, d):
                if c is not None:
                    q_proj(c)
                if d is not None:
                    t2(d)
                if c is not None:
                    q_feat(c, 0, 4)
                if d is not None:
                    scores(d)
                if c is not None:
                    q_feat(c, 4, 8)
                    num(c, d)
                if d is not None:
                    prob_t(d)
                    out_x(d)
                if c is not None:
                    att_t(c)
                    wo(c, d)
                if d is not None:
                    t3(d)
                    router(d)

            pe.wait_ge(ld_ffn, 16 * 5)
            body2(0, None)
            with pe.Fori(1, CH) as c:
                body2(c, c - 1)
            body2(None, CH - 1)

            pe.wait_ge(mask_rdy, 1)
            mm(pT[0][:, :], TRI[:, :], TMP[4])
            mm(pT[1][:, :], ONES[:, :], TMP[4]).then_inc(rt_ps, 1)

            def gate_up(u, f):
                i = NF * u + f
                wait(pe, h_rdy, i - 1)
                if SF[f] < P:
                    apart(pe)
                src = [XT[:, k, bass.ds(u * CT, CT)] for k in range(KD)]
                for w, dst, s in ((SG, pK[f % 2], g_ps), (SU, pF[f % 2], u_ps)):
                    for k in range(KD):
                        last = mm(dst[0:SF[f], :], w[:, k, f * P:f * P + SF[f]], src[k], start=(k == 0), stop=(k == KD - 1))
                    last.then_inc(s, 1)

            def down(u, f):
                i = NF * u + f
                pe.wait_ge(h_rdy, i + 1)
                if f == 0:
                    wait(pe, s_res, TPC * u)
                for j in range(TPC):
                    last = mm(pO[j // 2][:, D * (j % 2):D * (j % 2) + D], HT[f % 3][0:SF[f], j * P:j * P + P], SD[0:SF[f], f, :],
                              start=(f == 0 and j % 2 == 0), stop=(f == NF - 1 and j % 2 == 1), skip_group_check=True)
                last.then_inc(d_ps, 1)

            def shared(u):
                gate_up(u, 0)
                for f in range(1, NF):
                    gate_up(u, f)
                    down(u, f - 1)
                down(u, NF - 1)

            pe.wait_ge(xt_save[0], 16 * (B + CH))
            shared(0)
            with pe.Fori(1, CH // 2) as u:
                shared(u)

            pe.wait_ge(ld_exp, 16 * 5)
            pe.wait_ge(s_res, TPC * (CH // 2))
            pe.wait_ge(eid_rdy, 1)

            def tx(s, k, g):
                pe.wait_ge(xe_in[k % 4], 16 * (g + 1))
                wait(pe, e_tev, s - 1)
                for h in range(KD):
                    last = pe.transpose(pT[k % 2][:, h * P:h * P + P], XE[:, k % 4, h * P:h * P + P], IDENT[:, :])
                last.then_inc(e_t, 1)

            def gu(s, k):
                e = pe.value_load(EID[0:1, bass.ds(s, 1)], min_val=0, max_val=E - 1)
                pe.wait_ge(e_tev, s + 1)
                wait(pe, e_h, s - 1)
                for h in range(KD):
                    last = mm(pK[k % 2][:, 0:2 * FF], XET[:, k % 2, h * P:h * P + P], WGU[:, e, h, :],
                              start=(h == 0), stop=(h == KD - 1))
                last.then_inc(e_gu, 1)

            def th(s, k):
                pe.wait_ge(e_h, s + 1)
                wait(pe, e_htev, s - 1)
                pe.transpose(pF[k % 2][:, 0:P], HE[:, k % 2, :], IDENT[:, :]).then_inc(e_ht, 1)

            def dn(s, k):
                e = pe.value_load(EID[0:1, bass.ds(s, 1)], min_val=0, max_val=E - 1)
                pe.wait_ge(e_htev, s + 1)
                wait(pe, e_yev, s - 1)
                mm(pO[k % 2][:, 0:D], HET[:, k % 2, :], WDN[:, e, :]).then_inc(e_dn, 1)

            def expert(s, k, g):
                tx(s, k, g)
                gu(s - 1, k - 1)
                th(s - 2, k - 2)
                dn(s - 3, k - 3)

            for s in range(4):
                tx(s, s, 0)
                if s >= 1:
                    gu(s - 1, s - 1)
                if s >= 2:
                    th(s - 2, s - 2)
                if s >= 3:
                    dn(s - 3, s - 3)
            for s in range(4, 8):
                expert(s, s, 1)
            with pe.Fori(2, ST // 4) as g:
                for k in range(4):
                    expert(4 * g + k, k, g)
            gu(ST - 1, ST - 1)
            th(ST - 2, ST - 2)
            dn(ST - 3, ST - 3)
            th(ST - 1, ST - 1)
            dn(ST - 2, ST - 2)
            dn(ST - 1, ST - 1)
            pe.wait_ge(e_yev, ST)
            with pe.Fori(CH // 2, CH) as u:
                shared(u)

        @block.vector
        def _(dve):
            def stats(c, n):
                st, mv = lnbuf[n][0], lnbuf[n][1]
                for j in range(TPC):
                    dve.bn_stats(st[:, j, :], X[:, TPC * c + j, :]).then_inc(ln[n][0], 1)
                dve.wait_ge(ln[n][0], TPC * (c + 1))
                apart(dve)
                for j in range(TPC):
                    dve.bn_aggr(mv[:, j, :], st[:, j, :]).then_inc(ln[n][1], 1)

            def normalize(c, n, dst):
                mv, rs = lnbuf[n][1], lnbuf[n][3]
                dve.wait_ge(ln[n][3], c + 1)
                for j in range(TPC):
                    dve.tensor_scalar(dst(j), X[:, TPC * c + j, :], mv[:, j, 0:1], rs[:, j:j + 1],
                                      ALU.subtract, ALU.mult).then_inc(ln[n][4], 1)

            W2 = B * SKV
            dve.wait_ge(ld_const, 16 * NCONST)
            dve.wait_ge(orf_in, 64)
            dve.tensor_scalar(R[0:64, :], R[0:64, :], float(DK) ** -0.25, None, ALU.mult).then_inc(r_ready, 1)
            for m in range(KD):
                dve.wait_ge(prep_ps, m + 1)
                dve.tensor_scalar(KT[:, m, :], pT[m][:, 0:W2], XB[:, 1, m:m + 1], None, ALU.add).then_inc(prep_ev, 1)
            for m in range(KD):
                dve.wait_ge(prep_ps, m + 3)
                dve.tensor_scalar(VT[:, m, :], pK[m][:, 0:W2], XB[:, 2, m:m + 1], None, ALU.add).then_inc(prep_ev, 1)
            for m in range(KD):
                dve.wait_ge(prep_ps, m + 5)
                dve.tensor_copy(GK[:, m, :], pF[m][:, 0:W2]).then_inc(prep_ev, 1)
            dve.wait_ge(prep_ps, 7)
            dve.tensor_copy(GQ[0:1, :], pO[0][0:1, 0:W2]).then_inc(prep_ev, 1)
            for b in range(B):
                dve.wait_ge(prep_ps, 8 + (b | 1))
                dve.tensor_tensor(VP[0:SKV, b, :], pT[b // 2][0:SKV, D * (b % 2):D * (b % 2) + D], XBOR[0:SKV, :],
                                  ALU.add).then_inc(prep_ev, 1)

            def linear(c, dst, bias, ps, lin):
                for q in range(4):
                    r = 64 * (q % 2)
                    dve.wait_ge(ps, 2 * c + q // 2 + 1)
                    dve.tensor_scalar(dst[0:64, q, :], pK[q // 2][r:r + 64, :], bias[r:r + 64, q // 2:q // 2 + 1], None,
                                      ALU.add).then_inc(lin, 1)

            def body1(c, d, par):
                if c is not None:
                    stats(c, 0)
                    wait(dve, t1_ps, 2 * c)
                    normalize(c, 0, lambda j: XN[:, j, :])
                    dve.wait_ge(t1_ps, 2 * c + 2)
                    wait(dve, xt_save[par], 16 * ((c - par) // 2))
                    dve.tensor_copy(X1T[:, par, 1, :], pT[1][:, :]).then_inc(t1_d, 1)
                    if d is not None:
                        wait(dve, kf_ps, 8 * d)
                    linear(c, KDT[:, par], BQK[:, 1], k_ps, k_lin)
                    if d is not None:
                        wait(dve, kv_ps, TPC * d)
                    for i in range(2):
                        dve.wait_ge(v_ps, 2 * c + i + 1)
                        dve.tensor_tensor(
                            VEXT[:, par, 2 * i:2 * i + 2, :].rearrange("p j (h e) -> p j h e", h=H)[:, :, :, 0:DK],
                            pT[i][:, :].rearrange("p (j h e) -> p j h e", j=2, h=H),
                            BVR[:, None, :].to_broadcast((P, 2, D)).rearrange("p j (h e) -> p j h e", h=H),
                            ALU.add).then_inc(v_ev, 1)
                if d is not None and par == 0:
                    dve.wait_ge(kv_ps, TPC * (d + 1))
                    b = (d - 1) // 2 if isinstance(d, int) else (d - 1) // 2
                    state = pO[0][:, 0:HV].rearrange("p (q e) -> p q e", q=PAIRS)
                    kvx = KVX[:, b, :].rearrange("p (q e) -> p q e", q=PAIRS)
                    dve.tensor_copy(kvx[0:64, :, 0:DK + 1], state[0:64, :, 0:DK + 1]).then_inc(kv_ev, 1)
                    dve.tensor_copy(kvx[64:128, :, DK + 1:HV2], state[64:128, :, DK + 1:HV2]).then_inc(kv_ev, 1)

            dve.wait_ge(cleared, 7)
            dve.wait_ge(ld_x, 16 * CH)
            body1(0, None, 0)
            body1(1, 0, 1)
            with dve.Fori(1, B) as b:
                body1(2 * b, 2 * b - 1, 0)
                body1(2 * b + 1, 2 * b, 1)
            body1(None, CH - 1, 0)
            for b in range(B):
                dve.wait_ge(nb_ps, b + 1)
                dve.tensor_copy(NB[:, b, :], (pT + pK)[b][:, 0:HV]).then_inc(nb_ev, 1)
            dve.memset(LOG[:, :, :], 0.0).then_inc(r_ev, 1)

            def attend(c):
                for j in range(TPC):
                    dve.wait_ge(n_ps, TPC * c + j + 1)
                    ns = NSUM[:, j % 2, :].rearrange("p (h e) -> p h e", h=H)
                    dve.tensor_tensor(NSUM[:, j % 2, :], pN[j % 2][:, 0:HV], NB[:, c // 2, :], ALU.add).then_inc(n_step, 1)
                    dve.wait_ge(n_step, 8 * c + 2 * j + 1)
                    dve.reciprocal(REC[:, j % 2, :], ns[:, :, DK]).then_inc(n_step, 1)
                    dve.wait_ge(n_step, 8 * c + 2 * j + 2)
                    dve.tensor_tensor(ATT[:, j, :].rearrange("p (h e) -> p h e", h=H), ns[:, :, 0:DK],
                                      REC[:, j % 2, :, None].to_broadcast((P, H, DK)), ALU.mult).then_inc(att_rdy, 1)

            def residual(c, ps, done):
                for i in range(2):
                    dve.wait_ge(ps, 2 * c + i + 1)
                    xc = X[:, bass.ds(TPC * c + 2 * i, 2), :]
                    dve.tensor_tensor(xc, pO[i][:, :].rearrange("p (j d) -> p j d", j=2), xc, ALU.add).then_inc(done, 1)

            def softmax(d):
                dve.wait_ge(s_ps, d + 1)
                dve.tensor_reduce(SMX[:, 0, :], pS[:, :, 0:SKV], AX_X, ALU.max).then_inc(s_max, 1)
                dve.wait_ge(s_max, d + 1)
                dve.tensor_tensor(SDIF, pS[:, :, 0:SKV], SMX[:, 0, :, None].to_broadcast((P, TPC, SKV)),
                                  ALU.subtract).then_inc(s_dif, 1)
                dve.wait_ge(s_exp, d + 1)
                dve.tensor_reduce(SMX[:, 1, :], PEXP, AX_X, ALU.add).then_inc(s_step, 1)
                dve.wait_ge(s_step, 2 * d + 1)
                dve.reciprocal(SMX[:, 2, :], SMX[:, 1, :]).then_inc(s_step, 1)
                dve.wait_ge(s_step, 2 * d + 2)
                dve.tensor_tensor(PROB, PEXP, SMX[:, 2, :, None].to_broadcast((P, TPC, SKV)),
                                  ALU.mult).then_inc(prob, 1)

            def body2(c, d):
                if c is not None:
                    linear(c, KDT[:, 0], BQK[:, 0], q_ps, q_lin)
                if d is not None:
                    dve.wait_ge(t2_ps, 2 * d + 2)
                    dve.wait_ge(xt_save[0], 16 * (B + d))
                    dve.tensor_copy(X2T[:, 1, :], pT[1][:, :]).then_inc(t2_d, 1)
                    softmax(d)
                if c is not None:
                    attend(c)
                if d is not None:
                    residual(d, o_ps, x2)
                    dve.wait_ge(x2, 2 * d + 2)
                    apart(dve)
                    stats(d, 2)
                if c is not None:
                    dve.wait_ge(at_ps, 2 * c + 2)
                    dve.tensor_copy(AT[:, 1, :], pT[1][:, :]).then_inc(at_d, 1)
                if d is not None:
                    dve.wait_ge(xt_save[1], 16 * (B + d))
                    normalize(d, 2, lambda j: XN3C[:, j, :])
                if c is not None:
                    dve.wait_ge(bo_in, c + 1)
                    residual(c, wo_ps, x1)
                if d is not None:
                    dve.wait_ge(t3_ps, 2 * d + 2)
                    dve.tensor_copy(X2T[:, 1, :], pT[1][:, :]).then_inc(t3_d, 1)
                if c is not None:
                    dve.wait_ge(x1, 2 * c + 2)
                    apart(dve)
                    stats(c, 1)
                if d is not None:
                    dve.wait_ge(r_ps, d + 1)
                    dve.tensor_copy(LOG[:, bass.ds(TPC * d, TPC), :], pR[:, :, 0:E + 1]).then_inc(r_ev, 1)
                if c is not None:
                    normalize(c, 1, lambda j: XN[:, j, :])

            dve.wait_ge(r_ev, 1)
            body2(0, None)
            with dve.Fori(1, CH) as c:
                body2(c, c - 1)
            body2(None, CH - 1)

            steps = [0]

            def step(ins):
                steps[0] += 1
                ins.then_inc(rt, 1)
                dve.wait_ge(rt, steps[0])

            def te(i):
                return TMP[i].rearrange("p (t e) -> p t e", e=E)

            def over_e(a):
                return a[:, :, None].to_broadcast((P, T, E))

            MX, SUM, RSUM, M1, M2, PK1, PK2 = (SMALL[:, i, :] for i in range(7))
            desc = DESC[:, None, :].to_broadcast((P, T, E))
            dve.wait_ge(r_ev, CH + 1)
            step(dve.tensor_reduce(MX, LOG[:, :, 0:E], AX_X, ALU.max))
            dve.tensor_tensor(te(0), LOG[:, :, 0:E], over_e(MX), ALU.subtract).then_inc(probe_max, 1)
            dve.wait_ge(rt_a, 2)
            step(dve.tensor_reduce(SUM, te(1), AX_X, ALU.add))
            step(dve.reciprocal(RSUM, SUM))
            step(dve.tensor_tensor(te(2), te(1), over_e(RSUM), ALU.mult))
            step(dve.tensor_reduce(M1, te(2), AX_X, ALU.max))
            step(dve.tensor_tensor(te(0), te(2), over_e(M1), ALU.is_equal))
            step(dve.tensor_tensor(te(0), te(0), desc, ALU.mult))
            step(dve.tensor_reduce(PK1, te(0), AX_X, ALU.max))
            step(dve.tensor_tensor(te(1), desc, over_e(PK1), ALU.is_equal))
            step(dve.scalar_tensor_tensor(te(3), te(1), -4.0, te(2), ALU.mult, ALU.add))
            step(dve.tensor_reduce(M2, te(3), AX_X, ALU.max))
            step(dve.tensor_tensor(te(0), te(3), over_e(M2), ALU.is_equal))
            step(dve.tensor_tensor(te(0), te(0), desc, ALU.mult))
            step(dve.tensor_reduce(PK2, te(0), AX_X, ALU.max))
            step(dve.tensor_tensor(te(2), desc, over_e(PK2), ALU.is_equal))
            dve.tensor_tensor(te(4), te(1), te(2), ALU.add).then_inc(mask_rdy, 1)
            step(dve.tensor_tensor(SUM, M1, M2, ALU.add))
            step(dve.reciprocal(RSUM, SUM))
            step(dve.tensor_tensor(RW[:, 0, :], M1, RSUM, ALU.mult))
            step(dve.tensor_tensor(RW[:, 1, :], M2, RSUM, ALU.mult))
            step(dve.tensor_scalar(SIG[:, :], SIG[:, :], 1.0, None, ALU.add))
            step(dve.reciprocal(SIG[:, :], SIG[:, :]))
            cum = [VP[:, :, :].rearrange("p b d -> p (b d)")[:, 0:48 * E].rearrange("p (t e) -> p t e", e=E),
                   KVN[:, 1, 0:48 * E].rearrange("p (t e) -> p t e", e=E)]
            step(dve.memset(cum[0][:, 0:16, :], 0.0))
            step(dve.memset(cum[1][:, 0:16, :], 0.0))
            dve.wait_ge(rt_ps, 1)
            step(dve.tensor_copy(cum[0][:, 16:48, :], pT[1][:, :].rearrange("p (t e) -> p t e", e=E)))
            for i in range(5):
                a, b = cum[i % 2], cum[(i + 1) % 2]
                step(dve.tensor_tensor(b[:, 16:48, :], a[:, 16:48, :], a[:, 16 - (1 << i):48 - (1 << i), :], ALU.add))
            tot = cum[1]
            cnt = TMP[3].bitcast(I32)
            step(dve.tensor_scalar(cnt[:, 0:E], tot[:, 47, :], float(P - 1), None, ALU.add))
            step(dve.tensor_scalar(cnt[:, E:2 * E], cnt[:, 0:E], 7, None, ALU.logical_shift_right))
            end = [TMP[3][:, 64:88], TMP[3][:, 96:120]]
            step(dve.memset(TMP[3][:, 64:128], 0.0))
            step(dve.tensor_copy(end[0][:, 8:24], cnt[:, E:2 * E]))
            step(dve.tensor_copy(TMP[3][:, 32:48], cnt[:, E:2 * E]))
            for i in range(4):
                a, b = end[i % 2], end[(i + 1) % 2]
                step(dve.tensor_tensor(b[:, 8:24], a[:, 8:24], a[:, 8 - (1 << i):24 - (1 << i)], ALU.add))
            step(dve.tensor_tensor(TMP[3][:, 128:144], end[0][:, 8:24], TMP[3][:, 32:48], ALU.subtract))
            step(dve.tensor_scalar(TMP[3][:, 144:160], TMP[3][:, 128:144], float(P), None, ALU.mult))
            step(dve.tensor_tensor(te(4), tot[:, 15:47, :], pT[0][:, :].rearrange("p (t e) -> p t e", e=E), ALU.add))
            step(dve.tensor_tensor(te(4), te(4), TMP[3][:, None, 144:160].to_broadcast((P, T, E)), ALU.add))
            for j in range(2):
                step(dve.tensor_tensor(te(0), te(1 + j), te(4), ALU.mult))
                step(dve.tensor_reduce(SMALL[:, 7 + j, :], te(0), AX_X, ALU.add))
            step(dve.tensor_copy(SLOT[:, 0, :], SMALL[:, 7, :]))
            dve.tensor_copy(SLOT[:, 1, :], SMALL[:, 8, :]).then_inc(slots_rdy, 1)
            ge = KVN[:, :, :].rearrange("p a n -> p (a n)")[:, 0:ST * E].rearrange("p (s e) -> p s e", e=E)
            ends = end[0][:, None, 8:24].to_broadcast((P, ST, E))
            step(dve.tensor_tensor(ge, IOTA[:, :, None].to_broadcast((P, ST, E)), ends, ALU.is_ge))
            step(dve.tensor_reduce(TMP[0][:, 0:ST], ge, AX_X, ALU.add))
            dve.tensor_scalar(EID[:, :], TMP[0][:, 0:ST], float(E - 1), None, ALU.min).then_inc(eid_rdy, 1)

            def shared(u):
                for f in range(NF):
                    i = NF * u + f
                    dve.wait_ge(u_ps, i + 1)
                    dve.wait_ge(silu, i + 1)
                    wait(dve, d_ps, i - 2)
                    dve.tensor_tensor(HT[f % 3][0:SF[f], :], SIL[f % 2][0:SF[f], :], pF[f % 2][0:SF[f], :], ALU.mult).then_inc(h_rdy, 1)
                dve.wait_ge(d_ps, NF * u + NF)
                for j in range(TPC):
                    t = TPC * u + j
                    dve.scalar_tensor_tensor(X[:, t, :], pO[j // 2][:, D * (j % 2):D * (j % 2) + D], SIG[:, bass.ds(t, 1)],
                                             X[:, t, :], ALU.mult, ALU.add).then_inc(s_res, 1)

            shared(0)
            with dve.Fori(1, CH // 2) as u:
                shared(u)

            def hidden(s, k):
                dve.wait_ge(e_silu, s + 1)
                wait(dve, e_ht, s - 1)
                dve.tensor_tensor(HE[:, k % 2, :], ESIL[:, k % 2, :], pK[k % 2][:, FF:2 * FF], ALU.mult).then_inc(e_h, 1)

            def copy_ht(s, k):
                dve.wait_ge(e_ht, s + 1)
                wait(dve, e_dn, s - 1)
                dve.tensor_copy(HET[:, k % 2, :], pF[k % 2][:, 0:P]).then_inc(e_htev, 1)

            hidden(0, 0)
            for s in range(1, 4):
                hidden(s, s)
                copy_ht(s - 1, s - 1)
            with dve.Fori(1, ST // 4) as g:
                for k in range(4):
                    hidden(4 * g + k, k)
                    copy_ht(4 * g + k - 1, k - 1)
            copy_ht(ST - 1, ST - 1)

            def combine(t):
                for j in range(2):
                    k = 2 * (t % 8) + j
                    dve.wait_ge(yg_in[k], 16 * (t // 8 + 1))
                    if j:
                        dve.wait_ge(comb1, t + 1)
                    dve.scalar_tensor_tensor(X[:, t, :], YG[:, k, :], RW[:, j, t:t + 1], X[:, t, :],
                                             ALU.mult, ALU.add).then_inc(comb if j else comb1, 1)

            tiles = 0
            for u in range(CH // 2, CH):
                shared(u)
                upto = TPC * (CH if u == CH - 1 else 2 * (u - CH // 2) + 1)
                if tiles == 0:
                    dve.wait_ge(s_res, TPC * (CH // 2))
                dve.wait_ge(s_res, TPC * (u + 1))
                while tiles < upto:
                    combine(tiles)
                    tiles += 1


_OUTS = [((B, L, D), "float32")]


def kernel(**inputs):
    import numpy as np
    import concourse.bacc as bacc
    from concourse import mybir as mb
    from concourse.bass_utils import run_bass_kernel_spmd

    g = {k: np.asarray(v) for k, v in inputs.items()}
    t = lambda a: np.ascontiguousarray(a.T)
    arrays = {
        "x": g["x"].reshape(B * L, D), "ctxT": t(g["ctx_1024"].reshape(B * SKV, D)),
        "wqT": t(g["L0_attn_Wq"]), "bq": g["L0_attn_bq"], "wkT": t(g["L0_attn_Wk"]), "bk": g["L0_attn_bk"],
        "wvT": t(g["L0_attn_Wv"]), "bv": g["L0_attn_bv"], "woT": t(g["L0_attn_Wo"]), "bo": g["L0_attn_bo"],
        "orfT": t(g["L0_attn_orf"]),
        "xwq": g["L0_xattn_Wq"], "xbq": g["L0_xattn_bq"], "xwkT": t(g["L0_xattn_Wk"]), "xbk": g["L0_xattn_bk"],
        "xwvT": t(g["L0_xattn_Wv"]), "xbv": g["L0_xattn_bv"], "xwoT": t(g["L0_xattn_Wo"]), "xbo": g["L0_xattn_bo"],
        "gwT": t(np.concatenate([g["L0_ffn_gate_w"], g["L0_ffn_shared_gate_w"]], 0)),
        "wgu": g["L0_ffn_w_gate_up"], "wdn": g["L0_ffn_w_down"],
        "sgT": t(g["L0_ffn_shared_w_gate"]), "suT": t(g["L0_ffn_shared_w_up"]), "sdT": t(g["L0_ffn_shared_w_down"]),
        "ident": np.eye(P, dtype=np.float32), "tri": np.triu(np.ones((P, P), np.float32), 1),
        "normblk": np.kron(np.eye(4, dtype=np.float32), np.full((DK, M), -0.5 * float(DK) ** -0.5, np.float32)),
        "desc16": np.arange(E, 0, -1, dtype=np.float32)[None], "iota": np.arange(ST, dtype=np.float32)[None],
    }
    nc = bacc.Bacc("TRN2", target_bir_lowering=False, num_devices=1)
    arrays = {f"in_{k}": np.ascontiguousarray(v) for k, v in arrays.items()}
    args = [nc.dram_tensor(k, v.shape, mb.dt.from_np(v.dtype), kind="ExternalInput").ap() for k, v in arrays.items()]
    shape, dtype = _OUTS[0]
    o = nc.dram_tensor("out_0", (B * L, D), mb.dt.from_np(np.dtype(dtype)), kind="ExternalOutput").ap()
    decoder_layer(nc, *args, o)
    r = run_bass_kernel_spmd(nc, [arrays], core_ids=[0])
    return r.results[0]["out_0"].reshape(shape)
```

```python
from contextlib import ExitStack

import concourse.bass as bass
from concourse import mybir

F32 = mybir.dt.float32
I32 = mybir.dt.int32
ALU = mybir.AluOpType
ACT = mybir.ActivationFunctionType
AX_X = mybir.AxisListType.X

P = 128
B, L, D = 4, 1024, 256
H, DK, M = 16, 16, 64
SKV = 77
E, FF, SFF = 16, 128, 704
T = B * L // P
TPC = 4
CH = T // TPC
CT = TPC * P
KD = D // P
HV = H * (DK + 1)
HV2 = 2 * (DK + 1)
PAIRS = H // 2
SF = [P] * (SFF // P) + ([SFF % P] if SFF % P else [])
NF = len(SF)
ST = (2 * T * P + E * (P - 1)) // P
ST = -(-ST // 8) * 8
EW = KD * 2 * FF + D
KEPS = 1e-6
LN_EPS = 1e-5
NCONST = 9
NLATE = 4


def wait(eng, sem, value):
    if not (isinstance(value, int) and value <= 0):
        eng.wait_ge(sem, value)


def decoder_layer(nc, x, ctxT, wqT, bq, wkT, bk, wvT, bv, woT, bo, orfT,
                  xwq, xbq, xwkT, xbk, xwvT, xbv, xwoT, xbo,
                  gwT, wgu, wdn, sgT, suT, sdT, ident_d, tri_d, normblk_d, desc16_d, iota_d, out):
    slots_x = nc.dram_tensor("slots_x", (ST * P, D), F32, kind="Internal").ap()
    slots_y = nc.dram_tensor("slots_y", (ST * P, D), F32, kind="Internal").ap()

    with ExitStack() as ctx:
        def sb(name, shape, dt=F32):
            return ctx.enter_context(nc.sbuf_tensor(name, shape, dt))[tuple(slice(None) for _ in shape)]

        def sem(name):
            return ctx.enter_context(nc.semaphore(name))

        def bank(name):
            return ctx.enter_context(nc.psum_tensor(name, [P, 512], F32))

        X = sb("X", [P, T, D])
        XT = sb("XT", [P, KD, T * P])
        XN3 = sb("XN3", [P, T * D])
        ARENA = sb("ARENA", [P, 12288])
        WA = sb("WA", [P, 4, KD, D])
        XWO = sb("XWO", [P, KD, D])
        VP = sb("VP", [P, B, D])
        GK = sb("GK", [P, KD, B * SKV])
        GQ = sb("GQ", [1, B * SKV])
        KVN = sb("KVN", [P, 2, B * HV])
        SG = sb("SG", [P, KD, SFF])
        SU = sb("SU", [P, KD, SFF])
        SD = sb("SD", [P, NF, D])
        GW = sb("GW", [P, KD, E + 1])
        R = sb("R", [P, 4 * M])
        IDENT = sb("IDENT", [P, P])
        TRI = sb("TRI", [P, P])
        ONES = sb("ONES", [P, P])
        EPS = sb("EPS", [P, P])
        BQK = sb("BQK", [P, 2, KD])
        XB = sb("XB", [P, 3, KD])
        BVR = sb("BVR", [P, D])
        BOR = sb("BOR", [P, D])
        XBOR = sb("XBOR", [P, D])
        HALF = sb("HALF", [P, 4])
        DEN = sb("DEN", [P, TPC, H])
        REC = sb("REC", [P, TPC, H])
        SMX = sb("SMX", [P, 3, TPC])
        SOFT = sb("SOFT", [P, 3, TPC * SKV])
        PROBT = sb("PROBT", [P, CT])
        LOG = sb("LOG", [P, T, E + 1])
        RW = sb("RW", [P, 2, T])
        SIG = sb("SIG", [P, T])
        SLOT = sb("SLOT", [P, 2, T], I32)
        EID = sb("EID", [P, ST], I32)
        SMALL = sb("SMALL", [P, 12, T])
        DESC = sb("DESC", [P, E])
        IOTA = sb("IOTA", [P, ST])
        lnbuf = [[sb(f"ln{n}_{w}", [P, TPC] + s) for w, s in (("st", [6]), ("mv", [2]), ("ve", []), ("rstd", []))]
                 for n in range(3)]

        KDT = ARENA[:, 0:4096].rearrange("p (b q n) -> p b q n", b=2, q=4)
        QPHI = ARENA[:, 4096:8192].rearrange("p (i n) -> p i n", i=8)
        XN3C = ARENA[:, 2048:3072].rearrange("p (j d) -> p j d", j=TPC)
        X3T = ARENA[:, 3072:4096].rearrange("p (h n) -> p h n", h=KD)
        X1T = ARENA[:, 6144:8192].rearrange("p (b h n) -> p b h n", b=2, h=KD)
        XN = ARENA[:, 8192:9216].rearrange("p (j d) -> p j d", j=TPC)
        X2T = ARENA[:, 9216:10240].rearrange("p (h n) -> p h n", h=KD)
        AT = ARENA[:, 10240:11264].rearrange("p (h n) -> p h n", h=KD)
        ATT = ARENA[:, 11264:12288].rearrange("p (j d) -> p j d", j=TPC)
        WEXP = ARENA.rearrange("p (e n) -> p e n", e=E)
        VEXT = XN3[:, 0:8 * HV].rearrange("p (b j n) -> p b j n", b=2, j=TPC)
        KPHI = XN3[:, 2176:4224].rearrange("p (b n) -> p b n", b=2)
        n0 = 4224
        CTXT = XN3[:, n0:n0 + 616].rearrange("p (h n) -> p h n", h=KD)
        KT = XN3[:, n0 + 616:n0 + 1232].rearrange("p (h n) -> p h n", h=KD)
        VT = XN3[:, n0 + 1232:n0 + 1848].rearrange("p (h n) -> p h n", h=KD)
        XWQ, XWK, XWV = (XN3[:, n0 + 1848 + 512 * i:n0 + 2360 + 512 * i].rearrange("p (h n) -> p h n", h=KD)
                         for i in range(3))
        XN3T = XN3[:, :].rearrange("p (t d) -> p t d", t=T)
        ZERO = ARENA[:, 4096:6144]
        KVX = KVN[:, 0, :].rearrange("p (b n) -> p b n", b=B)
        NB = KVN[:, 1, :].rearrange("p (b n) -> p b n", b=B)
        HT = [KVN[:, i // 2, 512 * (i % 2):512 * (i % 2) + 512] for i in range(3)]
        SDIF, PEXP, PROB = (SOFT[:, i, :].rearrange("p (j n) -> p j n", j=TPC) for i in range(3))
        SIL = [SOFT[:, 0:2, :].rearrange("p a n -> p (a n)")[:, 0:512], PROBT[:, :]]
        WQ, WK, WV, WO = (WA[:, i] for i in range(4))
        spare = WA[:, 1:3].rearrange("p w k n -> p (w k n)")
        KVXB = spare[:, 0:HV]
        GKB = spare[:, 272:272 + KD * 80].rearrange("p (k n) -> p k n", k=KD)
        GQB = spare[0:1, 432:432 + SKV]
        VPB = spare[:, 512:512 + D]
        TMP = [WA[:, i].rearrange("p k n -> p (k n)") for i in range(4)] + [XWO[:, :, :].rearrange("p k n -> p (k n)")] \
            + [VP[:, 2 * i:2 * i + 2, :].rearrange("p k n -> p (k n)") for i in range(2)]
        XE = XN3[:, 0:1024].rearrange("p (b d) -> p b d", b=4)
        XET = XN3[:, 1024:1536].rearrange("p (b d) -> p b d", b=2)
        ESIL = XN3[:, 1536:1792].rearrange("p (b d) -> p b d", b=2)
        HE = XN3[:, 1792:2048].rearrange("p (b d) -> p b d", b=2)
        HET = XN3[:, 2048:2304].rearrange("p (b d) -> p b d", b=2)
        YE = XN3[:, 2304:3328].rearrange("p (b d) -> p b d", b=4)
        YG = XN3[:, 4096:8192].rearrange("p (b d) -> p b d", b=16)

        pT = [bank("pT0"), bank("pT1")]
        pK = [bank("pK0"), bank("pK1")]
        pF = [bank("pF0"), bank("pF1")]
        pO = [bank("pO0"), bank("pO1")]
        pN = [pK[0], pK[1], pO[0], pO[1]]
        pS = pT[1][:, 0:TPC * 80].rearrange("p (j n) -> p j n", j=TPC)
        pR = pF[0][:, 0:TPC * 32].rearrange("p (j n) -> p j n", j=TPC)

        ld_const = sem("ld_const")
        ld_ctx = sem("ld_ctx")
        ld_late = sem("ld_late")
        ld_kv = sem("ld_kv")
        ld_attn = sem("ld_attn")
        ld_x = [sem(f"ld_x{i}") for i in range(3)]
        ld_ffn = sem("ld_ffn")
        ld_exp = sem("ld_exp")
        cleared = sem("cleared")
        orf_in = sem("orf_in")
        r_ready = sem("r_ready")
        zeroed = sem("zeroed")
        prep_ps = sem("prep_ps")
        prep_ev = sem("prep_ev")
        ln = [[sem(f"ln{n}_{w}") for w in ("st", "mv", "ve", "rstd", "xn")] for n in range(3)]
        xt_save = [sem(f"xt_save{i}") for i in range(2)]
        t1_ps, t1_a, t1_d = sem("t1_ps"), sem("t1_a"), sem("t1_d")
        k_ps, k_lin, k_sq = sem("k_ps"), sem("k_lin"), sem("k_sq")
        v_ps, v_ev = sem("v_ps"), sem("v_ev")
        kf_ps, k_exp = sem("kf_ps"), sem("k_exp")
        kv_ps, kv_ev = sem("kv_ps"), sem("kv_ev")
        nb_ps, nb_ev = sem("nb_ps"), sem("nb_ev")
        bo_in = sem("bo_in")
        q_ps, q_lin, q_sq = sem("q_ps"), sem("q_lin"), sem("q_sq")
        qf_ps, q_exp = sem("qf_ps"), sem("q_exp")
        kvx_in, xat_in = sem("kvx_in"), sem("xat_in")
        n_ps, n_add, n_rec, att_rdy = sem("n_ps"), sem("n_add"), sem("n_rec"), sem("att_rdy")
        at_ps, at_a, at_d = sem("at_ps"), sem("at_a"), sem("at_d")
        wo_ps, x1 = sem("wo_ps"), sem("x1")
        t2_ps, t2_a, t2_d = sem("t2_ps"), sem("t2_a"), sem("t2_d")
        s_ps, s_max, s_dif, s_exp, s_step, prob = (sem(n) for n in ("s_ps", "s_max", "s_dif", "s_exp", "s_step", "prob"))
        pt_ps, pt_ev = sem("pt_ps"), sem("pt_ev")
        o_ps, x2 = sem("o_ps"), sem("x2")
        t3_ps, t3_a, t3_d = sem("t3_ps"), sem("t3_a"), sem("t3_d")
        r_ps, r_ev = sem("r_ps"), sem("r_ev")
        rt = sem("rt")
        rt_a = sem("rt_a")
        rt_ps = sem("rt_ps")
        mask_rdy, probe_max, slots_rdy, eid_rdy = sem("mask_rdy"), sem("probe_max"), sem("slots_rdy"), sem("eid_rdy")
        sc = sem("sc")
        g_ps, u_ps, silu, h_rdy, d_ps, s_res = (sem(n) for n in ("g_ps", "u_ps", "silu", "h_rdy", "d_ps", "s_res"))
        xe_in = [sem(f"xe_in{k}") for k in range(4)]
        e_t, e_tev, e_gu, e_silu, e_h, e_ht, e_htev, e_dn, e_yev = (
            sem(n) for n in ("e_t", "e_tev", "e_gu", "e_silu", "e_h", "e_ht", "e_htev", "e_dn", "e_yev"))
        ye_out = [sem(f"ye_out{k}") for k in range(4)]
        yg_in = [sem(f"yg_in{k}") for k in range(16)]
        comb1, comb = sem("comb1"), sem("comb")
        stored = sem("stored")
        passed = sem("passed")

        def apart(eng):
            eng.sem_inc(passed, 1)

        def tok(a, c):
            return a[bass.ds(c * CT, CT), :].rearrange("(p j) d -> p j d", j=TPC)

        def feat(a):
            return a.rearrange("(k p) n -> p k n", p=P)

        block = ctx.enter_context(nc.Block())

        @block.sync
        def _(sp):
            n = [0] * 4
            for c, s in ((0, ld_x[0]), (1, ld_x[1])):
                sp.dma_start(X[:, TPC * c:TPC * c + TPC, :], tok(x, c)).then_inc(s, 16)
                for dst, src in (((WK, wkT), (WV, wvT)) if c == 0 else ()):
                    sp.dma_start(dst, feat(src)).then_inc(ld_kv, 16)
            for dst, src in ((CTXT, feat(ctxT)), (XWK, feat(xwkT)), (XWV, feat(xwvT)), (XWQ, feat(xwq)), (XWO, feat(xwoT))):
                sp.dma_start(dst, src).then_inc(ld_ctx, 16)
            for c in range(2, CH):
                sp.dma_start(X[:, TPC * c:TPC * c + TPC, :], tok(x, c)).then_inc(ld_x[2], 16)
            for dst, src in ((WQ, wqT), (WO, woT)):
                sp.dma_start(dst, feat(src)).then_inc(ld_attn, 16)
            for dst, src in ((SG, feat(sgT)), (SU, feat(suT)), (GW, feat(gwT)),
                             (SD[:, 0:NF - 1, :], feat(sdT[0:(NF - 1) * P, :])), (SD[0:SF[-1], NF - 1, :], sdT[(NF - 1) * P:SFF, :])):
                sp.dma_start(dst, src).then_inc(ld_ffn, 16)
            sp.wait_ge(cleared, 7)
            flat = slots_x.rearrange("(p r) d -> p (r d)", p=P)
            per = ST * D // 10
            def zero(i):
                sp.dma_start(flat[:, bass.ds(i * per, per)], ZERO[:, 0:per]).then_inc(zeroed, 16)

            def save(c, src, rdy_a, rdy_d, n, s):
                sp.wait_ge(rdy_a, n)
                sp.wait_ge(rdy_d, n)
                sp.dma_start(XT[:, :, bass.ds(c * CT, CT)], src).then_inc(s, 16)

            zero(0)
            zero(1)
            with sp.Fori(0, B) as b:
                for i in range(2):
                    save(2 * b + i, X1T[:, i], t1_a, t1_d, 2 * b + i + 1, xt_save[i])
                    zero(2 * b + i + 2)
            with sp.Fori(0, CH) as d:
                sp.wait_ge(ln[2][4], TPC * (d + 1))
                sp.dma_start(XN3T[:, bass.ds(TPC * d, TPC), :], XN3C).then_inc(xt_save[1], 16)
                save(d, X3T, t3_a, t3_d, d + 1, xt_save[0])
            sp.wait_ge(r_ps, CH)
            for i in range(2):
                sp.wait_ge(xt_save[i], 16 * (B + CH))
            for k in range(KD):
                sp.dma_start(WEXP[:, :, 2 * FF * k:2 * FF * (k + 1)], wgu[:, k * P:k * P + P, :].rearrange("e p f -> p e f")).then_inc(ld_exp, 16)
            sp.dma_start(WEXP[:, :, 2 * FF * KD:EW], wdn.rearrange("e p d -> p e d")).then_inc(ld_exp, 16)

            sp.wait_ge(sc, 16 * 2 * T)

            def load(s, k):
                wait(sp, e_t, s - 3)
                sp.dma_start(XE[:, k % 4, :], slots_x[bass.ds(s * P, P), :]).then_inc(xe_in[k % 4], 16)

            def store(s, k):
                sp.wait_ge(e_yev, s + 1)
                sp.dma_start(slots_y[bass.ds(s * P, P), :], YE[:, k % 4, :]).then_inc(ye_out[k % 4], 16)

            for s in range(8):
                load(s, s)
            with sp.Fori(1, ST // 8) as g:
                for k in range(8):
                    load(8 * g + k, k)
                    store(8 * g + k - 8, k)
            for s in range(ST - 8, ST):
                store(s, s)
            for c in range(CH):
                sp.wait_ge(comb, TPC * (c + 1))
                sp.dma_start(tok(out, c), X[:, TPC * c:TPC * c + TPC, :]).then_inc(stored, 16)
            sp.wait_ge(stored, 16 * CH)

        @block.gpsimd
        def _(pool):
            pool.memset(R[:, :], 0.0).then_inc(cleared, 1)
            pool.memset(HALF[:, :], -0.5).then_inc(cleared, 1)
            pool.memset(EPS[:, :], KEPS).then_inc(cleared, 1)
            pool.memset(VEXT, 1.0).then_inc(cleared, 1)
            pool.memset(ONES[:, :], 1.0).then_inc(cleared, 1)
            pool.memset(KVN[:, 0, :], 0.0).then_inc(cleared, 1)
            pool.memset(ZERO, 0.0).then_inc(cleared, 1)

            def rstd(c, n):
                _, mv, ve, rs = lnbuf[n]
                _, s_mv, s_ve, s_rstd, _ = ln[n]
                pool.wait_ge(s_mv, TPC * (c + 1))
                apart(pool)
                pool.tensor_scalar(ve[:, :], mv[:, :, 1], LN_EPS, None, ALU.add).then_inc(s_ve, 1)
                pool.wait_ge(s_ve, c + 1)
                pool.tensor_tensor(rs[:, :], ve[:, :], HALF[:, :], ALU.pow).then_inc(s_rstd, 1)

            pool.wait_ge(cleared, 2)
            with pool.Fori(0, CH) as c:
                rstd(c, 0)
            pool.wait_ge(ln[0][4], TPC * CH)
            pool.wait_ge(ld_late, 16 * NLATE)
            with pool.Fori(0, CH) as c:
                xc = X[:, bass.ds(TPC * c, TPC), :]
                pool.tensor_tensor(xc, xc, BOR[:, None, :].to_broadcast((P, TPC, D)), ALU.add).then_inc(bo_in, 1)

            def attn_state(c):
                wait(pool, n_ps, TPC * c)
                apart(pool)
                pool.tensor_copy(KVXB, KVX[:, c // 2, :]).then_inc(kvx_in, 1)

            def ctx_products(d):
                wait(pool, o_ps, 2 * d)
                apart(pool)
                pool.tensor_copy(GKB[:, :, 0:SKV], GK[:, :, bass.ds((d // 2) * SKV, SKV)]).then_inc(xat_in, 1)
                pool.tensor_copy(GQB, GQ[0:1, bass.ds((d // 2) * SKV, SKV)]).then_inc(xat_in, 1)
                pool.tensor_copy(VPB[0:SKV, :], VP[0:SKV, d // 2, :]).then_inc(xat_in, 1)

            pool.wait_ge(nb_ev, B)
            attn_state(0)
            rstd(0, 1)
            with pool.Fori(1, CH) as c:
                attn_state(c)
                ctx_products(c - 1)
                rstd(c - 1, 2)
                rstd(c, 1)
            ctx_products(CH - 1)
            rstd(CH - 1, 2)

            pool.wait_ge(slots_rdy, 1)
            pool.wait_ge(zeroed, 160)
            pool.wait_ge(xt_save[1], 16 * (B + CH))
            for t in range(T):
                for j in range(2):
                    pool.indirect_dma_start(slots_x, bass.IndirectOffsetOnAxis(ap=SLOT[:, j, t:t + 1], axis=0),
                                            XN3T[:, t, :], None).then_inc(sc, 16)
            for k in range(4):
                pool.wait_ge(ye_out[k], 16 * (ST // 4))
            for t in range(T):
                if t >= 8:
                    pool.wait_ge(comb, t - 7)
                for j in range(2):
                    k = 2 * (t % 8) + j
                    pool.indirect_dma_start(YG[:, k, :], None, slots_y,
                                            bass.IndirectOffsetOnAxis(ap=SLOT[:, j, t:t + 1], axis=0)).then_inc(yg_in[k], 16)

        @block.scalar
        def _(act):
            with nc.allow_non_contiguous_dma(reason="a few hundred bias values"):
                for dst, src in ((IDENT[:, :], ident_d),
                                 (BQK[:, 0, :], bq.rearrange("(k p) -> p k", p=P)), (BQK[:, 1, :], bk.rearrange("(k p) -> p k", p=P)),
                                 (BVR[:, :], bv[None, :].to_broadcast((P, D))),
                                 (XB[:, 0, :], xbq.rearrange("(k p) -> p k", p=P)), (XB[:, 1, :], xbk.rearrange("(k p) -> p k", p=P)),
                                 (XB[:, 2, :], xbv.rearrange("(k p) -> p k", p=P)),
                                 (XBOR[:, :], xbo[None, :].to_broadcast((P, D)))):
                    act.dma_start(dst, src).then_inc(ld_const, 16)
                act.wait_ge(cleared, 1)
                act.dma_start(R[64:128, :], normblk_d).then_inc(ld_const, 16)
                for h in range(4):
                    act.dma_start(R[DK * h:DK * h + DK, M * h:M * h + M], orfT).then_inc(orf_in, 16)
                for dst, src in ((BOR[:, :], bo[None, :].to_broadcast((P, D))), (TRI[:, :], tri_d),
                                 (DESC[:, :], desc16_d.to_broadcast((P, E))), (IOTA[:, :], iota_d.to_broadcast((P, ST)))):
                    act.dma_start(dst, src).then_inc(ld_late, 16)

            def exp_k(c, j, par):
                for half in range(2):
                    n = TPC * c + j
                    act.wait_ge(kf_ps, 2 * n + half + 1)
                    if half == 0:
                        wait(act, kv_ps, n - 1)
                    act.activation(KPHI[:, j % 2, 512 * half:512 * half + 512], pF[half][:, :], ACT.Exp).then_inc(k_exp, 1)

            def square(c, dst, bias, ps, lin, sq):
                for q in range(4):
                    if q < 2:
                        act.wait_ge(lin, 2 * c + q + 1)
                        act.activation(dst[64:128, q, :], dst[0:64, q, :], ACT.Square).then_inc(sq, 1)
                    else:
                        r = 64 * (q % 2)
                        act.wait_ge(ps, 2 * c + 2)
                        act.activation(dst[0:64, q, :], pK[1][r:r + 64, :], ACT.Identity, bias=bias[r:r + 64, 1:2])
                        act.activation(dst[64:128, q, :], pK[1][r:r + 64, :], ACT.Square, bias=bias[r:r + 64, 1:2]).then_inc(sq, 1)

            def front(c, par):
                act.wait_ge(t1_ps, 2 * c + 1)
                wait(act, xt_save[par], 16 * ((c - par) // 2))
                act.copy(X1T[:, par, 0, :], pT[0][:, :]).then_inc(t1_a, 1)

            def body1(c, d, par):
                if d is not None:
                    exp_k(d, 0, 1 - par)
                if c is not None:
                    front(c, par)
                if d is not None:
                    exp_k(d, 1, 1 - par)
                if c is not None:
                    square(c, KDT[:, par], BQK[:, 1], k_ps, k_lin, k_sq)
                if d is not None:
                    exp_k(d, 2, 1 - par)
                    exp_k(d, 3, 1 - par)

            act.wait_ge(ld_const, 16 * NCONST)
            body1(0, None, 0)
            body1(1, 0, 1)
            with act.Fori(1, B) as b:
                body1(2 * b, 2 * b - 1, 0)
                body1(2 * b + 1, 2 * b, 1)
            body1(None, CH - 1, 0)

            def exp_q(c, lo, hi):
                for i in range(lo, hi):
                    act.wait_ge(qf_ps, 8 * c + i + 1)
                    act.activation(QPHI[:, i, :], pF[i % 2][:, :], ACT.Exp).then_inc(q_exp, 1)

            def body2(c, d, e):
                if c is not None:
                    square(c, KDT[:, 0], BQK[:, 0], q_ps, q_lin, q_sq)
                    exp_q(c, 0, 5)
                if d is not None:
                    act.wait_ge(t2_ps, 2 * d + 1)
                    act.copy(X2T[:, 0, :], pT[0][:, :]).then_inc(t2_a, 1)
                if c is not None:
                    exp_q(c, 5, 8)
                if d is not None:
                    act.wait_ge(s_dif, d + 1)
                    act.activation(PEXP, SDIF, ACT.Exp, scale=float(D) ** -0.5).then_inc(s_exp, 1)
                if e is not None:
                    act.wait_ge(t3_ps, 2 * e + 1)
                    act.wait_ge(xt_save[0], 16 * (B + e))
                    act.copy(X3T[:, 0, :], pF[0][:, :]).then_inc(t3_a, 1)
                if d is not None:
                    act.wait_ge(pt_ps, d + 1)
                    act.copy(PROBT[0:SKV, :], pT[0][0:SKV, :]).then_inc(pt_ev, 1)
                if c is not None:
                    act.wait_ge(at_ps, 2 * c + 1)
                    act.copy(AT[:, 0, :], pT[0][:, :]).then_inc(at_a, 1)

            act.wait_ge(zeroed, 160)
            body2(0, None, None)
            body2(1, 0, None)
            with act.Fori(1, B) as b:
                body2(2 * b, 2 * b - 1, 2 * b - 2)
                body2(2 * b + 1, 2 * b, 2 * b - 1)
            body2(None, CH - 1, CH - 2)
            body2(None, None, CH - 1)

            act.wait_ge(probe_max, 1)
            act.activation(TMP[1], TMP[0], ACT.Exp).then_inc(rt_a, 1)
            act.activation(SIG[:, :], LOG[:, :, E], ACT.Exp, scale=-1.0).then_inc(rt_a, 1)

            def shared(u):
                for f in range(NF):
                    i = NF * u + f
                    act.wait_ge(g_ps, i + 1)
                    wait(act, h_rdy, i - 1)
                    act.activation(SIL[f % 2][0:SF[f], :], pK[f % 2][0:SF[f], :], ACT.Silu).then_inc(silu, 1)

            shared(0)
            with act.Fori(1, CH // 2) as u:
                shared(u)

            def copy_xt(s, k):
                act.wait_ge(e_t, s + 1)
                wait(act, e_gu, s - 1)
                act.copy(XET[:, k % 2, :], pT[k % 2][:, 0:D]).then_inc(e_tev, 1)

            def silu_e(s, k):
                act.wait_ge(e_gu, s + 1)
                wait(act, e_h, s - 1)
                act.activation(ESIL[:, k % 2, :], pK[k % 2][:, 0:FF], ACT.Silu).then_inc(e_silu, 1)

            def copy_y(s, k, n):
                act.wait_ge(e_dn, s + 1)
                wait(act, ye_out[k % 4], 16 * n)
                act.copy(YE[:, k % 4, :], pO[k % 2][:, 0:D]).then_inc(e_yev, 1)

            for s in range(8):
                copy_xt(s, s)
                if s >= 1:
                    silu_e(s - 1, s - 1)
                if s >= 3:
                    copy_y(s - 3, s - 3, (s - 3) // 4)
            with act.Fori(1, ST // 8) as g:
                for k in range(8):
                    copy_xt(8 * g + k, k)
                    silu_e(8 * g + k - 1, k - 1)
                    copy_y(8 * g + k - 3, k - 3, 2 * g + (k - 3) // 4)
            silu_e(ST - 1, ST - 1)
            for s in range(ST - 3, ST):
                copy_y(s, s, s // 4)
            with act.Fori(CH // 2, CH) as u:
                shared(u)

        @block.tensor
        def _(pe):
            def mm(out_, lhsT, rhs, start=True, stop=True, **kw):
                return pe.matmul(out_, lhsT, rhs, start=start, stop=stop, **kw)

            def project(dst, w, src, m):
                for k in range(KD):
                    last = mm(dst, w[:, k, m * P:m * P + P], src[k], start=(k == 0), stop=(k == KD - 1))
                return last

            def t1(c):
                pe.wait_ge(ln[0][4], TPC * (c + 1))
                wait(pe, v_ev, 2 * c)
                for h in range(KD):
                    for j in range(TPC):
                        last = pe.transpose(pT[h][:, j * P:j * P + P], XN[:, j, h * P:h * P + P], IDENT[:, :])
                    last.then_inc(t1_ps, 1)

            def k_proj(c, par):
                pe.wait_ge(t1_a, c + 1)
                pe.wait_ge(t1_d, c + 1)
                for m in range(KD):
                    project(pK[m][:, :], WK, [X1T[:, par, k, :] for k in range(KD)], m).then_inc(k_ps, 1)

            def v_proj(c, par):
                for j in range(TPC):
                    for k in range(KD):
                        last = mm(pT[j // 2][:, D * (j % 2):D * (j % 2) + D], X1T[:, par, k, j * P:j * P + P], WV[:, k, :],
                                  start=(k == 0), stop=(k == KD - 1))
                    if j % 2:
                        last.then_inc(v_ps, 1)

            def k_feat(c, j, par):
                for half in range(2):
                    n = TPC * c + j
                    if j == 0:
                        pe.wait_ge(k_sq, 4 * c + 2 * half + 2)
                    wait(pe, k_exp, 2 * n - 1 + half)
                    for q in range(2):
                        last = mm(pF[half][:, 256 * q:256 * q + 256], KDT[:, par, 2 * half + q, j * P:j * P + P], R[:, :])
                    last.then_inc(kf_ps, 1)

            def kv(c, j, par):
                n = TPC * c + j
                if j == 0:
                    pe.wait_ge(v_ev, 2 * c + 2)
                first = j == 0 and par == 0
                if first:
                    wait(pe, kv_ev, c)
                pe.wait_ge(k_exp, 2 * n + 2)
                mm(pO[0][:, 0:HV], EPS[:, :], VEXT[:, par, j, :], start=first, stop=False, skip_group_check=True)
                for p in range(PAIRS):
                    last = mm(pO[0][:, HV2 * p:HV2 * p + HV2], KPHI[:, j % 2, P * p:P * p + P],
                              VEXT[:, par, j, HV2 * p:HV2 * p + HV2], start=False, stop=(j == TPC - 1 and par == 1 and p == PAIRS - 1),
                              skip_group_check=True)
                last.then_inc(kv_ps, 1)

            def body1(c, d, par):
                if d is not None:
                    k_feat(d, 0, 1 - par)
                if c is not None:
                    t1(c)
                if d is not None:
                    k_feat(d, 1, 1 - par)
                    kv(d, 0, 1 - par)
                if c is not None:
                    k_proj(c, par)
                if d is not None:
                    k_feat(d, 2, 1 - par)
                    kv(d, 1, 1 - par)
                if c is not None:
                    v_proj(c, par)
                if d is not None:
                    k_feat(d, 3, 1 - par)
                    kv(d, 2, 1 - par)
                    kv(d, 3, 1 - par)

            pe.wait_ge(ld_const, 16 * NCONST)
            pe.wait_ge(ld_kv, 16 * 2)
            body1(0, None, 0)
            pe.wait_ge(ld_ctx, 16 * 5)
            pe.wait_ge(v_ev, 2)
            pe.wait_ge(k_sq, 4)
            W2 = B * SKV
            for m in range(KD):
                project(pT[m][:, 0:W2], XWK, [CTXT[:, 0, :], CTXT[:, 1, :]], m).then_inc(prep_ps, 1)
            for m in range(KD):
                project(pK[m][:, 0:W2], XWV, [CTXT[:, 0, :], CTXT[:, 1, :]], m).then_inc(prep_ps, 1)
            pe.wait_ge(prep_ev, 2)
            for m in range(KD):
                project(pF[m][:, 0:W2], XWQ, [KT[:, 0, :], KT[:, 1, :]], m).then_inc(prep_ps, 1)
            for k in range(KD):
                last = mm(pO[0][0:1, 0:W2], XB[:, 0, k:k + 1], KT[:, k, :], start=(k == 0), stop=(k == KD - 1))
            last.then_inc(prep_ps, 1)
            pe.wait_ge(prep_ev, 4)
            for b in range(B):
                dst = (pT[b // 2])[0:SKV, D * (b % 2):D * (b % 2) + D]
                for k in range(KD):
                    last = mm(dst, VT[:, k, b * SKV:b * SKV + SKV], XWO[:, k, :], start=(k == 0), stop=(k == KD - 1))
                last.then_inc(prep_ps, 1)
            pe.wait_ge(prep_ev, 11)

            pe.wait_ge(r_ready, 1)
            body1(1, 0, 1)
            with pe.Fori(1, B) as b:
                body1(2 * b, 2 * b - 1, 0)
                body1(2 * b + 1, 2 * b, 1)
            body1(None, CH - 1, 0)
            pe.wait_ge(kv_ev, 2 * B)
            for b in range(B):
                mm((pT + pK)[b][:, 0:HV], EPS[:, :], KVX[:, b, :]).then_inc(nb_ps, 1)
            pe.wait_ge(nb_ev, B)
            for i in range(2):
                pe.wait_ge(xt_save[i], 16 * B)

            def q_proj(c):
                for m in range(KD):
                    project(pK[m][:, :], WQ, [XT[:, k, bass.ds(c * CT, CT)] for k in range(KD)], m).then_inc(q_ps, 1)

            def q_feat(c, lo, hi):
                for i in range(lo, hi):
                    pe.wait_ge(q_sq, 4 * c + i // 2 + 1)
                    if i == 0:
                        wait(pe, r_ev, c - 1)
                    if i >= 2:
                        pe.wait_ge(q_exp, 8 * c + i - 1)
                    mm(pF[i % 2][:, :], R[:, P * (i % 2):P * (i % 2) + P], KDT[:, 0, i // 2, :]).then_inc(qf_ps, 1)

            def num(c, p):
                if p == 0:
                    pe.wait_ge(kvx_in, c + 1)
                    pe.wait_ge(q_sq, 4 * c + 4)
                pe.wait_ge(q_exp, 8 * c + p + 1)
                for j in (2, 3, 0, 1):
                    last = mm(pN[j][:, HV2 * p:HV2 * p + HV2], QPHI[:, p, j * P:j * P + P], KVXB[:, HV2 * p:HV2 * p + HV2])
                    if p == PAIRS - 1:
                        last.then_inc(n_ps, 1)

            def transpose_chunk(src, ps):
                for h in range(KD):
                    for j in range(TPC):
                        last = pe.transpose(pT[h][:, j * P:j * P + P], src(j, h), IDENT[:, :])
                    last.then_inc(ps, 1)

            def att_t(c):
                pe.wait_ge(att_rdy, c + 1)
                transpose_chunk(lambda j, h: ATT[:, j, h * P:h * P + P], at_ps)

            def wo(c, d):
                pe.wait_ge(at_a, c + 1)
                pe.wait_ge(at_d, c + 1)
                if d is not None:
                    pe.wait_ge(x2, 2 * d + 2)
                for j in range(TPC):
                    for k in range(KD):
                        last = mm(pO[j // 2][:, D * (j % 2):D * (j % 2) + D], AT[:, k, j * P:j * P + P], WO[:, k, :],
                                  start=(k == 0), stop=(k == KD - 1))
                    if j % 2:
                        last.then_inc(wo_ps, 1)

            def t2(d):
                pe.wait_ge(ln[1][4], TPC * (d + 1))
                transpose_chunk(lambda j, h: XN[:, j, h * P:h * P + P], t2_ps)

            def scores(d, j):
                if j == 0:
                    pe.wait_ge(t2_a, d + 1)
                    pe.wait_ge(t2_d, d + 1)
                    pe.wait_ge(xat_in, 3 * (d + 1))
                for k in range(KD):
                    mm(pS[:, j, 0:SKV], X2T[:, k, j * P:j * P + P], GKB[:, k, 0:SKV], start=(k == 0), stop=False)
                last = mm(pS[:, j, 0:SKV], ONES[0:1, :], GQB, start=False)
                if j == TPC - 1:
                    last.then_inc(s_ps, 1)

            def prob_t(d):
                pe.wait_ge(prob, d + 1)
                for j in range(TPC):
                    last = pe.transpose(pT[0][0:SKV, j * P:j * P + P], PROB[:, j, :], IDENT[:, :])
                last.then_inc(pt_ps, 1)

            def out_x(c, d):
                pe.wait_ge(pt_ev, d + 1)
                if c is not None:
                    pe.wait_ge(n_add, 8 * c + 4)
                for j in range(TPC):
                    dst = pO[j // 2][:, D * (j % 2):D * (j % 2) + D]
                    for k in range(KD):
                        mm(dst, X2T[:, k, j * P:j * P + P], XWO[:, k, :], start=(k == 0), stop=False)
                    last = mm(dst, PROBT[0:SKV, j * P:j * P + P], VPB[0:SKV, :], start=False)
                    if j % 2:
                        last.then_inc(o_ps, 1)

            def t3(c, e, h):
                pe.wait_ge(ln[2][4], TPC * (e + 1))
                if c is not None:
                    pe.wait_ge(q_exp, 8 * c + 7 + h)
                for j in range(TPC):
                    last = pe.transpose(pF[h][:, j * P:j * P + P], XN3C[:, j, h * P:h * P + P], IDENT[:, :])
                last.then_inc(t3_ps, 1)

            def router(d):
                pe.wait_ge(t3_a, d + 1)
                pe.wait_ge(t3_d, d + 1)
                pe.wait_ge(r_ev, d + 1)
                for j in range(TPC):
                    for k in range(KD):
                        last = mm(pR[:, j, 0:E + 1], X3T[:, k, j * P:j * P + P], GW[:, k, :],
                                  start=(k == 0), stop=(k == KD - 1))
                last.then_inc(r_ps, 1)

            def body2(c, d, e):
                if c is not None:
                    q_proj(c)
                    q_feat(c, 0, 4)
                for p in range(PAIRS):
                    if c is not None:
                        num(c, p)
                        if p < 4:
                            q_feat(c, p + 4, p + 5)
                    if d is not None and p == 0:
                        t2(d)
                    if d is not None and p in (1, 2, 3, 4):
                        scores(d, p - 1)
                    if e is not None and p >= PAIRS - 2:
                        t3(c, e, p - (PAIRS - 2))
                if d is not None:
                    prob_t(d)
                    out_x(c, d)
                if c is not None:
                    att_t(c)
                if e is not None:
                    router(e)
                if c is not None:
                    wo(c, d)

            pe.wait_ge(ld_attn, 16 * 2)
            pe.wait_ge(ld_ffn, 16 * 5)
            body2(0, None, None)
            body2(1, 0, None)
            with pe.Fori(1, B) as b:
                body2(2 * b, 2 * b - 1, 2 * b - 2)
                body2(2 * b + 1, 2 * b, 2 * b - 1)
            body2(None, CH - 1, CH - 2)
            body2(None, None, CH - 1)

            pe.wait_ge(ld_late, 16 * NLATE)
            pe.wait_ge(mask_rdy, 1)
            mm(pT[0][:, :], TRI[:, :], TMP[4])
            mm(pT[1][:, :], ONES[:, :], TMP[4]).then_inc(rt_ps, 1)

            def gate_up(u, f):
                i = NF * u + f
                wait(pe, h_rdy, i - 1)
                if SF[f] < P:
                    apart(pe)
                src = [XT[:, k, bass.ds(u * CT, CT)] for k in range(KD)]
                for w, dst, s in ((SG, pK[f % 2], g_ps), (SU, pF[f % 2], u_ps)):
                    for k in range(KD):
                        last = mm(dst[0:SF[f], :], w[:, k, f * P:f * P + SF[f]], src[k], start=(k == 0), stop=(k == KD - 1))
                    last.then_inc(s, 1)

            def down(u, f):
                i = NF * u + f
                pe.wait_ge(h_rdy, i + 1)
                if f == 0:
                    wait(pe, s_res, TPC * u)
                for j in range(TPC):
                    last = mm(pO[j // 2][:, D * (j % 2):D * (j % 2) + D], HT[f % 3][0:SF[f], j * P:j * P + P], SD[0:SF[f], f, :],
                              start=(f == 0 and j % 2 == 0), stop=(f == NF - 1 and j % 2 == 1), skip_group_check=True)
                last.then_inc(d_ps, 1)

            def shared(u):
                gate_up(u, 0)
                for f in range(1, NF):
                    gate_up(u, f)
                    down(u, f - 1)
                down(u, NF - 1)

            pe.wait_ge(xt_save[0], 16 * (B + CH))
            shared(0)
            with pe.Fori(1, CH // 2) as u:
                shared(u)

            pe.wait_ge(ld_exp, 16 * 3)
            pe.wait_ge(s_res, TPC * (CH // 2))
            pe.wait_ge(eid_rdy, 1)

            def experts_of(first, n):
                return nc.values_load_multi_w_load_instructions(
                    EID[0:1, bass.ds(first, n)], engines=[mybir.EngineType.PE], min_val=0, max_val=(E - 1) * EW,
                    skip_runtime_bounds_check_because="a count of at most E experts, held to E - 1, times EW")[1]

            def tx(s, k, n):
                pe.wait_ge(xe_in[k % 4], 16 * (n + 1))
                wait(pe, e_tev, s - 1)
                for h in range(KD):
                    last = pe.transpose(pT[k % 2][:, h * P:h * P + P], XE[:, k % 4, h * P:h * P + P], IDENT[:, :])
                last.then_inc(e_t, 1)

            def gu(s, k, w):
                pe.wait_ge(e_tev, s + 1)
                wait(pe, e_h, s - 1)
                for h in range(KD):
                    last = mm(pK[k % 2][:, 0:2 * FF], XET[:, k % 2, h * P:h * P + P], ARENA[:, bass.ds(w + h * 2 * FF, 2 * FF)],
                              start=(h == 0), stop=(h == KD - 1))
                last.then_inc(e_gu, 1)

            def th(s, k):
                pe.wait_ge(e_h, s + 1)
                wait(pe, e_htev, s - 1)
                pe.transpose(pF[k % 2][:, 0:P], HE[:, k % 2, :], IDENT[:, :]).then_inc(e_ht, 1)

            def dn(s, k, w):
                pe.wait_ge(e_htev, s + 1)
                wait(pe, e_yev, s - 1)
                mm(pO[k % 2][:, 0:D], HET[:, k % 2, :], ARENA[:, bass.ds(w + KD * 2 * FF, D)]).then_inc(e_dn, 1)

            w = experts_of(0, 8)
            for s in range(8):
                tx(s, s, s // 4)
                if s >= 1:
                    gu(s - 1, s - 1, w[s - 1])
                if s >= 2:
                    th(s - 2, s - 2)
                if s >= 3:
                    dn(s - 3, s - 3, w[s - 3])
            with pe.Fori(1, ST // 8) as g:
                w = experts_of(8 * g - 4, 12)
                for k in range(8):
                    tx(8 * g + k, k, 2 * g + k // 4)
                    gu(8 * g + k - 1, k - 1, w[k + 3])
                    th(8 * g + k - 2, k - 2)
                    dn(8 * g + k - 3, k - 3, w[k + 1])
            w = experts_of(ST - 4, 4)
            gu(ST - 1, ST - 1, w[3])
            th(ST - 2, ST - 2)
            dn(ST - 3, ST - 3, w[1])
            th(ST - 1, ST - 1)
            dn(ST - 2, ST - 2, w[2])
            dn(ST - 1, ST - 1, w[3])
            pe.wait_ge(e_yev, ST)
            with pe.Fori(CH // 2, CH) as u:
                shared(u)

        @block.vector
        def _(dve):
            def stats(c, n):
                st, mv = lnbuf[n][0], lnbuf[n][1]
                for j in range(TPC):
                    dve.bn_stats(st[:, j, :], X[:, TPC * c + j, :]).then_inc(ln[n][0], 1)
                dve.wait_ge(ln[n][0], TPC * (c + 1))
                apart(dve)
                for j in range(TPC):
                    dve.bn_aggr(mv[:, j, :], st[:, j, :]).then_inc(ln[n][1], 1)

            def normalize(c, n, dst):
                mv, rs = lnbuf[n][1], lnbuf[n][3]
                dve.wait_ge(ln[n][3], c + 1)
                for j in range(TPC):
                    dve.tensor_scalar(dst(j), X[:, TPC * c + j, :], mv[:, j, 0:1], rs[:, j:j + 1],
                                      ALU.subtract, ALU.mult).then_inc(ln[n][4], 1)

            def linear(c, dst, bias, ps, lin):
                for q in range(2):
                    r = 64 * q
                    dve.wait_ge(ps, 2 * c + 1)
                    dve.tensor_scalar(dst[0:64, q, :], pK[0][r:r + 64, :], bias[r:r + 64, 0:1], None, ALU.add).then_inc(lin, 1)

            def norm1(c):
                stats(c, 0)
                wait(dve, t1_ps, 2 * c)
                normalize(c, 0, lambda j: XN[:, j, :])

            def body1(c, d, par):
                if c is not None:
                    dve.wait_ge(t1_ps, 2 * c + 2)
                    wait(dve, xt_save[par], 16 * ((c - par) // 2))
                    dve.tensor_copy(X1T[:, par, 1, :], pT[1][:, :]).then_inc(t1_d, 1)
                    if d is not None:
                        wait(dve, kf_ps, 8 * d)
                    linear(c, KDT[:, par], BQK[:, 1], k_ps, k_lin)
                    if d is not None:
                        wait(dve, kv_ps, TPC * d)
                    for i in range(2):
                        dve.wait_ge(v_ps, 2 * c + i + 1)
                        dve.tensor_tensor(
                            VEXT[:, par, 2 * i:2 * i + 2, :].rearrange("p j (h e) -> p j h e", h=H)[:, :, :, 0:DK],
                            pT[i][:, :].rearrange("p (j h e) -> p j h e", j=2, h=H),
                            BVR[:, None, :].to_broadcast((P, 2, D)).rearrange("p j (h e) -> p j h e", h=H),
                            ALU.add).then_inc(v_ev, 1)
                    if not (isinstance(c, int) and c == CH - 1):
                        norm1(c + 1)
                if d is not None and par == 0:
                    dve.wait_ge(kv_ps, TPC * (d + 1))
                    b = (d - 1) // 2
                    state = pO[0][:, 0:HV].rearrange("p (q e) -> p q e", q=PAIRS)
                    kvx = KVX[:, b, :].rearrange("p (q e) -> p q e", q=PAIRS)
                    dve.tensor_copy(kvx[0:64, :, 0:DK + 1], state[0:64, :, 0:DK + 1]).then_inc(kv_ev, 1)
                    dve.tensor_copy(kvx[64:128, :, DK + 1:HV2], state[64:128, :, DK + 1:HV2]).then_inc(kv_ev, 1)

            dve.wait_ge(ld_x[0], 16)
            norm1(0)
            dve.wait_ge(cleared, 7)
            dve.wait_ge(ld_const, 16 * NCONST)
            dve.wait_ge(ld_x[1], 16)
            body1(0, None, 0)
            W2 = B * SKV
            dve.wait_ge(orf_in, 64)
            dve.tensor_scalar(R[0:64, :], R[0:64, :], float(DK) ** -0.25, None, ALU.mult).then_inc(r_ready, 1)
            for m in range(KD):
                dve.wait_ge(prep_ps, m + 1)
                dve.tensor_scalar(KT[:, m, :], pT[m][:, 0:W2], XB[:, 1, m:m + 1], None, ALU.add).then_inc(prep_ev, 1)
            for m in range(KD):
                dve.wait_ge(prep_ps, m + 3)
                dve.tensor_scalar(VT[:, m, :], pK[m][:, 0:W2], XB[:, 2, m:m + 1], None, ALU.add).then_inc(prep_ev, 1)
            for m in range(KD):
                dve.wait_ge(prep_ps, m + 5)
                dve.tensor_copy(GK[:, m, :], pF[m][:, 0:W2]).then_inc(prep_ev, 1)
            dve.wait_ge(prep_ps, 7)
            dve.tensor_copy(GQ[0:1, :], pO[0][0:1, 0:W2]).then_inc(prep_ev, 1)
            for b in range(B):
                dve.wait_ge(prep_ps, 8 + (b | 1))
                dve.tensor_tensor(VP[0:SKV, b, :], pT[b // 2][0:SKV, D * (b % 2):D * (b % 2) + D], XBOR[0:SKV, :],
                                  ALU.add).then_inc(prep_ev, 1)

            dve.wait_ge(ld_x[2], 16 * (CH - 2))
            body1(1, 0, 1)
            with dve.Fori(1, B - 1) as b:
                body1(2 * b, 2 * b - 1, 0)
                body1(2 * b + 1, 2 * b, 1)
            body1(CH - 2, CH - 3, 0)
            body1(CH - 1, CH - 2, 1)
            body1(None, CH - 1, 0)
            for b in range(B):
                dve.wait_ge(nb_ps, b + 1)
                dve.tensor_copy(NB[:, b, :], (pT + pK)[b][:, 0:HV]).then_inc(nb_ev, 1)
            dve.memset(LOG[:, :, :], 0.0).then_inc(r_ev, 1)

            def sums(c):
                nb = NB[:, c // 2, :].rearrange("p (h e) -> p h e", h=H)
                for j in (2, 3, 0, 1):
                    dve.wait_ge(n_ps, TPC * c + (j + 2) % 4 + 1)
                    ns = pN[j][:, 0:HV].rearrange("p (h e) -> p h e", h=H)
                    dve.tensor_tensor(DEN[:, j, :], ns[:, :, DK], nb[:, :, DK], ALU.add).then_inc(n_add, 1)
                    dve.tensor_tensor(ATT[:, j, :].rearrange("p (h e) -> p h e", h=H), ns[:, :, 0:DK], nb[:, :, 0:DK],
                                      ALU.add).then_inc(n_add, 1)

            def divide(c):
                dve.wait_ge(n_add, 8 * c + 8)
                dve.reciprocal(REC[:, :, :], DEN[:, :, :]).then_inc(n_rec, 1)
                dve.wait_ge(n_rec, c + 1)
                att = ATT.rearrange("p j (h e) -> p j h e", h=H)
                dve.tensor_tensor(att, att, REC[:, :, :, None].to_broadcast((P, TPC, H, DK)), ALU.mult).then_inc(att_rdy, 1)

            def residual(c, ps, done):
                for i in range(2):
                    dve.wait_ge(ps, 2 * c + i + 1)
                    xc = X[:, bass.ds(TPC * c + 2 * i, 2), :]
                    dve.tensor_tensor(xc, pO[i][:, :].rearrange("p (j d) -> p j d", j=2), xc, ALU.add).then_inc(done, 1)

            def softmax(d):
                dve.wait_ge(s_ps, d + 1)
                dve.tensor_reduce(SMX[:, 0, :], pS[:, :, 0:SKV], AX_X, ALU.max).then_inc(s_max, 1)
                dve.wait_ge(s_max, d + 1)
                dve.tensor_tensor(SDIF, pS[:, :, 0:SKV], SMX[:, 0, :, None].to_broadcast((P, TPC, SKV)),
                                  ALU.subtract).then_inc(s_dif, 1)
                dve.wait_ge(s_exp, d + 1)
                dve.tensor_reduce(SMX[:, 1, :], PEXP, AX_X, ALU.add).then_inc(s_step, 1)
                dve.wait_ge(s_step, 2 * d + 1)
                dve.reciprocal(SMX[:, 2, :], SMX[:, 1, :]).then_inc(s_step, 1)
                dve.wait_ge(s_step, 2 * d + 2)
                dve.tensor_tensor(PROB, PEXP, SMX[:, 2, :, None].to_broadcast((P, TPC, SKV)),
                                  ALU.mult).then_inc(prob, 1)

            def body2(c, d, e):
                if d is not None:
                    normalize(d, 1, lambda j: XN[:, j, :])
                    dve.wait_ge(t2_ps, 2 * d + 2)
                    dve.tensor_copy(X2T[:, 1, :], pT[1][:, :]).then_inc(t2_d, 1)
                    softmax(d)
                if c is not None:
                    sums(c)
                if e is not None:
                    dve.wait_ge(t3_ps, 2 * e + 2)
                    dve.wait_ge(xt_save[0], 16 * (B + e))
                    dve.tensor_copy(X3T[:, 1, :], pF[1][:, :]).then_inc(t3_d, 1)
                if c is not None:
                    divide(c)
                if d is not None:
                    residual(d, o_ps, x2)
                if c is not None:
                    dve.wait_ge(at_ps, 2 * c + 2)
                    dve.tensor_copy(AT[:, 1, :], pT[1][:, :]).then_inc(at_d, 1)
                if d is not None:
                    dve.wait_ge(x2, 2 * d + 2)
                    apart(dve)
                    stats(d, 2)
                if e is not None:
                    dve.wait_ge(r_ps, e + 1)
                    dve.tensor_copy(LOG[:, bass.ds(TPC * e, TPC), :], pR[:, :, 0:E + 1]).then_inc(r_ev, 1)
                if c is not None:
                    dve.wait_ge(bo_in, c + 1)
                    residual(c, wo_ps, x1)
                if d is not None:
                    dve.wait_ge(xt_save[1], 16 * (B + d))
                    normalize(d, 2, lambda j: XN3C[:, j, :])
                if c is not None and not (isinstance(c, int) and c == CH - 1):
                    linear(c + 1, KDT[:, 0], BQK[:, 0], q_ps, q_lin)
                if c is not None:
                    dve.wait_ge(x1, 2 * c + 2)
                    apart(dve)
                    stats(c, 1)

            dve.wait_ge(r_ev, 1)
            linear(0, KDT[:, 0], BQK[:, 0], q_ps, q_lin)
            body2(0, None, None)
            body2(1, 0, None)
            with dve.Fori(1, B - 1) as b:
                body2(2 * b, 2 * b - 1, 2 * b - 2)
                body2(2 * b + 1, 2 * b, 2 * b - 1)
            for c in range(CH - 2, CH):
                body2(c, c - 1, c - 2)
            body2(None, CH - 1, CH - 2)
            body2(None, None, CH - 1)

            steps = [0]

            def step(ins):
                steps[0] += 1
                ins.then_inc(rt, 1)
                dve.wait_ge(rt, steps[0])

            def te(i):
                return TMP[i].rearrange("p (t e) -> p t e", e=E)

            def over_e(a):
                return a[:, :, None].to_broadcast((P, T, E))

            dve.wait_ge(ld_late, 16 * NLATE)
            MX, SUM, RSUM, M1, M2, PK1, PK2 = (SMALL[:, i, :] for i in range(7))
            desc = DESC[:, None, :].to_broadcast((P, T, E))
            dve.wait_ge(r_ev, CH + 1)
            step(dve.tensor_reduce(MX, LOG[:, :, 0:E], AX_X, ALU.max))
            dve.tensor_tensor(te(0), LOG[:, :, 0:E], over_e(MX), ALU.subtract).then_inc(probe_max, 1)
            dve.wait_ge(rt_a, 2)
            step(dve.tensor_reduce(SUM, te(1), AX_X, ALU.add))
            step(dve.reciprocal(RSUM, SUM))
            step(dve.tensor_tensor(te(2), te(1), over_e(RSUM), ALU.mult))
            step(dve.tensor_reduce(M1, te(2), AX_X, ALU.max))
            step(dve.tensor_tensor(te(0), te(2), over_e(M1), ALU.is_equal))
            step(dve.tensor_tensor(te(0), te(0), desc, ALU.mult))
            step(dve.tensor_reduce(PK1, te(0), AX_X, ALU.max))
            step(dve.tensor_tensor(te(1), desc, over_e(PK1), ALU.is_equal))
            step(dve.scalar_tensor_tensor(te(3), te(1), -4.0, te(2), ALU.mult, ALU.add))
            step(dve.tensor_reduce(M2, te(3), AX_X, ALU.max))
            step(dve.tensor_tensor(te(0), te(3), over_e(M2), ALU.is_equal))
            step(dve.tensor_tensor(te(0), te(0), desc, ALU.mult))
            step(dve.tensor_reduce(PK2, te(0), AX_X, ALU.max))
            step(dve.tensor_tensor(te(2), desc, over_e(PK2), ALU.is_equal))
            dve.tensor_tensor(te(4), te(1), te(2), ALU.add).then_inc(mask_rdy, 1)
            step(dve.tensor_tensor(SUM, M1, M2, ALU.add))
            step(dve.reciprocal(RSUM, SUM))
            step(dve.tensor_tensor(RW[:, 0, :], M1, RSUM, ALU.mult))
            step(dve.tensor_tensor(RW[:, 1, :], M2, RSUM, ALU.mult))
            step(dve.tensor_scalar(SIG[:, :], SIG[:, :], 1.0, None, ALU.add))
            step(dve.reciprocal(SIG[:, :], SIG[:, :]))
            cum = [VP[:, :, :].rearrange("p b d -> p (b d)")[:, 0:48 * E].rearrange("p (t e) -> p t e", e=E),
                   KVN[:, 1, 0:48 * E].rearrange("p (t e) -> p t e", e=E)]
            step(dve.memset(cum[0][:, 0:16, :], 0.0))
            step(dve.memset(cum[1][:, 0:16, :], 0.0))
            dve.wait_ge(rt_ps, 1)
            step(dve.tensor_copy(cum[0][:, 16:48, :], pT[1][:, :].rearrange("p (t e) -> p t e", e=E)))
            for i in range(5):
                a, b = cum[i % 2], cum[(i + 1) % 2]
                step(dve.tensor_tensor(b[:, 16:48, :], a[:, 16:48, :], a[:, 16 - (1 << i):48 - (1 << i), :], ALU.add))
            tot = cum[1]
            cnt = TMP[3].bitcast(I32)
            step(dve.tensor_scalar(cnt[:, 0:E], tot[:, 47, :], float(P - 1), None, ALU.add))
            step(dve.tensor_scalar(cnt[:, E:2 * E], cnt[:, 0:E], 7, None, ALU.logical_shift_right))
            end = [TMP[3][:, 64:88], TMP[3][:, 96:120]]
            step(dve.memset(TMP[3][:, 64:128], 0.0))
            step(dve.tensor_copy(end[0][:, 8:24], cnt[:, E:2 * E]))
            step(dve.tensor_copy(TMP[3][:, 32:48], cnt[:, E:2 * E]))
            for i in range(4):
                a, b = end[i % 2], end[(i + 1) % 2]
                step(dve.tensor_tensor(b[:, 8:24], a[:, 8:24], a[:, 8 - (1 << i):24 - (1 << i)], ALU.add))
            step(dve.tensor_tensor(TMP[3][:, 128:144], end[0][:, 8:24], TMP[3][:, 32:48], ALU.subtract))
            step(dve.tensor_scalar(TMP[3][:, 144:160], TMP[3][:, 128:144], float(P), None, ALU.mult))
            step(dve.tensor_tensor(te(4), tot[:, 15:47, :], pT[0][:, :].rearrange("p (t e) -> p t e", e=E), ALU.add))
            step(dve.tensor_tensor(te(4), te(4), TMP[3][:, None, 144:160].to_broadcast((P, T, E)), ALU.add))
            for j in range(2):
                step(dve.tensor_tensor(te(0), te(1 + j), te(4), ALU.mult))
                step(dve.tensor_reduce(SMALL[:, 7 + j, :], te(0), AX_X, ALU.add))
            step(dve.tensor_copy(SLOT[:, 0, :], SMALL[:, 7, :]))
            dve.tensor_copy(SLOT[:, 1, :], SMALL[:, 8, :]).then_inc(slots_rdy, 1)
            ge = KVN[:, :, :].rearrange("p a n -> p (a n)")[:, 0:ST * E].rearrange("p (s e) -> p s e", e=E)
            ends = end[0][:, None, 8:24].to_broadcast((P, ST, E))
            step(dve.tensor_tensor(ge, IOTA[:, :, None].to_broadcast((P, ST, E)), ends, ALU.is_ge))
            step(dve.tensor_reduce(TMP[0][:, 0:ST], ge, AX_X, ALU.add))
            dve.tensor_scalar(EID[:, :], TMP[0][:, 0:ST], float(E - 1), float(EW), ALU.min, ALU.mult).then_inc(eid_rdy, 1)

            def shared(u):
                for f in range(NF):
                    i = NF * u + f
                    dve.wait_ge(u_ps, i + 1)
                    dve.wait_ge(silu, i + 1)
                    wait(dve, d_ps, i - 2)
                    dve.tensor_tensor(HT[f % 3][0:SF[f], :], SIL[f % 2][0:SF[f], :], pF[f % 2][0:SF[f], :], ALU.mult).then_inc(h_rdy, 1)
                dve.wait_ge(d_ps, NF * u + NF)
                for j in range(TPC):
                    t = TPC * u + j
                    dve.scalar_tensor_tensor(X[:, t, :], pO[j // 2][:, D * (j % 2):D * (j % 2) + D], SIG[:, bass.ds(t, 1)],
                                             X[:, t, :], ALU.mult, ALU.add).then_inc(s_res, 1)

            shared(0)
            with dve.Fori(1, CH // 2) as u:
                shared(u)

            def hidden(s, k):
                dve.wait_ge(e_silu, s + 1)
                wait(dve, e_ht, s - 1)
                dve.tensor_tensor(HE[:, k % 2, :], ESIL[:, k % 2, :], pK[k % 2][:, FF:2 * FF], ALU.mult).then_inc(e_h, 1)

            def copy_ht(s, k):
                dve.wait_ge(e_ht, s + 1)
                wait(dve, e_dn, s - 1)
                dve.tensor_copy(HET[:, k % 2, :], pF[k % 2][:, 0:P]).then_inc(e_htev, 1)

            hidden(0, 0)
            for s in range(1, 8):
                hidden(s, s)
                copy_ht(s - 1, s - 1)
            with dve.Fori(1, ST // 8) as g:
                for k in range(8):
                    hidden(8 * g + k, k)
                    copy_ht(8 * g + k - 1, k - 1)
            copy_ht(ST - 1, ST - 1)

            def combine(t):
                for j in range(2):
                    k = 2 * (t % 8) + j
                    dve.wait_ge(yg_in[k], 16 * (t // 8 + 1))
                    if j:
                        dve.wait_ge(comb1, t + 1)
                    dve.scalar_tensor_tensor(X[:, t, :], YG[:, k, :], RW[:, j, t:t + 1], X[:, t, :],
                                             ALU.mult, ALU.add).then_inc(comb if j else comb1, 1)

            tiles = 0
            for u in range(CH // 2, CH):
                shared(u)
                upto = TPC * (CH if u == CH - 1 else 2 * (u - CH // 2) + 1)
                if tiles == 0:
                    dve.wait_ge(s_res, TPC * (CH // 2))
                dve.wait_ge(s_res, TPC * (u + 1))
                while tiles < upto:
                    combine(tiles)
                    tiles += 1


_OUTS = [((B, L, D), "float32")]


def kernel(**inputs):
    import numpy as np
    import concourse.bacc as bacc
    from concourse import mybir as mb
    from concourse.bass_utils import run_bass_kernel_spmd

    g = {k: np.asarray(v) for k, v in inputs.items()}
    t = lambda a: np.ascontiguousarray(a.T)
    arrays = {
        "x": g["x"].reshape(B * L, D), "ctxT": t(g["ctx_1024"].reshape(B * SKV, D)),
        "wqT": t(g["L0_attn_Wq"]), "bq": g["L0_attn_bq"], "wkT": t(g["L0_attn_Wk"]), "bk": g["L0_attn_bk"],
        "wvT": t(g["L0_attn_Wv"]), "bv": g["L0_attn_bv"], "woT": t(g["L0_attn_Wo"]), "bo": g["L0_attn_bo"],
        "orfT": t(g["L0_attn_orf"]),
        "xwq": g["L0_xattn_Wq"], "xbq": g["L0_xattn_bq"], "xwkT": t(g["L0_xattn_Wk"]), "xbk": g["L0_xattn_bk"],
        "xwvT": t(g["L0_xattn_Wv"]), "xbv": g["L0_xattn_bv"], "xwoT": t(g["L0_xattn_Wo"]), "xbo": g["L0_xattn_bo"],
        "gwT": t(np.concatenate([g["L0_ffn_gate_w"], g["L0_ffn_shared_gate_w"]], 0)),
        "wgu": g["L0_ffn_w_gate_up"], "wdn": g["L0_ffn_w_down"],
        "sgT": t(g["L0_ffn_shared_w_gate"]), "suT": t(g["L0_ffn_shared_w_up"]), "sdT": t(g["L0_ffn_shared_w_down"]),
        "ident": np.eye(P, dtype=np.float32), "tri": np.triu(np.ones((P, P), np.float32), 1),
        "normblk": np.kron(np.eye(4, dtype=np.float32), np.full((DK, M), -0.5 * float(DK) ** -0.5, np.float32)),
        "desc16": np.arange(E, 0, -1, dtype=np.float32)[None], "iota": np.arange(ST, dtype=np.float32)[None],
    }
    nc = bacc.Bacc("TRN2", target_bir_lowering=False, num_devices=1)
    arrays = {f"in_{k}": np.ascontiguousarray(v) for k, v in arrays.items()}
    args = [nc.dram_tensor(k, v.shape, mb.dt.from_np(v.dtype), kind="ExternalInput").ap() for k, v in arrays.items()]
    shape, dtype = _OUTS[0]
    o = nc.dram_tensor("out_0", (B * L, D), mb.dt.from_np(np.dtype(dtype)), kind="ExternalOutput").ap()
    decoder_layer(nc, *args, o)
    r = run_bass_kernel_spmd(nc, [arrays], core_ids=[0])
    return r.results[0]["out_0"].reshape(shape)
```

```python
from contextlib import ExitStack

import concourse.bass as bass
from concourse import mybir

F32 = mybir.dt.float32
F32R = mybir.dt.float32r
I32 = mybir.dt.int32
ALU = mybir.AluOpType
ACT = mybir.ActivationFunctionType
AX_X = mybir.AxisListType.X

P = 128
B, L, D = 4, 1024, 256
H, DK, M = 16, 16, 64
SKV = 77
E, FF, SFF = 16, 128, 704
T = B * L // P
TPC = 4
CH = T // TPC
CT = TPC * P
KD = D // P
HV = H * (DK + 1)
HV2 = 2 * (DK + 1)
PAIRS = H // 2
SF = [P] * (SFF // P) + ([SFF % P] if SFF % P else [])
NF = len(SF)
SW = (NF - 1) * P
assert 2 * SF[-1] == P
CB = 5
CS = 3
ST = (2 * T * P + E * (P - 1)) // P
ST = -(-ST // 8) * 8
EW = KD * 2 * FF + D
KEPS = 1e-6
LN_EPS = 1e-5
NFIRST = 4
NPREP = 2
NLATE = 4


def r32(a):
    return a.bitcast(F32R)


def wait(eng, sem, value):
    if not (isinstance(value, int) and value <= 0):
        eng.wait_ge(sem, value)


def decoder_layer(nc, x, ctxT, wqT, bq, wkT, bk, wvT, bv, woT, bo, orfT,
                  xwq, xbq, xwkT, xbk, xwvT, xbv, xwoT, xbo,
                  gwT, wgu, wdn, sgT, suT, sdT, ident_d, tri_d, normblk_d, desc16_d, iota_d, out):
    slots_x = nc.dram_tensor("slots_x", (ST * P, D), F32, kind="Internal").ap()
    slots_y = nc.dram_tensor("slots_y", (ST * P, D), F32, kind="Internal").ap()

    with ExitStack() as ctx:
        def sb(name, shape, dt=F32):
            return ctx.enter_context(nc.sbuf_tensor(name, shape, dt))[tuple(slice(None) for _ in shape)]

        def sem(name):
            return ctx.enter_context(nc.semaphore(name))

        def bank(name):
            return ctx.enter_context(nc.psum_tensor(name, [P, 512], F32))

        X = sb("X", [P, T, D])
        XN3 = sb("XN3", [P, T * D])
        GW = sb("GW", [P, KD, E + 1])
        R = sb("R", [P, 4 * M])
        IDENT = sb("IDENT", [P, P])
        TRI = sb("TRI", [P, P])
        ONES = sb("ONES", [P, P])
        EPS = sb("EPS", [P, P])
        BQK = sb("BQK", [P, 2, KD])
        XB = sb("XB", [P, 3, KD])
        HALF = sb("HALF", [P, 4])
        DEN = sb("DEN", [P, TPC, H])
        REC = sb("REC", [P, TPC, H])
        SMX = sb("SMX", [P, 3, TPC])
        LOG = sb("LOG", [P, T, E + 1])
        RW = sb("RW", [P, 2, T])
        SIG = sb("SIG", [P, T])
        SLOT = sb("SLOT", [P, 2, T], I32)
        EID = sb("EID", [P, ST], I32)
        SMALL = sb("SMALL", [P, 12, T])
        DESC = sb("DESC", [P, E])
        IOTA = sb("IOTA", [P, ST])
        lnbuf = [[sb(f"ln{n}_{w}", [P, TPC] + s) for w, s in (("st", [6]), ("mv", [2]), ("ve", []), ("rstd", []))]
                 for n in range(3)]

        with ExitStack() as early:
            def eb(name, shape):
                return early.enter_context(nc.sbuf_tensor(name, shape, F32))[tuple(slice(None) for _ in shape)]

            ARENA = eb("ARENA", [P, E * EW])
            XT = eb("XT", [P, KD, T * P])
            SG = eb("SG", [P, KD, SW])
            SU = eb("SU", [P, KD, SW])
            SGU = eb("SGU", [P, KD, P])
            SD = eb("SD", [P, NF, D])
            WQO = eb("WQO", [P, 2, KD, D])
            BVR = eb("BVR", [P, D])
            BOR = eb("BOR", [P, D])
            XBOR = eb("XBOR", [P, D])
            XWO = eb("XWO", [P, KD, D])
            VP = eb("VP", [P, B, D])
            PROBT = eb("PROBT", [P, CT])
            WKV = eb("WKV", [P, 2, KD, D])
            KVN = eb("KVN", [P, 2, B * HV])
            GK = eb("GK", [P, KD, B * SKV])
            GQ = eb("GQ", [P, B * SKV])
            SOFT = eb("SOFT", [P, 3, TPC * SKV])
        x0 = E * EW
        g0 = x0 + KD * T * P
        u0, gu0, d0 = g0 + KD * SW, g0 + 2 * KD * SW, g0 + 2 * KD * SW + KD * P
        q0 = d0 + NF * D
        free0 = q0 + 2 * KD * D + 3 * D
        wkv0 = free0 + KD * D + B * D + CT
        kvn0 = wkv0 + 2 * KD * D
        SPLIT = sb("SPLIT", [P, kvn0 + 2 * B * HV + (KD + 1) * B * SKV + 3 * TPC * SKV])
        XS = SPLIT[:, x0:g0].rearrange("p (k n) -> p k n", k=KD)
        GLO = SPLIT[:, g0:u0].rearrange("p (k n) -> p k n", k=KD)
        ULO = SPLIT[:, u0:gu0].rearrange("p (k n) -> p k n", k=KD)
        GULO = SPLIT[:, gu0:d0].rearrange("p (k n) -> p k n", k=KD)
        DLO = SPLIT[:, d0:q0].rearrange("p (f n) -> p f n", f=NF)

        KDT = ARENA[:, 0:4096].rearrange("p (b q n) -> p b q n", b=2, q=4)
        QPHI = ARENA[:, 4096:8192].rearrange("p (i n) -> p i n", i=8)
        XBQ = ARENA[:, 2048:2048 + KD * P].rearrange("p (k n) -> p k n", k=KD)
        X1H, X1L = (SPLIT[:, 9216 + 1024 * i:10240 + 1024 * i].rearrange("p (h n) -> p h n", h=KD) for i in range(2))
        WKVH = SPLIT[:, 11264:12288].rearrange("p (w k n) -> p w k n", w=2, k=KD)
        WKVL = SPLIT[:, wkv0:kvn0].rearrange("p (w k n) -> p w k n", w=2, k=KD)
        XN3C = ARENA[:, 2048:3072].rearrange("p (j d) -> p j d", j=TPC)
        X3T = ARENA[:, 3072:4096].rearrange("p (h n) -> p h n", h=KD)
        X1T = ARENA[:, 6144:8192].rearrange("p (b h n) -> p b h n", b=2, h=KD)
        XN = ARENA[:, 8192:9216].rearrange("p (j d) -> p j d", j=TPC)
        X2T = ARENA[:, 9216:10240].rearrange("p (h n) -> p h n", h=KD)
        ATH, ATL = (SPLIT[:, 10240 + 1024 * i:11264 + 1024 * i].rearrange("p (h n) -> p h n", h=KD) for i in range(2))
        WOL, WOH = (SPLIT[:, q0 + KD * D * i:q0 + KD * D * (i + 1)].rearrange("p (k n) -> p k n", k=KD) for i in (1, 2))
        ATT = ARENA[:, 11264:12288].rearrange("p (j d) -> p j d", j=TPC)
        WEXP = ARENA.rearrange("p (e n) -> p e n", e=E)
        VEXT = XN3[:, 0:8 * HV].rearrange("p (b j n) -> p b j n", b=2, j=TPC)
        KPHI = XN3[:, 2176:4224].rearrange("p (b n) -> p b n", b=2)
        n0 = 4224
        CTXT = XN3[:, n0:n0 + 616].rearrange("p (h n) -> p h n", h=KD)
        KT = XN3[:, n0 + 616:n0 + 1232].rearrange("p (h n) -> p h n", h=KD)
        VT = XN3[:, n0 + 1232:n0 + 1848].rearrange("p (h n) -> p h n", h=KD)
        XWQ, XWK, XWV = (XN3[:, n0 + 1848 + 512 * i:n0 + 2360 + 512 * i].rearrange("p (h n) -> p h n", h=KD)
                         for i in range(3))
        VSUM = XN3[:, 7608:7608 + HV]
        XN3T = XN3[:, :].rearrange("p (t d) -> p t d", t=T)
        ZERO = ARENA[:, 4096:6144]
        KVX = KVN[:, 0, :].rearrange("p (b n) -> p b n", b=B)
        NB = KVN[:, 1, :].rearrange("p (b n) -> p b n", b=B)
        HT = [KVN[:, i // 2, 512 * (i % 2):512 * (i % 2) + 512] for i in range(3)]
        SDIF, PEXP, PROB = (SOFT[:, i, :].rearrange("p (j n) -> p j n", j=TPC) for i in range(3))
        WQ, WO, WK, WV = WQO[:, 0], WQO[:, 1], WKV[:, 0], WKV[:, 1]
        spare = WKV[:, :, :, :].rearrange("p w k n -> p (w k n)")
        KVXB = spare[:, 0:HV]
        GKB = spare[:, 272:272 + KD * 80].rearrange("p (k n) -> p k n", k=KD)
        GQB = spare[:, 432:432 + SKV]
        VPB = spare[:, 512:512 + D]
        SIL = [WQO[:, i].rearrange("p k n -> p (k n)") for i in range(2)]
        h1 = kvn0 + B * HV + CT
        nhi, before = 3 * NF - 1, (kvn0 - free0) // D
        hi = [SPLIT[:, a:a + D] for a in [free0 + D * i for i in range(before)] + [h1 + D * i for i in range(nhi - before)]]
        gate_hi, up_hi = ([hi[2 * f + i].rearrange("p (k n) -> p k n", k=KD) for f in range(NF - 1)] for i in range(2))
        gu_hi, down_hi = hi[2 * NF - 2].rearrange("p (k n) -> p k n", k=KD), hi[2 * NF - 1:3 * NF - 1]
        h2 = h1 + D * (nhi - before)
        HTH = [SPLIT[:, a:a + CT] for a in (h2, kvn0, kvn0 + CT)]
        HTL = [SPLIT[:, h2 + CT:h2 + 2 * CT], XS[:, 0, 0:CT], XS[:, 1, 0:CT]]
        WSPLIT = [p for f in range(NF - 1) for p in ((SG[:, :, f * P:f * P + P], gate_hi[f], GLO[:, :, f * P:f * P + P]),
                                                     (SU[:, :, f * P:f * P + P], up_hi[f], ULO[:, :, f * P:f * P + P]))] \
            + [(SGU[:, :, :], gu_hi, GULO)] \
            + [(SD[0:SF[f], f, :], down_hi[f][0:SF[f], :], DLO[0:SF[f], f, :]) for f in range(NF)]
        NW = 2 * NF - 1

        def x_whole(u):
            return XT[:, :, bass.ds(u * CT, CT)]

        def x_lo(u):
            return XS[:, :, bass.ds(u * CT, CT)]

        def x_hi(u):
            return XS[:, :, bass.ds((u - 2) * CT, CT)]

        TMP = [ARENA[:, 4096 + 512 * i:4608 + 512 * i] for i in range(5)]
        CUM = [ARENA[:, 6656 + 768 * i:7424 + 768 * i].rearrange("p (t e) -> p t e", e=E) for i in range(2)]
        GE = ARENA[:, 0:ST * E].rearrange("p (s e) -> p s e", e=E)
        XE = XN3[:, 0:1024].rearrange("p (b d) -> p b d", b=4)
        XET = XN3[:, 1024:1536].rearrange("p (b d) -> p b d", b=2)
        ESIL = XN3[:, 1536:1792].rearrange("p (b d) -> p b d", b=2)
        HE = XN3[:, 1792:2048].rearrange("p (b d) -> p b d", b=2)
        YE = XN3[:, 2048:3072].rearrange("p (b d) -> p b d", b=4)
        WE = XN3[:, 3072:4096].rearrange("p (b n) -> p b n", b=2)
        YG = XN3[:, 4096:8192].rearrange("p (b d) -> p b d", b=16)

        pT = [bank("pT0"), bank("pT1")]
        pK = [bank("pK0"), bank("pK1")]
        pF = [bank("pF0"), bank("pF1")]
        pO = [bank("pO0"), bank("pO1")]
        pN = [pK[0], pK[1], pO[0], pO[1]]
        pS = pT[1][:, 0:TPC * 80].rearrange("p (j n) -> p j n", j=TPC)
        pR = pT[0][:, 0:TPC * 32].rearrange("p (j n) -> p j n", j=TPC)

        ld_first = sem("ld_first")
        ld_xb = sem("ld_xb")
        ld_prep = sem("ld_prep")
        ld_ctx = sem("ld_ctx")
        ld_xqo = sem("ld_xqo")
        ld_late = sem("ld_late")
        ld_kv = sem("ld_kv")
        ld_attn = sem("ld_attn")
        ld_x = [sem(f"ld_x{i}") for i in range(3)]
        ld_ffn = sem("ld_ffn")
        ld_exp = sem("ld_exp")
        cleared = sem("cleared")
        orf_in = sem("orf_in")
        r_ready = sem("r_ready")
        zeroed = sem("zeroed")
        prep_ps = sem("prep_ps")
        prep_ev = sem("prep_ev")
        xbq_rdy = sem("xbq_rdy")
        ln = [[sem(f"ln{n}_{w}") for w in ("st", "mv", "ve", "rstd", "xn")] for n in range(3)]
        xt_save = [sem(f"xt_save{i}") for i in range(2)]
        t1_ps, t1_a, t1_d = sem("t1_ps"), sem("t1_a"), sem("t1_d")
        wkv_hi, wkv_lo = sem("wkv_hi"), sem("wkv_lo")
        x1_hi, x1_lo = sem("x1_hi"), sem("x1_lo")
        k_ps, k_lin, k_sq = sem("k_ps"), sem("k_lin"), sem("k_sq")
        v_ps, v_ev = sem("v_ps"), sem("v_ev")
        v_sum = sem("v_sum")
        kf_ps, k_exp = sem("kf_ps"), sem("k_exp")
        eps_ps = sem("eps_ps")
        kv_ps, kv_ev = sem("kv_ps"), sem("kv_ev")
        nb_ps, nb_ev = sem("nb_ps"), sem("nb_ev")
        bo_in = sem("bo_in")
        q_ps, q_lin, q_sq = sem("q_ps"), sem("q_lin"), sem("q_sq")
        qf_ps, q_exp = sem("qf_ps"), sem("q_exp")
        kvx_in, xat_in = sem("kvx_in"), sem("xat_in")
        n_ps, n_add, n_rec, att_rdy = sem("n_ps"), sem("n_add"), sem("n_rec"), sem("att_rdy")
        at_ps, at_hi, at_lo = sem("at_ps"), sem("at_hi"), sem("at_lo")
        wo_hi, wo_lo = sem("wo_hi"), sem("wo_lo")
        wo_ps, x1 = sem("wo_ps"), sem("x1")
        t2_ps, t2_a, t2_d = sem("t2_ps"), sem("t2_a"), sem("t2_d")
        s_ps, s_add, s_max, s_dif, s_exp, s_step, prob = (sem(n) for n in ("s_ps", "s_add", "s_max", "s_dif", "s_exp", "s_step", "prob"))
        pt_ps, pt_ev = sem("pt_ps"), sem("pt_ev")
        o_ps, x2 = sem("o_ps"), sem("x2")
        t3_ps, t3_a, t3_d = sem("t3_ps"), sem("t3_a"), sem("t3_d")
        r_ps, r_ev = sem("r_ps"), sem("r_ev")
        rt = sem("rt")
        rt_a = sem("rt_a")
        rt_ps = sem("rt_ps")
        mask_rdy, probe_max, slots_rdy, eid_rdy = sem("mask_rdy"), sem("probe_max"), sem("slots_rdy"), sem("eid_rdy")
        sc = sem("sc")
        g_ps, u_ps, silu_rdy, h_rdy, d_ps, s_res = (sem(n) for n in ("g_ps", "u_ps", "silu_rdy", "h_rdy", "d_ps", "s_res"))
        w_hi, w_lo = sem("w_hi"), sem("w_lo")
        x_hi_rdy, x_lo_rdy = sem("x_hi_rdy"), sem("x_lo_rdy")
        h_hi, h_lo = sem("h_hi"), sem("h_lo")
        xe_in = [sem(f"xe_in{k}") for k in range(4)]
        e_t, e_tev, e_w, e_gu, e_silu, e_h, e_dn, e_yev = (
            sem(n) for n in ("e_t", "e_tev", "e_w", "e_gu", "e_silu", "e_h", "e_dn", "e_yev"))
        ye_out = [sem(f"ye_out{k}") for k in range(4)]
        yg_in = [sem(f"yg_in{k}") for k in range(16)]
        comb1, comb = sem("comb1"), sem("comb")
        stored = sem("stored")
        warm = sem("warm")
        passed = sem("passed")

        def apart(eng):
            eng.sem_inc(passed, 1)

        def tok(a, c):
            return a[bass.ds(c * CT, CT), :].rearrange("(p j) d -> p j d", j=TPC)

        def feat(a):
            return a.rearrange("(k p) n -> p k n", p=P)

        def experts_of(first, n, engine):
            return nc.values_load_multi_w_load_instructions(
                EID[0:1, bass.ds(first, n)], engines=[engine], min_val=0, max_val=(E - 1) * EW,
                skip_runtime_bounds_check_because="a count of at most E experts, held to E - 1, times EW")[1]

        block = ctx.enter_context(nc.Block())

        @block.sync
        def _(sp):
            n = [0] * 4
            sp.dma_start(X[:, 0:TPC, :], tok(x, 0)).then_inc(ld_x[0], 16)
            for dst, src in ((CTXT, feat(ctxT)), (XWK, feat(xwkT)), (XWV, feat(xwvT))):
                sp.dma_start(dst, src).then_inc(ld_ctx, 16)
            for dst, src in ((WK, wkT), (WV, wvT)):
                sp.dma_start(dst, feat(src)).then_inc(ld_kv, 16)
            with nc.allow_non_contiguous_dma(reason="a few hundred bias values"):
                for i, b in enumerate((xbk, xbv, xbq)):
                    sp.dma_start(XB[:, (i + 1) % 3, :], b.rearrange("(k p) -> p k", p=P)).then_inc(ld_xb, 16)
            sp.dma_start(X[:, TPC:2 * TPC, :], tok(x, 1)).then_inc(ld_x[1], 16)
            for dst, src in ((XWQ, feat(xwq)), (XWO, feat(xwoT))):
                sp.dma_start(dst, src).then_inc(ld_xqo, 16)
            sp.dma_start(XBOR[:, :], xbo[None, :].to_broadcast((P, D))).then_inc(ld_prep, 16)
            sp.wait_ge(cleared, 1)
            sp.dma_start(R[64:128, :], normblk_d).then_inc(ld_prep, 16)
            for h in range(4):
                sp.dma_start(R[DK * h:DK * h + DK, M * h:M * h + M], orfT).then_inc(orf_in, 16)
            for c in range(2, CH):
                sp.dma_start(X[:, TPC * c:TPC * c + TPC, :], tok(x, c)).then_inc(ld_x[2], 16)
            for dst, src in ((WQ, wqT), (WO, woT)):
                sp.dma_start(dst, feat(src)).then_inc(ld_attn, 16)
            for dst, src in ((BOR[:, :], bo[None, :].to_broadcast((P, D))), (TRI[:, :], tri_d),
                             (DESC[:, :], desc16_d.to_broadcast((P, E))), (IOTA[:, :], iota_d.to_broadcast((P, ST)))):
                sp.dma_start(dst, src).then_inc(ld_late, 16)
            for dst, src in ((SG, feat(sgT)[:, :, 0:SW]), (SU, feat(suT)[:, :, 0:SW]), (GW, feat(gwT)),
                             (SGU[:, :, 0:SF[-1]], feat(sgT)[:, :, SW:SFF]), (SGU[:, :, SF[-1]:P], feat(suT)[:, :, SW:SFF]),
                             (SD[:, 0:NF - 1, :], feat(sdT[0:(NF - 1) * P, :])), (SD[0:SF[-1], NF - 1, :], sdT[(NF - 1) * P:SFF, :])):
                sp.dma_start(dst, src).then_inc(ld_ffn, 16)
            sp.wait_ge(cleared, 7)
            flat = slots_x.rearrange("(p r) d -> p (r d)", p=P)
            per = ST * D // 10
            def zero(i):
                sp.dma_start(flat[:, bass.ds(i * per, per)], ZERO[:, 0:per]).then_inc(zeroed, 16)

            def save(c, src, rdy_a, rdy_d, n, s):
                sp.wait_ge(rdy_a, n)
                sp.wait_ge(rdy_d, n)
                sp.dma_start(XT[:, :, bass.ds(c * CT, CT)], src).then_inc(s, 16)

            zero(0)
            zero(1)
            with sp.Fori(0, B) as b:
                for i in range(2):
                    save(2 * b + i, X1T[:, i], t1_a, t1_d, 2 * b + i + 1, xt_save[i])
                    zero(2 * b + i + 2)
            with sp.Fori(0, CH) as d:
                sp.wait_ge(ln[2][4], TPC * (d + 1))
                sp.dma_start(XN3T[:, bass.ds(TPC * d, TPC), :], XN3C).then_inc(xt_save[1], 16)
                save(d, X3T, t3_a, t3_d, d + 1, xt_save[0])
            sp.wait_ge(r_ps, CH)
            sp.wait_ge(eid_rdy, 1)
            for i in range(2):
                sp.wait_ge(xt_save[i], 16 * (B + CH))
            for k in range(KD):
                sp.dma_start(WEXP[:, :, 2 * FF * k:2 * FF * (k + 1)], wgu[:, k * P:k * P + P, :].rearrange("e p f -> p e f")).then_inc(ld_exp, 16)
            sp.dma_start(WEXP[:, :, 2 * FF * KD:EW], wdn.rearrange("e p d -> p e d")).then_inc(ld_exp, 16)

            sp.wait_ge(sc, 16 * 2 * T)

            def load(s, k):
                wait(sp, e_t, s - 3)
                sp.dma_start(XE[:, k % 4, :], slots_x[bass.ds(s * P, P), :]).then_inc(xe_in[k % 4], 16)

            def store(s, k):
                sp.wait_ge(e_yev, s + 1)
                sp.dma_start(slots_y[bass.ds(s * P, P), :], YE[:, k % 4, :]).then_inc(ye_out[k % 4], 16)

            for s in range(8):
                load(s, s)
            with sp.Fori(1, ST // 8) as g:
                for k in range(8):
                    load(8 * g + k, k)
                    store(8 * g + k - 8, k)
            for s in range(ST - 8, ST):
                store(s, s)
            for c in range(CH):
                sp.wait_ge(comb, TPC * (c + 1))
                sp.wait_ge(s_res, TPC * (c + 1))
                sp.dma_start(tok(out, c), X[:, TPC * c:TPC * c + TPC, :]).then_inc(stored, 16)
            sp.wait_ge(stored, 16 * CH)

        @block.gpsimd
        def _(pool):
            pool.memset(R[:, :], 0.0).then_inc(cleared, 1)
            pool.memset(HALF[:, :], -0.5).then_inc(cleared, 1)
            pool.memset(EPS[:, :], KEPS).then_inc(cleared, 1)
            pool.memset(VEXT, 1.0).then_inc(cleared, 1)
            pool.memset(ONES[:, :], 1.0).then_inc(cleared, 1)
            pool.memset(KVN[:, 0, :], 0.0).then_inc(cleared, 1)
            pool.memset(ZERO, 0.0).then_inc(cleared, 1)

            def rstd(c, n):
                _, mv, ve, rs = lnbuf[n]
                _, s_mv, s_ve, s_rstd, _ = ln[n]
                pool.wait_ge(s_mv, TPC * (c + 1))
                apart(pool)
                pool.tensor_scalar(ve[:, :], mv[:, :, 1], LN_EPS, None, ALU.add).then_inc(s_ve, 1)
                pool.wait_ge(s_ve, c + 1)
                pool.tensor_tensor(rs[:, :], ve[:, :], HALF[:, :], ALU.pow).then_inc(s_rstd, 1)

            pool.wait_ge(cleared, 2)

            def values_sum(c, par):
                pool.wait_ge(v_ev, 2 * c + 2)
                wait(pool, eps_ps, c)
                apart(pool)
                pool.tensor_tensor(VSUM, VEXT[:, par, 0, :], VEXT[:, par, 1, :], ALU.add).then_inc(v_sum, 1)
                for j in range(2, TPC):
                    pool.wait_ge(v_sum, 3 * c + j - 1)
                    pool.tensor_tensor(VSUM, VSUM, VEXT[:, par, j, :], ALU.add).then_inc(v_sum, 1)

            rstd(0, 0)
            pool.wait_ge(cleared, 7)
            with pool.Fori(0, B - 1) as b:
                for i in range(2):
                    rstd(2 * b + i + 1, 0)
                    values_sum(2 * b + i, i)
            rstd(CH - 1, 0)
            values_sum(CH - 2, 0)
            values_sum(CH - 1, 1)
            pool.wait_ge(ln[0][4], TPC * CH)
            pool.wait_ge(ld_late, 16 * NLATE)
            with pool.Fori(0, CH) as c:
                xc = X[:, bass.ds(TPC * c, TPC), :]
                pool.tensor_tensor(xc, xc, BOR[:, None, :].to_broadcast((P, TPC, D)), ALU.add).then_inc(bo_in, 1)

            def attn_state(c):
                wait(pool, n_ps, TPC * c)
                apart(pool)
                pool.tensor_copy(KVXB, KVX[:, c // 2, :]).then_inc(kvx_in, 1)

            def ctx_products(d):
                wait(pool, o_ps, 2 * d)
                apart(pool)
                pool.tensor_copy(GKB[:, :, 0:SKV], GK[:, :, bass.ds((d // 2) * SKV, SKV)]).then_inc(xat_in, 1)
                pool.tensor_copy(GQB, GQ[:, bass.ds((d // 2) * SKV, SKV)]).then_inc(xat_in, 1)
                pool.tensor_copy(VPB[0:SKV, :], VP[0:SKV, d // 2, :]).then_inc(xat_in, 1)

            pool.wait_ge(nb_ev, B)
            def chunk(c):
                if not (isinstance(c, int) and c == CH - 1):
                    attn_state(c + 1)
                if not (isinstance(c, int) and c == 0):
                    rstd(c - 1, 2)
                rstd(c, 1)
                ctx_products(c)

            attn_state(0)
            chunk(0)
            chunk(1)
            with pool.Fori(1, B - 1) as b:
                chunk(2 * b)
                chunk(2 * b + 1)
            chunk(CH - 2)
            chunk(CH - 1)
            rstd(CH - 1, 2)

            pool.wait_ge(slots_rdy, 1)
            pool.wait_ge(zeroed, 160)
            pool.wait_ge(xt_save[1], 16 * (B + CH))
            for t in range(T):
                for j in range(2):
                    pool.indirect_dma_start(slots_x, bass.IndirectOffsetOnAxis(ap=SLOT[:, j, t:t + 1], axis=0),
                                            XN3T[:, t, :], None).then_inc(sc, 16)
            for k in range(4):
                pool.wait_ge(ye_out[k], 16 * (ST // 4))
            for t in range(T):
                if t >= 8:
                    pool.wait_ge(comb, t - 7)
                for j in range(2):
                    k = 2 * (t % 8) + j
                    pool.indirect_dma_start(YG[:, k, :], None, slots_y,
                                            bass.IndirectOffsetOnAxis(ap=SLOT[:, j, t:t + 1], axis=0)).then_inc(yg_in[k], 16)

        @block.scalar
        def _(act):
            with nc.allow_non_contiguous_dma(reason="a few hundred bias values"):
                for dst, src in ((IDENT[:, :], ident_d), (BQK[:, 1, :], bk.rearrange("(k p) -> p k", p=P)),
                                 (BVR[:, :], bv[None, :].to_broadcast((P, D))), (BQK[:, 0, :], bq.rearrange("(k p) -> p k", p=P))):
                    act.dma_start(dst, src).then_inc(ld_first, 16)

            def exp_k(c, j, par):
                for half in range(2):
                    n = TPC * c + j
                    act.wait_ge(kf_ps, 2 * n + half + 1)
                    if half == 0:
                        wait(act, kv_ps, n - 1)
                    act.activation(KPHI[:, j % 2, 512 * half:512 * half + 512], pF[half][:, :], ACT.Exp).then_inc(k_exp, 1)

            def square(c, dst, bias, ps, lin, sq, qs=range(4)):
                for q in qs:
                    if q < 2:
                        act.wait_ge(lin, 2 * c + q + 1)
                        act.activation(dst[64:128, q, :], dst[0:64, q, :], ACT.Square).then_inc(sq, 1)
                    else:
                        r = 64 * (q % 2)
                        act.wait_ge(ps, 2 * c + 2)
                        act.activation(dst[0:64, q, :], pK[1][r:r + 64, :], ACT.Identity, bias=bias[r:r + 64, 1:2])
                        act.activation(dst[64:128, q, :], pK[1][r:r + 64, :], ACT.Square, bias=bias[r:r + 64, 1:2]).then_inc(sq, 1)

            def front(c, par):
                act.wait_ge(t1_ps, 2 * c + 1)
                wait(act, xt_save[par], 16 * ((c - par) // 2))
                act.copy(X1T[:, par, 0, :], pT[0][:, :]).then_inc(t1_a, 1)
                for h, s in enumerate((t1_a, t1_d)):
                    act.wait_ge(s, c + 1)
                    act.copy(r32(X1H[:, h, :]), X1T[:, par, h, :]).then_inc(x1_hi, 1)

            def body1(c, d, par):
                if d is not None:
                    exp_k(d, 0, 1 - par)
                if c is not None:
                    front(c, par)
                if d is not None:
                    exp_k(d, 1, 1 - par)
                if c is not None:
                    square(c, KDT[:, par], BQK[:, 1], k_ps, k_lin, k_sq)
                if d is not None:
                    exp_k(d, 2, 1 - par)
                    exp_k(d, 3, 1 - par)

            act.wait_ge(cleared, 2)
            act.activation(REC[:, 0, 0:1], HALF[:, 0:1], ACT.Exp).then_inc(warm, 1)
            act.wait_ge(ld_kv, 16 * 2)
            act.copy(r32(WKVH[:, 0]), WK).then_inc(wkv_hi, 1)
            act.copy(r32(WKVH[:, 1]), WV).then_inc(wkv_hi, 1)
            act.wait_ge(ld_first, 16 * NFIRST)
            body1(0, None, 0)
            body1(1, 0, 1)
            with act.Fori(1, B) as b:
                body1(2 * b, 2 * b - 1, 0)
                body1(2 * b + 1, 2 * b, 1)
            body1(None, CH - 1, 0)

            def exp_q(c, lo, hi):
                for i in range(lo, hi):
                    act.wait_ge(qf_ps, 8 * c + i + 1)
                    act.activation(QPHI[:, i, :], pF[i % 2][:, :], ACT.Exp).then_inc(q_exp, 1)

            def body2(c, d, e):
                if c is not None:
                    for q, first, last in ((0, 0, 0), (1, 0, 0), (2, 0, 0), (3, 0, 5)):
                        square(c, KDT[:, 0], BQK[:, 0], q_ps, q_lin, q_sq, (q,))
                        exp_q(c, first, last)
                if d is not None:
                    act.wait_ge(t2_ps, 2 * d + 1)
                    act.copy(X2T[:, 0, :], pT[0][:, :]).then_inc(t2_a, 1)
                if c is not None:
                    exp_q(c, 5, 8)
                if isinstance(c, int) and c == 0:
                    act.wait_ge(bo_in, CH)
                    act.wait_ge(v_ev, 2 * CH)
                    act.wait_ge(ld_attn, 16 * 2)
                    act.copy(r32(WOH), WO).then_inc(wo_hi, 1)
                if d is not None:
                    act.wait_ge(s_dif, d + 1)
                    act.activation(PEXP, SDIF, ACT.Exp, scale=float(D) ** -0.5).then_inc(s_exp, 1)
                if e is not None:
                    act.wait_ge(t3_ps, 2 * e + 1)
                    act.wait_ge(xt_save[0], 16 * (B + e))
                    act.copy(X3T[:, 0, :], pF[0][:, :]).then_inc(t3_a, 1)
                if d is not None:
                    act.wait_ge(pt_ps, d + 1)
                    act.copy(PROBT[0:SKV, :], pT[0][0:SKV, :]).then_inc(pt_ev, 1)
                if c is not None:
                    for h in range(KD):
                        act.wait_ge(at_ps, 2 * c + h + 1)
                        act.copy(r32(ATH[:, h, :]), pT[h][:, :]).then_inc(at_hi, 1)

            act.wait_ge(zeroed, 160)
            body2(0, None, None)
            body2(1, 0, None)
            with act.Fori(1, B) as b:
                body2(2 * b, 2 * b - 1, 2 * b - 2)
                body2(2 * b + 1, 2 * b, 2 * b - 1)

            def silu(u, f):
                i = NF * u + f
                act.wait_ge(g_ps, i + 1)
                wait(act, h_rdy, i - 1)
                act.activation(SIL[f % 2][P - SF[f]:P, :], pK[f % 2][0:SF[f], :], ACT.Silu).then_inc(silu_rdy, 1)

            def copy_x3(e, bank):
                act.wait_ge(t3_ps, 2 * e + 1)
                act.wait_ge(xt_save[0], 16 * (B + e))
                act.copy(X3T[:, 0, :], bank[:, :]).then_inc(t3_a, 1)

            d = CH - 1
            copy_x3(d - 1, pT[0])
            silu(0, 0)
            act.wait_ge(t2_ps, 2 * d + 1)
            act.copy(X2T[:, 0, :], pT[0][:, :]).then_inc(t2_a, 1)
            silu(0, 1)
            act.wait_ge(s_dif, d + 1)
            act.activation(PEXP, SDIF, ACT.Exp, scale=float(D) ** -0.5).then_inc(s_exp, 1)
            silu(0, 2)
            act.wait_ge(pt_ps, d + 1)
            act.copy(PROBT[0:SKV, :], pT[0][0:SKV, :]).then_inc(pt_ev, 1)
            silu(0, 3)
            copy_x3(d, pT[0])
            silu(0, 4)
            act.wait_ge(probe_max, 1)
            act.activation(SIG[:, :], LOG[:, :, E], ACT.Exp, scale=-1.0).then_inc(rt_a, 1)
            act.activation(TMP[1], TMP[0], ACT.Exp).then_inc(rt_a, 1)
            silu(0, 5)
            act.wait_ge(o_ps, 2 * CH)
            for f in range(NF):
                silu(1, f)
                for w, w_h, _ in WSPLIT[3 * f:3 * f + 3]:
                    act.copy(r32(w_h), w).then_inc(w_hi, 1)

            def split_x(u):
                act.copy(r32(x_hi(u)), x_whole(u)).then_inc(x_hi_rdy, 1)

            def silu_s(u, f):
                act.wait_ge(h_lo, NF * (u - CS) + f + 1)
                silu(u, f)

            def h_split(u, f):
                act.wait_ge(h_rdy, NF * u + f + 1)
                act.wait_ge(d_ps, NF * u + f - 2)
                act.copy(r32(HTH[f % 3][0:SF[f], :]), SIL[f % 2][0:SF[f], :]).then_inc(h_hi, 1)

            def shared_s(u):
                for f in range(NF):
                    silu_s(u, f)
                    h_split(u, f)
                    if f == 1 and not (isinstance(u, int) and u == CH - 1):
                        split_x(u + 1)

            silu(2, 0)
            silu(2, 1)
            split_x(CS)
            for f in range(2, NF):
                silu(2, f)
            with act.Fori(CS, CB) as u:
                shared_s(u)

            def copy_xt(s, k):
                act.wait_ge(e_t, s + 1)
                wait(act, e_gu, s - 1)
                act.copy(XET[:, k % 2, :], pT[k % 2][:, 0:D]).then_inc(e_tev, 1)

            def silu_e(s, k):
                act.wait_ge(e_gu, s + 1)
                wait(act, e_h, s - 1)
                act.activation(ESIL[:, k % 2, :], pK[k % 2][:, 0:FF], ACT.Silu).then_inc(e_silu, 1)

            def copy_y(s, k, n):
                act.wait_ge(e_dn, s + 1)
                wait(act, ye_out[k % 4], 16 * n)
                act.copy(YE[:, k % 4, :], pO[k % 2][:, 0:D]).then_inc(e_yev, 1)

            for s in range(8):
                copy_xt(s, s)
                if s >= 1:
                    silu_e(s - 1, s - 1)
                if s >= 2:
                    copy_y(s - 2, s - 2, (s - 2) // 4)
            with act.Fori(1, ST // 8) as g:
                for k in range(8):
                    copy_xt(8 * g + k, k)
                    silu_e(8 * g + k - 1, k - 1)
                    copy_y(8 * g + k - 2, k - 2, 2 * g + (k - 2) // 4)
            silu_e(ST - 1, ST - 1)
            for s in range(ST - 2, ST):
                copy_y(s, s, s // 4)
            with act.Fori(CB, CH - 1) as u:
                shared_s(u)
            shared_s(CH - 1)

        @block.tensor
        def _(pe):
            def mm(out_, lhsT, rhs, start=True, stop=True, **kw):
                return pe.matmul(out_, lhsT, rhs, start=start, stop=stop, **kw)

            def split_mm(dst, w, x, start, stop):
                for i, (a, b) in enumerate(((w[0], x[0]), (w[1], x[0]), (w[0], x[1]))):
                    last = mm(dst, r32(a), r32(b), start=start and i == 0, stop=stop and i == 2, skip_group_check=True)
                return last

            def project(dst, w, src, m):
                for k in range(KD):
                    last = mm(dst[:, 0:src[k].shape[-1]], w[:, k, m * P:m * P + P], src[k], start=(k == 0), stop=(k == KD - 1))
                return last

            def t1(c):
                pe.wait_ge(ln[0][4], TPC * (c + 1))
                wait(pe, v_ev, 2 * c)
                for h in range(KD):
                    for j in range(TPC):
                        last = pe.transpose(pT[h][:, j * P:j * P + P], XN[:, j, h * P:h * P + P], IDENT[:, :])
                    last.then_inc(t1_ps, 1)

            def k_proj(c, par):
                pe.wait_ge(x1_lo, 2 * c + 2)
                for m in range(KD):
                    for k in range(KD):
                        ws = [w[:, 0, k, m * P:m * P + P] for w in (WKVH, WKVL)]
                        last = split_mm(pK[m][:, :], ws, (X1H[:, k, :], X1L[:, k, :]), k == 0, k == KD - 1)
                    last.then_inc(k_ps, 1)

            def v_proj(c, par, half):
                for j in (2 * half, 2 * half + 1):
                    for k in range(KD):
                        xs = [x[:, k, j * P:j * P + P] for x in (X1H, X1L)]
                        last = split_mm(pT[j // 2][:, D * (j % 2):D * (j % 2) + D], xs, (WKVH[:, 1, k, :], WKVL[:, 1, k, :]),
                                        k == 0, k == KD - 1)
                    if j % 2:
                        last.then_inc(v_ps, 1)

            def k_feat(c, j, par):
                for half in range(2):
                    n = TPC * c + j
                    if j == 0:
                        pe.wait_ge(k_sq, 4 * c + 2 * half + 2)
                    wait(pe, k_exp, 2 * n - 1 + half)
                    for q in range(2):
                        last = mm(pF[half][:, 256 * q:256 * q + 256], KDT[:, par, 2 * half + q, j * P:j * P + P], R[:, :])
                    last.then_inc(kf_ps, 1)

            def kv(c, j, par):
                n = TPC * c + j
                if j == 0:
                    pe.wait_ge(v_ev, 2 * c + 2)
                first = j == 0 and par == 0
                if first:
                    wait(pe, kv_ev, c)
                pe.wait_ge(k_exp, 2 * n + 2)
                if j == 0:
                    pe.wait_ge(v_sum, 3 * c + 3)
                    mm(pO[0][:, 0:HV], EPS[:, :], VSUM, start=first, stop=False, skip_group_check=True).then_inc(eps_ps, 1)
                for p in range(PAIRS):
                    last = mm(pO[0][:, HV2 * p:HV2 * p + HV2], KPHI[:, j % 2, P * p:P * p + P],
                              VEXT[:, par, j, HV2 * p:HV2 * p + HV2], start=False, stop=(j == TPC - 1 and par == 1 and p == PAIRS - 1),
                              skip_group_check=True)
                last.then_inc(kv_ps, 1)

            def body1(c, d, par):
                if d is not None:
                    k_feat(d, 0, 1 - par)
                if c is not None:
                    t1(c)
                if d is not None:
                    k_feat(d, 1, 1 - par)
                    kv(d, 0, 1 - par)
                if c is not None:
                    k_proj(c, par)
                if d is not None:
                    k_feat(d, 2, 1 - par)
                    kv(d, 1, 1 - par)
                if c is not None:
                    v_proj(c, par, 0)
                if d is not None:
                    k_feat(d, 3, 1 - par)
                    kv(d, 2, 1 - par)
                if c is not None:
                    v_proj(c, par, 1)
                if d is not None:
                    kv(d, 3, 1 - par)

            pe.wait_ge(ld_ctx, 16 * 3)
            W2 = B * SKV
            ctx_t = [CTXT[:, 0, :], CTXT[:, 1, :]]
            for m in range(KD):
                project(pF[m], XWK, ctx_t, m).then_inc(prep_ps, 1)
            for m in range(KD):
                project(pO[m], XWV, ctx_t, m).then_inc(prep_ps, 1)
            pe.wait_ge(ld_first, 16 * NFIRST)
            pe.wait_ge(wkv_lo, 2)
            body1(0, None, 0)
            pe.wait_ge(ld_xqo, 16 * 2)
            pe.wait_ge(prep_ev, 2)
            pe.wait_ge(xbq_rdy, 1)
            pe.wait_ge(v_ev, 2)
            for m in range(KD):
                project(pT[m], XWQ, [KT[:, 0, :], KT[:, 1, :]], m).then_inc(prep_ps, 1)
            pe.wait_ge(k_sq, 4)
            for k in range(KD):
                last = mm(pK[0][:, 0:W2], XBQ[:, k, :], KT[:, k, :], start=(k == 0), stop=(k == KD - 1))
            last.then_inc(prep_ps, 1)
            pe.wait_ge(prep_ev, 4)
            for b in range(B):
                dst = (pF[b // 2])[0:SKV, D * (b % 2):D * (b % 2) + D]
                for k in range(KD):
                    last = mm(dst, VT[:, k, b * SKV:b * SKV + SKV], XWO[:, k, :], start=(k == 0), stop=(k == KD - 1))
                last.then_inc(prep_ps, 1)
            pe.wait_ge(prep_ev, 11)
            pe.wait_ge(ld_prep, 16 * NPREP)
            pe.wait_ge(r_ready, 1)
            body1(1, 0, 1)
            with pe.Fori(1, B) as b:
                body1(2 * b, 2 * b - 1, 0)
                body1(2 * b + 1, 2 * b, 1)
            body1(None, CH - 1, 0)
            def q_proj(c, ms=range(KD)):
                for m in ms:
                    project(pK[m][:, :], WQ, [XT[:, k, bass.ds(c * CT, CT)] for k in range(KD)], m).then_inc(q_ps, 1)

            def q_feat(c, lo, hi):
                for i in range(lo, hi):
                    pe.wait_ge(q_sq, 4 * c + i // 2 + 1)
                    if i < 2:
                        wait(pe, (t3_a, t3_d)[i], c - 2)
                    if i >= 2:
                        pe.wait_ge(q_exp, 8 * c + i - 1)
                    mm(pF[i % 2][:, :], R[:, P * (i % 2):P * (i % 2) + P], KDT[:, 0, i // 2, :]).then_inc(qf_ps, 1)

            def num(c, p):
                if p == 0:
                    pe.wait_ge(kvx_in, c + 1)
                    pe.wait_ge(q_sq, 4 * c + 4)
                    wait(pe, x1, 2 * c)
                pe.wait_ge(q_exp, 8 * c + p + 1)
                for j in (2, 3, 0, 1):
                    last = mm(pN[j][:, HV2 * p:HV2 * p + HV2], QPHI[:, p, j * P:j * P + P], KVXB[:, HV2 * p:HV2 * p + HV2])
                    if p == PAIRS - 1:
                        last.then_inc(n_ps, 1)

            def transpose_chunk(src, ps):
                for h in range(KD):
                    for j in range(TPC):
                        last = pe.transpose(pT[h][:, j * P:j * P + P], src(j, h), IDENT[:, :])
                    last.then_inc(ps, 1)

            def att_t(c):
                pe.wait_ge(att_rdy, c + 1)
                transpose_chunk(lambda j, h: ATT[:, j, h * P:h * P + P], at_ps)

            def wo(c, d):
                pe.wait_ge(at_lo, 2 * c + 2)
                pe.wait_ge(wo_lo, 1)
                if d is not None:
                    pe.wait_ge(x2, 2 * d + 2)
                for j in range(TPC):
                    for k in range(KD):
                        xs = [x[:, k, j * P:j * P + P] for x in (ATH, ATL)]
                        last = split_mm(pO[j // 2][:, D * (j % 2):D * (j % 2) + D], xs, (WOH[:, k, :], WOL[:, k, :]),
                                        k == 0, k == KD - 1)
                    if j % 2:
                        last.then_inc(wo_ps, 1)

            def t2(d):
                pe.wait_ge(ln[1][4], TPC * (d + 1))
                wait(pe, r_ev, d)
                transpose_chunk(lambda j, h: XN[:, j, h * P:h * P + P], t2_ps)

            def scores(d, j):
                if j == 0:
                    pe.wait_ge(t2_a, d + 1)
                    pe.wait_ge(t2_d, d + 1)
                    pe.wait_ge(xat_in, 3 * (d + 1))
                for k in range(KD):
                    last = mm(pS[:, j, 0:SKV], X2T[:, k, j * P:j * P + P], GKB[:, k, 0:SKV], start=(k == 0), stop=(k == KD - 1))
                if j == TPC - 1:
                    last.then_inc(s_ps, 1)

            def prob_t(d):
                pe.wait_ge(prob, d + 1)
                for j in range(TPC):
                    last = pe.transpose(pT[0][0:SKV, j * P:j * P + P], PROB[:, j, :], IDENT[:, :])
                last.then_inc(pt_ps, 1)

            def out_x(c, d):
                if c is not None:
                    pe.wait_ge(n_add, 8 * c + 4)

                def dst(j):
                    return pO[j // 2][:, D * (j % 2):D * (j % 2) + D]

                for j in range(TPC):
                    for k in range(KD):
                        mm(dst(j), X2T[:, k, j * P:j * P + P], XWO[:, k, :], start=(k == 0 and j % 2 == 0), stop=False,
                           skip_group_check=True)
                pe.wait_ge(pt_ev, d + 1)
                for j in range(TPC):
                    last = mm(dst(j), PROBT[0:SKV, j * P:j * P + P], VPB[0:SKV, :], start=False, stop=(j % 2 == 1),
                              skip_group_check=True)
                    if j % 2:
                        last.then_inc(o_ps, 1)

            def t3(c, e, h, bank=pF):
                pe.wait_ge(ln[2][4], TPC * (e + 1))
                if c is not None:
                    pe.wait_ge(q_exp, 8 * c + 7 + h)
                for j in range(TPC):
                    last = pe.transpose(bank[h][:, j * P:j * P + P], XN3C[:, j, h * P:h * P + P], IDENT[:, :])
                last.then_inc(t3_ps, 1)

            def router(d):
                pe.wait_ge(t3_a, d + 1)
                pe.wait_ge(t3_d, d + 1)
                pe.wait_ge(r_ev, d + 1)
                for j in range(TPC):
                    for k in range(KD):
                        last = mm(pR[:, j, 0:E + 1], X3T[:, k, j * P:j * P + P], GW[:, k, :],
                                  start=(k == 0), stop=(k == KD - 1))
                last.then_inc(r_ps, 1)

            def body2(c, d, e):
                if c is not None:
                    q_feat(c, 2, 4)
                for p in range(PAIRS):
                    if c is not None:
                        num(c, p)
                        if p < 4:
                            q_feat(c, p + 4, p + 5)
                    if d is not None and p == 0:
                        t2(d)
                    if d is not None and p in (1, 2, 3, 4):
                        scores(d, p - 1)
                    if e is not None and p == PAIRS - 2:
                        t3(c, e, 0)
                if d is not None:
                    prob_t(d)
                if e is not None:
                    t3(c, e, 1)
                if d is not None:
                    out_x(c, d)
                more = not (isinstance(c, int) and c == CH - 1)
                first = isinstance(c, int) and c == 0
                if first:
                    pe.wait_ge(n_add, 8)
                    q_proj(1, (0,))
                att_t(c)
                if first:
                    q_proj(1, (1,))
                if more and not first:
                    q_proj(c + 1)
                wo(c, d)
                if more:
                    q_feat(c + 1, 0, 2)
                if e is not None:
                    router(e)

            pe.wait_ge(ld_attn, 16 * 2)
            pe.wait_ge(xt_save[0], 16)
            q_proj(0)
            pe.wait_ge(kv_ev, 2 * B)
            banks = (pT[0], pT[1], pO[1], pT[0])
            for b in range(B):
                if b == B - 1:
                    pe.wait_ge(nb_ev, 1)
                mm(banks[b][:, 0:HV], EPS[:, :], KVX[:, b, :]).then_inc(nb_ps, 1)
            q_feat(0, 0, 2)
            pe.wait_ge(nb_ev, B)
            for i in range(2):
                pe.wait_ge(xt_save[i], 16 * B)
            body2(0, None, None)
            pe.wait_ge(ld_ffn, 16 * 7)
            body2(1, 0, None)
            with pe.Fori(1, B - 1) as b:
                body2(2 * b, 2 * b - 1, 2 * b - 2)
                body2(2 * b + 1, 2 * b, 2 * b - 1)
            for c in range(CH - 2, CH):
                body2(c, c - 1, c - 2)

            def gate_up(u, f):
                i = NF * u + f
                wait(pe, h_rdy, i - 1)
                src = [XT[:, k, bass.ds(u * CT, CT)] for k in range(KD)]
                if f == NF - 1:
                    project(pK[f % 2], SGU, src, 0).then_inc(g_ps, 1)
                else:
                    project(pK[f % 2], SG, src, f).then_inc(g_ps, 1)
                    project(pF[f % 2], SU, src, f).then_inc(u_ps, 1)

            def down(u, f):
                i = NF * u + f
                pe.wait_ge(h_rdy, i + 1)
                if f == 0:
                    wait(pe, s_res, TPC * u)
                for j in range(TPC):
                    last = mm(pO[j // 2][:, D * (j % 2):D * (j % 2) + D], HT[f % 3][0:SF[f], j * P:j * P + P], SD[0:SF[f], f, :],
                              start=(f == 0 and j % 2 == 0), stop=(f == NF - 1 and j % 2 == 1), skip_group_check=True)
                last.then_inc(d_ps, 1)

            def counts():
                pe.wait_ge(mask_rdy, 1)
                mm(pT[0][:, :], TRI[:, :], TMP[4])
                mm(pT[1][:, :], ONES[:, :], TMP[4]).then_inc(rt_ps, 1)

            def shared(u, begin):
                for f in range(1, NF):
                    gate_up(u, f)
                    if u == 1 and f == 4:
                        counts()
                    down(u, f - 1)
                begin(u + 1)
                down(u, NF - 1)

            def gate_up_s(u, f):
                pe.wait_ge(h_rdy, NF * u + f - 1)
                xs = [(x_hi(u)[:, k, :], x_lo(u)[:, k, :]) for k in range(KD)]
                if f == NF - 1:
                    sides = ((gu_hi, GULO, pK[f % 2], g_ps),)
                    pe.wait_ge(w_lo, NW)
                else:
                    sides = ((gate_hi[f], GLO[:, :, f * P:f * P + P], pK[f % 2], g_ps), (up_hi[f], ULO[:, :, f * P:f * P + P], pF[f % 2], u_ps))
                    pe.wait_ge(w_lo, 2 * f + 2)
                for w_h, w_l, dst, s in sides:
                    for k in range(KD):
                        last = split_mm(dst[:, :], (w_h[:, k, :], w_l[:, k, :]), xs[k], k == 0, k == KD - 1)
                    last.then_inc(s, 1)

            def down_s(u, f):
                pe.wait_ge(h_lo, NF * (u - CS) + f + 3)
                pe.wait_ge(w_lo, NW + f + 1)
                if f == 0:
                    pe.wait_ge(s_res, TPC * u)
                for j in range(TPC):
                    hs = [a[0:SF[f], j * P:j * P + P] for a in (HTH[f % 3], HTL[f % 3])]
                    last = split_mm(pO[j // 2][:, D * (j % 2):D * (j % 2) + D], hs, (down_hi[f][0:SF[f], :], DLO[0:SF[f], f, :]),
                                    f == 0 and j % 2 == 0, f == NF - 1 and j % 2 == 1)
                last.then_inc(d_ps, 1)

            def begin_s(u):
                pe.wait_ge(x_lo_rdy, u - CS + 1)
                gate_up_s(u, 0)

            def shared_s(u, more):
                for f in range(1, NF):
                    gate_up_s(u, f)
                    if f >= 2:
                        down_s(u, f - 2)
                if more:
                    begin_s(u + 1)
                down_s(u, NF - 2)
                down_s(u, NF - 1)

            d = CH - 1
            pe.wait_ge(xt_save[0], 16 * (B + 1))
            gate_up(0, 0)
            pe.wait_ge(r_ev, d)
            for h in range(KD):
                t3(d, d - 1, h, pT)
            gate_up(0, 1)
            router(d - 1)
            pe.wait_ge(r_ev, d + 1)
            t2(d)
            for j in range(TPC):
                scores(d, j)
            gate_up(0, 2)
            prob_t(d)
            out_x(None, d)
            gate_up(0, 3)
            pe.wait_ge(x2, 2 * d + 2)
            down(0, 0)
            down(0, 1)
            down(0, 2)
            for h in range(KD):
                t3(None, d, h, pT)
            gate_up(0, 4)
            down(0, 3)
            router(d)
            gate_up(0, 5)
            down(0, 4)
            gate_up(1, 0)
            down(0, 5)
            pe.wait_ge(ld_late, 16 * NLATE)
            pe.wait_ge(xt_save[0], 16 * (B + CH))
            shared(1, lambda u: gate_up(u, 0))
            shared(2, begin_s)
            for u in range(CS, CB):
                shared_s(u, u < CB - 1)

            pe.wait_ge(ld_exp, 16 * 3)
            pe.wait_ge(eid_rdy, 1)

            def tx(s, k, n):
                pe.wait_ge(xe_in[k % 4], 16 * (n + 1))
                wait(pe, e_tev, s - 1)
                for h in range(KD):
                    last = pe.transpose(pT[k % 2][:, h * P:h * P + P], XE[:, k % 4, h * P:h * P + P], IDENT[:, :])
                last.then_inc(e_t, 1)

            def gu(s, k):
                pe.wait_ge(e_w, s + 1)
                pe.wait_ge(e_tev, s + 1)
                wait(pe, e_h, s - 1)
                for i in range(2):
                    for h in range(KD):
                        last = mm(pK[k % 2][:, P * i:P * i + P], WE[:, k % 2, 2 * FF * h + FF * i:2 * FF * h + FF * i + FF],
                                  XET[:, k % 2, h * P:h * P + P], start=(h == 0), stop=(h == KD - 1))
                last.then_inc(e_gu, 1)

            def dn(s, k, w):
                pe.wait_ge(e_h, s + 1)
                wait(pe, e_yev, s - 1)
                mm(pO[k % 2][:, 0:D], HE[:, k % 2, :], ARENA[:, bass.ds(w + KD * 2 * FF, D)]).then_inc(e_dn, 1)

            w = experts_of(0, 8, mybir.EngineType.PE)
            for s in range(8):
                tx(s, s, s // 4)
                if s >= 1:
                    gu(s - 1, s - 1)
                if s == 2:
                    pe.wait_ge(s_res, TPC * CB)
                if s >= 2:
                    dn(s - 2, s - 2, w[s - 2])
            with pe.Fori(1, ST // 8) as g:
                w = experts_of(8 * g - 4, 12, mybir.EngineType.PE)
                for k in range(8):
                    tx(8 * g + k, k, 2 * g + k // 4)
                    gu(8 * g + k - 1, k - 1)
                    dn(8 * g + k - 2, k - 2, w[k + 2])
            w = experts_of(ST - 4, 4, mybir.EngineType.PE)
            gu(ST - 1, ST - 1)
            dn(ST - 2, ST - 2, w[2])
            dn(ST - 1, ST - 1, w[3])
            begin_s(CB)
            pe.wait_ge(e_yev, ST)
            with pe.Fori(CB, CH - 1) as u:
                shared_s(u, True)
            shared_s(CH - 1, False)

        @block.vector
        def _(dve):
            def stats(c, n):
                st, mv = lnbuf[n][0], lnbuf[n][1]
                for j in range(TPC):
                    dve.bn_stats(st[:, j, :], X[:, TPC * c + j, :]).then_inc(ln[n][0], 1)
                dve.wait_ge(ln[n][0], TPC * (c + 1))
                apart(dve)
                for j in range(TPC):
                    dve.bn_aggr(mv[:, j, :], st[:, j, :]).then_inc(ln[n][1], 1)

            def normalize(c, n, dst):
                mv, rs = lnbuf[n][1], lnbuf[n][3]
                dve.wait_ge(ln[n][3], c + 1)
                for j in range(TPC):
                    dve.tensor_scalar(dst(j), X[:, TPC * c + j, :], mv[:, j, 0:1], rs[:, j:j + 1],
                                      ALU.subtract, ALU.mult).then_inc(ln[n][4], 1)

            def linear(c, dst, bias, ps, lin):
                for q in range(2):
                    r = 64 * q
                    dve.wait_ge(ps, 2 * c + 1)
                    dve.tensor_scalar(dst[0:64, q, :], pK[0][r:r + 64, :], bias[r:r + 64, 0:1], None, ALU.add).then_inc(lin, 1)

            def body1(c, d, par):
                if c is not None:
                    dve.wait_ge(t1_ps, 2 * c + 2)
                    wait(dve, xt_save[par], 16 * ((c - par) // 2))
                    dve.tensor_copy(X1T[:, par, 1, :], pT[1][:, :]).then_inc(t1_d, 1)
                    for h, s in enumerate((t1_a, t1_d)):
                        dve.wait_ge(s, c + 1)
                        dve.wait_ge(x1_hi, 2 * c + h + 1)
                        dve.tensor_tensor(r32(X1L[:, h, :]), X1T[:, par, h, :], X1H[:, h, :], ALU.subtract).then_inc(x1_lo, 1)
                    if d is not None:
                        wait(dve, kf_ps, 8 * d)
                    linear(c, KDT[:, par], BQK[:, 1], k_ps, k_lin)
                    if d is not None:
                        wait(dve, kv_ps, TPC * d)
                    more = not (isinstance(c, int) and c == CH - 1)
                    if more:
                        stats(c + 1, 0)
                    for i in range(2):
                        if i == 1 and more:
                            normalize(c + 1, 0, lambda j: XN[:, j, :])
                        dve.wait_ge(v_ps, 2 * c + i + 1)
                        dve.tensor_tensor(
                            VEXT[:, par, 2 * i:2 * i + 2, :].rearrange("p j (h e) -> p j h e", h=H)[:, :, :, 0:DK],
                            pT[i][:, :].rearrange("p (j h e) -> p j h e", j=2, h=H),
                            BVR[:, None, :].to_broadcast((P, 2, D)).rearrange("p j (h e) -> p j h e", h=H),
                            ALU.add).then_inc(v_ev, 1)
                if d is not None and par == 0:
                    dve.wait_ge(kv_ps, TPC * (d + 1))
                    b = (d - 1) // 2
                    state = pO[0][:, 0:HV].rearrange("p (q e) -> p q e", q=PAIRS)
                    kvx = KVX[:, b, :].rearrange("p (q e) -> p q e", q=PAIRS)
                    dve.tensor_copy(kvx[0:64, :, 0:DK + 1], state[0:64, :, 0:DK + 1]).then_inc(kv_ev, 1)
                    dve.tensor_copy(kvx[64:128, :, DK + 1:HV2], state[64:128, :, DK + 1:HV2]).then_inc(kv_ev, 1)

            dve.sem_inc(h_lo, 2)
            dve.wait_ge(ld_x[0], 16)
            stats(0, 0)
            normalize(0, 0, lambda j: XN[:, j, :])
            W2 = B * SKV
            dve.wait_ge(wkv_hi, 2)
            for i, w in enumerate((WK, WV)):
                dve.tensor_tensor(r32(WKVL[:, i]), w, WKVH[:, i], ALU.subtract).then_inc(wkv_lo, 1)
            dve.wait_ge(ld_xb, 16 * 3)
            for m in range(KD):
                dve.wait_ge(prep_ps, m + 1)
                dve.tensor_scalar(KT[:, m, :], pF[m][:, 0:W2], XB[:, 1, m:m + 1], None, ALU.add).then_inc(prep_ev, 1)
            for m in range(KD):
                dve.wait_ge(prep_ps, m + 3)
                dve.tensor_scalar(VT[:, m, :], pO[m][:, 0:W2], XB[:, 2, m:m + 1], None, ALU.add).then_inc(prep_ev, 1)
            dve.wait_ge(cleared, 7)
            dve.wait_ge(ld_first, 16 * NFIRST)
            dve.wait_ge(ld_x[1], 16)
            body1(0, None, 0)
            dve.tensor_copy(XBQ, XB[:, 0, :, None].to_broadcast((P, KD, P))).then_inc(xbq_rdy, 1)
            dve.wait_ge(orf_in, 64)
            dve.tensor_scalar(R[0:64, :], R[0:64, :], float(DK) ** -0.25, None, ALU.mult).then_inc(r_ready, 1)
            for m in range(KD):
                dve.wait_ge(prep_ps, m + 5)
                dve.tensor_copy(GK[:, m, :], pT[m][:, 0:W2]).then_inc(prep_ev, 1)
            dve.wait_ge(prep_ps, 7)
            dve.tensor_copy(GQ[:, :], pK[0][:, 0:W2]).then_inc(prep_ev, 1)
            dve.wait_ge(ld_prep, 16 * NPREP)
            for b in range(B):
                dve.wait_ge(prep_ps, 8 + (b | 1))
                dve.tensor_tensor(VP[0:SKV, b, :], pF[b // 2][0:SKV, D * (b % 2):D * (b % 2) + D], XBOR[0:SKV, :],
                                  ALU.add).then_inc(prep_ev, 1)

            dve.wait_ge(ld_x[2], 16 * (CH - 2))
            body1(1, 0, 1)
            with dve.Fori(1, B - 1) as b:
                body1(2 * b, 2 * b - 1, 0)
                body1(2 * b + 1, 2 * b, 1)
            body1(CH - 2, CH - 3, 0)
            body1(CH - 1, CH - 2, 1)
            body1(None, CH - 1, 0)

            def sums(c):
                nb = NB[:, c // 2, :].rearrange("p (h e) -> p h e", h=H)
                for j in (2, 3, 0, 1):
                    dve.wait_ge(n_ps, TPC * c + (j + 2) % 4 + 1)
                    ns = pN[j][:, 0:HV].rearrange("p (h e) -> p h e", h=H)
                    dve.tensor_tensor(DEN[:, j, :], ns[:, :, DK], nb[:, :, DK], ALU.add).then_inc(n_add, 1)
                    dve.tensor_tensor(ATT[:, j, :].rearrange("p (h e) -> p h e", h=H), ns[:, :, 0:DK], nb[:, :, 0:DK],
                                      ALU.add).then_inc(n_add, 1)

            def divide(c):
                dve.wait_ge(n_add, 8 * c + 8)
                dve.reciprocal(REC[:, :, :], DEN[:, :, :]).then_inc(n_rec, 1)
                dve.wait_ge(n_rec, c + 1)
                att = ATT.rearrange("p j (h e) -> p j h e", h=H)
                dve.tensor_tensor(att, att, REC[:, :, :, None].to_broadcast((P, TPC, H, DK)), ALU.mult).then_inc(att_rdy, 1)

            def residual(c, ps, done):
                for i in range(2):
                    dve.wait_ge(ps, 2 * c + i + 1)
                    xc = X[:, bass.ds(TPC * c + 2 * i, 2), :]
                    dve.tensor_tensor(xc, pO[i][:, :].rearrange("p (j d) -> p j d", j=2), xc, ALU.add).then_inc(done, 1)

            def softmax(d):
                dve.wait_ge(s_ps, d + 1)
                dve.wait_ge(xat_in, 3 * (d + 1))
                dve.tensor_tensor(SDIF, pS[:, :, 0:SKV], GQB[:, None, :].to_broadcast((P, TPC, SKV)), ALU.add).then_inc(s_add, 1)
                dve.wait_ge(s_add, d + 1)
                dve.tensor_reduce(SMX[:, 0, :], SDIF, AX_X, ALU.max).then_inc(s_max, 1)
                dve.wait_ge(s_max, d + 1)
                dve.tensor_tensor(SDIF, SDIF, SMX[:, 0, :, None].to_broadcast((P, TPC, SKV)),
                                  ALU.subtract).then_inc(s_dif, 1)
                dve.wait_ge(s_exp, d + 1)
                dve.tensor_reduce(SMX[:, 1, :], PEXP, AX_X, ALU.add).then_inc(s_step, 1)
                dve.wait_ge(s_step, 2 * d + 1)
                dve.reciprocal(SMX[:, 2, :], SMX[:, 1, :]).then_inc(s_step, 1)
                dve.wait_ge(s_step, 2 * d + 2)
                dve.tensor_tensor(PROB, PEXP, SMX[:, 2, :, None].to_broadcast((P, TPC, SKV)),
                                  ALU.mult).then_inc(prob, 1)

            def body2(c, d, e):
                if d is not None:
                    normalize(d, 1, lambda j: XN[:, j, :])
                    dve.wait_ge(t2_ps, 2 * d + 2)
                    dve.tensor_copy(X2T[:, 1, :], pT[1][:, :]).then_inc(t2_d, 1)
                    softmax(d)
                if isinstance(c, int) and c == 0:
                    dve.wait_ge(wo_hi, 1)
                    dve.tensor_tensor(r32(WOL), WO, WOH, ALU.subtract).then_inc(wo_lo, 1)
                if c is not None:
                    sums(c)
                if e is not None:
                    dve.wait_ge(t3_ps, 2 * e + 2)
                    dve.wait_ge(xt_save[0], 16 * (B + e))
                    dve.tensor_copy(X3T[:, 1, :], pF[1][:, :]).then_inc(t3_d, 1)
                if c is not None:
                    divide(c)
                if d is not None:
                    residual(d, o_ps, x2)
                if c is not None:
                    dve.wait_ge(at_ps, 2 * c + 2)
                    for h in range(KD):
                        dve.wait_ge(at_hi, 2 * c + h + 1)
                        dve.tensor_tensor(r32(ATL[:, h, :]), pT[h][:, :], ATH[:, h, :], ALU.subtract).then_inc(at_lo, 1)
                if c is not None and not (isinstance(c, int) and c == CH - 1):
                    linear(c + 1, KDT[:, 0], BQK[:, 0], q_ps, q_lin)
                if d is not None:
                    dve.wait_ge(x2, 2 * d + 2)
                    apart(dve)
                    stats(d, 2)
                if c is not None:
                    dve.wait_ge(bo_in, c + 1)
                    residual(c, wo_ps, x1)
                if c is not None:
                    dve.wait_ge(x1, 2 * c + 2)
                    apart(dve)
                    stats(c, 1)
                if d is not None:
                    dve.wait_ge(xt_save[1], 16 * (B + d))
                    normalize(d, 2, lambda j: XN3C[:, j, :])
                if e is not None:
                    dve.wait_ge(r_ps, e + 1)
                    dve.tensor_copy(LOG[:, bass.ds(TPC * e, TPC), :], pR[:, :, 0:E + 1]).then_inc(r_ev, 1)

            dve.wait_ge(warm, 1)
            linear(0, KDT[:, 0], BQK[:, 0], q_ps, q_lin)
            for b in range(B):
                dve.wait_ge(nb_ps, b + 1)
                dve.tensor_copy(NB[:, b, :], (pT[0], pT[1], pO[1], pT[0])[b][:, 0:HV]).then_inc(nb_ev, 1)
            dve.memset(LOG[:, :, :], 0.0).then_inc(r_ev, 1)
            dve.wait_ge(r_ev, 1)
            body2(0, None, None)
            body2(1, 0, None)
            with dve.Fori(1, B - 1) as b:
                body2(2 * b, 2 * b - 1, 2 * b - 2)
                body2(2 * b + 1, 2 * b, 2 * b - 1)
            for c in range(CH - 2, CH):
                body2(c, c - 1, c - 2)

            def hid(u, f):
                i = NF * u + f
                up = pF[f % 2]
                if f < NF - 1:
                    dve.wait_ge(u_ps, (NF - 1) * u + f + 1)
                else:
                    up = pK[f % 2]
                dve.wait_ge(silu_rdy, i + 1)
                wait(dve, d_ps, i - 2)
                dve.tensor_tensor(HT[f % 3][0:SF[f], :], SIL[f % 2][P - SF[f]:P, :], up[P - SF[f]:P, :], ALU.mult).then_inc(h_rdy, 1)

            def shared_out(u):
                dve.wait_ge(d_ps, NF * u + NF)
                for j in range(TPC):
                    t = TPC * u + j
                    dve.scalar_tensor_tensor(X[:, t, :], pO[j // 2][:, D * (j % 2):D * (j % 2) + D], SIG[:, bass.ds(t, 1)],
                                             X[:, t, :], ALU.mult, ALU.add).then_inc(s_res, 1)

            def w_split(i):
                w, w_h, w_l = WSPLIT[i]
                dve.wait_ge(w_hi, i + 1)
                dve.tensor_tensor(r32(w_l), w, w_h, ALU.subtract).then_inc(w_lo, 1)

            def split_x(u):
                dve.wait_ge(x_hi_rdy, u - CS + 1)
                dve.tensor_tensor(r32(x_lo(u)), x_whole(u), x_hi(u), ALU.subtract).then_inc(x_lo_rdy, 1)

            def hid_s(u, f, between=lambda: None):
                i = NF * u + f
                up = pF[f % 2]
                if f < NF - 1:
                    dve.wait_ge(u_ps, (NF - 1) * u + f + 1)
                else:
                    up = pK[f % 2]
                dve.wait_ge(silu_rdy, i + 1)
                sil = SIL[f % 2]
                dve.tensor_tensor(sil[0:SF[f], :], sil[P - SF[f]:P, :], up[P - SF[f]:P, :], ALU.mult).then_inc(h_rdy, 1)
                between()
                dve.wait_ge(d_ps, i - 2)
                dve.wait_ge(h_hi, NF * (u - CS) + f + 1)
                dve.tensor_tensor(r32(HTL[f % 3][0:SF[f], :]), sil[0:SF[f], :], HTH[f % 3][0:SF[f], :], ALU.subtract).then_inc(h_lo, 1)

            steps = [0]

            def step(ins):
                steps[0] += 1
                ins.then_inc(rt, 1)
                dve.wait_ge(rt, steps[0])

            def te(i):
                return TMP[i].rearrange("p (t e) -> p t e", e=E)

            def over_e(a):
                return a[:, :, None].to_broadcast((P, T, E))

            MX, SUM, RSUM, M1, M2, PK1, PK2 = (SMALL[:, i, :] for i in range(7))
            desc = DESC[:, None, :].to_broadcast((P, T, E))

            def less_max():
                dve.wait_ge(r_ev, CH + 1)
                step(dve.tensor_reduce(MX, LOG[:, :, 0:E], AX_X, ALU.max))
                dve.tensor_tensor(te(0), LOG[:, :, 0:E], over_e(MX), ALU.subtract).then_inc(probe_max, 1)

            def gates_and_probabilities():
                dve.wait_ge(rt_a, 2)
                step(dve.tensor_scalar(SIG[:, :], SIG[:, :], 1.0, None, ALU.add))
                step(dve.reciprocal(SIG[:, :], SIG[:, :]))
                step(dve.tensor_reduce(SUM, te(1), AX_X, ALU.add))
                step(dve.reciprocal(RSUM, SUM))
                step(dve.tensor_tensor(te(2), te(1), over_e(RSUM), ALU.mult))

            def first_choice():
                step(dve.tensor_reduce(M1, te(2), AX_X, ALU.max))
                step(dve.tensor_tensor(te(0), te(2), over_e(M1), ALU.is_equal))
                step(dve.tensor_tensor(te(0), te(0), desc, ALU.mult))
                step(dve.tensor_reduce(PK1, te(0), AX_X, ALU.max))
                step(dve.tensor_tensor(te(1), desc, over_e(PK1), ALU.is_equal))
                step(dve.scalar_tensor_tensor(te(3), te(1), -4.0, te(2), ALU.mult, ALU.add))

            def second_choice():
                step(dve.tensor_reduce(M2, te(3), AX_X, ALU.max))
                step(dve.tensor_tensor(te(0), te(3), over_e(M2), ALU.is_equal))
                step(dve.tensor_tensor(te(0), te(0), desc, ALU.mult))
                step(dve.tensor_reduce(PK2, te(0), AX_X, ALU.max))
                step(dve.tensor_tensor(te(2), desc, over_e(PK2), ALU.is_equal))
                dve.tensor_tensor(te(4), te(1), te(2), ALU.add).then_inc(mask_rdy, 1)

            def weights():
                step(dve.tensor_tensor(SUM, M1, M2, ALU.add))
                step(dve.reciprocal(RSUM, SUM))
                step(dve.tensor_tensor(RW[:, 0, :], M1, RSUM, ALU.mult))
                step(dve.tensor_tensor(RW[:, 1, :], M2, RSUM, ALU.mult))
                step(dve.memset(CUM[0][:, 0:16, :], 0.0))
                step(dve.memset(CUM[1][:, 0:16, :], 0.0))
                step(dve.memset(TMP[3][:, 64:128], 0.0))

            tot = CUM[1]

            def running_counts():
                dve.wait_ge(rt_ps, 1)
                step(dve.tensor_copy(CUM[0][:, 16:48, :], pT[1][:, :].rearrange("p (t e) -> p t e", e=E)))
                for i in range(5):
                    a, b = CUM[i % 2], CUM[(i + 1) % 2]
                    step(dve.tensor_tensor(b[:, 16:48, :], a[:, 16:48, :], a[:, 16 - (1 << i):48 - (1 << i), :], ALU.add))

            end = [TMP[3][:, 64:88], TMP[3][:, 96:120]]

            def first_slots():
                cnt = TMP[3].bitcast(I32)
                step(dve.tensor_scalar(cnt[:, 0:E], tot[:, 47, :], float(P - 1), None, ALU.add))
                step(dve.tensor_scalar(cnt[:, E:2 * E], cnt[:, 0:E], 7, None, ALU.logical_shift_right))
                step(dve.tensor_copy(end[0][:, 8:24], cnt[:, E:2 * E]))
                step(dve.tensor_copy(TMP[3][:, 32:48], cnt[:, E:2 * E]))
                for i in range(4):
                    a, b = end[i % 2], end[(i + 1) % 2]
                    step(dve.tensor_tensor(b[:, 8:24], a[:, 8:24], a[:, 8 - (1 << i):24 - (1 << i)], ALU.add))
                step(dve.tensor_tensor(TMP[3][:, 128:144], end[0][:, 8:24], TMP[3][:, 32:48], ALU.subtract))
                step(dve.tensor_scalar(TMP[3][:, 144:160], TMP[3][:, 128:144], float(P), None, ALU.mult))

            def slots():
                step(dve.tensor_tensor(te(4), tot[:, 15:47, :], pT[0][:, :].rearrange("p (t e) -> p t e", e=E), ALU.add))
                step(dve.tensor_tensor(te(4), te(4), TMP[3][:, None, 144:160].to_broadcast((P, T, E)), ALU.add))
                for j in range(2):
                    step(dve.tensor_tensor(te(0), te(1 + j), te(4), ALU.mult))
                    step(dve.tensor_reduce(SMALL[:, 7 + j, :], te(0), AX_X, ALU.add))
                step(dve.tensor_copy(SLOT[:, 0, :], SMALL[:, 7, :]))
                dve.tensor_copy(SLOT[:, 1, :], SMALL[:, 8, :]).then_inc(slots_rdy, 1)

            def tile_experts():
                ends = end[0][:, None, 8:24].to_broadcast((P, ST, E))
                step(dve.tensor_tensor(GE, IOTA[:, :, None].to_broadcast((P, ST, E)), ends, ALU.is_ge))
                step(dve.tensor_reduce(TMP[0][:, 0:ST], GE, AX_X, ALU.add))
                dve.tensor_scalar(EID[:, :], TMP[0][:, 0:ST], float(E - 1), float(EW), ALU.min, ALU.mult).then_inc(eid_rdy, 1)

            def copy_x3(e, bank):
                dve.wait_ge(t3_ps, 2 * e + 2)
                dve.wait_ge(xt_save[0], 16 * (B + e))
                dve.tensor_copy(X3T[:, 1, :], bank[:, :]).then_inc(t3_d, 1)

            def logits(e):
                dve.wait_ge(r_ps, e + 1)
                dve.tensor_copy(LOG[:, TPC * e:TPC * e + TPC, :], pR[:, :, 0:E + 1]).then_inc(r_ev, 1)

            d = CH - 1
            copy_x3(d - 1, pT[1])
            normalize(d, 1, lambda j: XN[:, j, :])
            logits(d - 1)
            hid(0, 0)
            dve.wait_ge(t2_ps, 2 * d + 2)
            dve.tensor_copy(X2T[:, 1, :], pT[1][:, :]).then_inc(t2_d, 1)
            hid(0, 1)
            softmax(d)
            hid(0, 2)
            residual(d, o_ps, x2)
            dve.wait_ge(x2, 2 * d + 2)
            stats(d, 2)
            dve.wait_ge(xt_save[1], 16 * (B + d))
            normalize(d, 2, lambda j: XN3C[:, j, :])
            hid(0, 3)
            copy_x3(d, pT[1])
            hid(0, 4)
            dve.wait_ge(ld_late, 16 * NLATE)
            logits(d)
            less_max()
            hid(0, 5)
            gates_and_probabilities()
            shared_out(0)
            for f, stage in enumerate((first_choice, second_choice, weights, running_counts, first_slots, slots)):
                hid(1, f)
                stage()
            shared_out(1)
            for f in range(NF):
                hid(2, f)
                if f == 0:
                    tile_experts()
                for i in range(2 * f, min(2 * f + 2, NW)):
                    w_split(i)
                if f == 2:
                    split_x(CS)
            shared_out(2)
            for u in range(CS, CB):
                for f in range(NF):
                    hid_s(u, f, (lambda i=NW + f: w_split(i)) if u == CS else (lambda: None))
                    if f == 2:
                        split_x(u + 1)
                shared_out(u)

            def copy_w(s, k, w):
                wait(dve, e_gu, s - 1)
                dve.tensor_copy(WE[:, k % 2, :], ARENA[:, bass.ds(w, KD * 2 * FF)]).then_inc(e_w, 1)

            def hidden(s, k):
                dve.wait_ge(e_silu, s + 1)
                wait(dve, e_dn, s - 1)
                dve.tensor_tensor(HE[:, k % 2, :], ESIL[:, k % 2, :], pK[k % 2][:, FF:2 * FF], ALU.mult).then_inc(e_h, 1)

            dve.wait_ge(ld_exp, 16 * 3)
            dve.wait_ge(sc, 16 * 2 * T)
            w = experts_of(0, 8, mybir.EngineType.DVE)
            for s in range(8):
                copy_w(s, s, w[s])
                if s >= 1:
                    hidden(s - 1, s - 1)
            with dve.Fori(1, ST // 8) as g:
                w = experts_of(8 * g, 8, mybir.EngineType.DVE)
                for k in range(8):
                    copy_w(8 * g + k, k, w[k])
                    hidden(8 * g + k - 1, k - 1)
            hidden(ST - 1, ST - 1)

            def combine(t):
                for j in range(2):
                    k = 2 * (t % 8) + j
                    dve.wait_ge(yg_in[k], 16 * (t // 8 + 1))
                    if j:
                        dve.wait_ge(comb1, t + 1)
                    dve.scalar_tensor_tensor(X[:, t, :], YG[:, k, :], RW[:, j, t:t + 1], X[:, t, :],
                                             ALU.mult, ALU.add).then_inc(comb if j else comb1, 1)

            dve.wait_ge(s_res, TPC * CB)
            tiles = 0
            for u in range(CB, CH):
                for f in range(NF):
                    first = tiles
                    pair = max(0, min(T, 2 * (NF * (u - CB) + f) - 3) - tiles)
                    hid_s(u, f, (lambda t=first: combine(t)) if pair else (lambda: None))
                    for t in range(first + 1, first + pair):
                        combine(t)
                    tiles += pair
                    if f == 2 and u < CH - 1:
                        split_x(u + 1)
                while u == CH - 1 and tiles < T:
                    combine(tiles)
                    tiles += 1
                dve.wait_ge(comb, tiles)
                shared_out(u)


_OUTS = [((B, L, D), "float32")]


def kernel(**inputs):
    import numpy as np
    import concourse.bacc as bacc
    from concourse import mybir as mb
    from concourse.bass_utils import run_bass_kernel_spmd

    g = {k: np.asarray(v) for k, v in inputs.items()}
    t = lambda a: np.ascontiguousarray(a.T)
    arrays = {
        "x": g["x"].reshape(B * L, D), "ctxT": t(g["ctx_1024"].reshape(B * SKV, D)),
        "wqT": t(g["L0_attn_Wq"]), "bq": g["L0_attn_bq"], "wkT": t(g["L0_attn_Wk"]), "bk": g["L0_attn_bk"],
        "wvT": t(g["L0_attn_Wv"]), "bv": g["L0_attn_bv"], "woT": t(g["L0_attn_Wo"]), "bo": g["L0_attn_bo"],
        "orfT": t(g["L0_attn_orf"]),
        "xwq": g["L0_xattn_Wq"], "xbq": g["L0_xattn_bq"], "xwkT": t(g["L0_xattn_Wk"]), "xbk": g["L0_xattn_bk"],
        "xwvT": t(g["L0_xattn_Wv"]), "xbv": g["L0_xattn_bv"], "xwoT": t(g["L0_xattn_Wo"]), "xbo": g["L0_xattn_bo"],
        "gwT": t(np.concatenate([g["L0_ffn_gate_w"], g["L0_ffn_shared_gate_w"]], 0)),
        "wgu": g["L0_ffn_w_gate_up"], "wdn": g["L0_ffn_w_down"],
        "sgT": t(g["L0_ffn_shared_w_gate"]), "suT": t(g["L0_ffn_shared_w_up"]), "sdT": t(g["L0_ffn_shared_w_down"]),
        "ident": np.eye(P, dtype=np.float32), "tri": np.triu(np.ones((P, P), np.float32), 1),
        "normblk": np.kron(np.eye(4, dtype=np.float32), np.full((DK, M), -0.5 * float(DK) ** -0.5, np.float32)),
        "desc16": np.arange(E, 0, -1, dtype=np.float32)[None], "iota": np.arange(ST, dtype=np.float32)[None],
    }
    nc = bacc.Bacc("TRN2", target_bir_lowering=False, num_devices=1)
    arrays = {f"in_{k}": np.ascontiguousarray(v) for k, v in arrays.items()}
    args = [nc.dram_tensor(k, v.shape, mb.dt.from_np(v.dtype), kind="ExternalInput").ap() for k, v in arrays.items()]
    shape, dtype = _OUTS[0]
    o = nc.dram_tensor("out_0", (B * L, D), mb.dt.from_np(np.dtype(dtype)), kind="ExternalOutput").ap()
    decoder_layer(nc, *args, o)
    r = run_bass_kernel_spmd(nc, [arrays], core_ids=[0])
    return r.results[0]["out_0"].reshape(shape)
```
